# Optimizing a Trainium2 kernel written in Bass

```python
import numpy as np
import jax
import jax.numpy as jnp

def _softmax(x, axis=-1):
    return jax.nn.softmax(x, axis=axis)

def _gelu(x):
    return jax.nn.gelu(x, approximate=True)

def _silu(x):
    return jax.nn.silu(x)

def _sigmoid(x):
    return jax.nn.sigmoid(x)

def _layernorm(x, axis=-1, eps=1e-05):
    m = jnp.mean(x, axis=axis, keepdims=True)
    v = jnp.var(x, axis=axis, keepdims=True)
    return (x - m) / jnp.sqrt(v + eps)

def _scatter_add(tgt, idx, src, axis=0):
    return tgt.at[idx].add(src)

def _segment_sum(src, seg, n):
    return jax.ops.segment_sum(src, seg, n)
kernel_name = 'mk_adaln_ffn_d4_seqx_r4_2ae2e1'

def setup_inputs(seed: int=0):
    np.random.seed(seed)
    _w = jnp.asarray

    def _rec_inputs():
        import jax
        import jax.numpy as jnp
        _rk = jax.random.key(seed)
        x = 7.22e-05 + 1 * jax.random.normal(jax.random.fold_in(_rk, 1), (2, 1024, 256), jnp.float32)
        _lenS = 1024 - jax.random.randint(jax.random.fold_in(_rk, 7), (2,), 0, max(1, 1024 // 4) + 1, jnp.int32)
        _lenS2 = 1024 - jax.random.randint(jax.random.fold_in(_rk, 8), (2,), 0, max(1, 1024 // 4) + 1, jnp.int32)
        cond_64 = -0.104238 + 1.01173 * jax.random.normal(jax.random.fold_in(_rk, 11), (2, 64), jnp.float32)
        fside_16xSxS_0 = -5.72187e-05 + 0.999849 * jax.random.normal(jax.random.fold_in(_rk, 13), (16, 1024, 1024), jnp.float32)
        _validS = jnp.arange(1024)[None, :] < _lenS[:, None]
        _validS2 = jnp.arange(1024)[None, :] < _lenS2[:, None]
        _causal = jnp.tril(jnp.ones((1024, 1024), dtype=bool))
        mask_BxS_bf1 = jnp.ones((2, 1024), dtype=bool)
        mask_BxS_bk0 = jnp.logical_not(jnp.broadcast_to(_validS[:, :], (2, 1024)))
        return (x, cond_64, fside_16xSxS_0, mask_BxS_bf1, mask_BxS_bk0)
    x, cond_64, fside_16xSxS_0, mask_BxS_bf1, mask_BxS_bk0 = _rec_inputs()

    def _L0_cond_setup():
        import jax, jax.numpy as jnp
        import numpy as np
        B, S, H = (4, 512, 256)
        E = 8
        M = 128
        K = 2
        N_SHARED = 2
        SM = M * N_SHARED
        G = 64
        GE_TEMP = 1.0
        ALPHA = 0.001
        SEQ_AUX = True
        NORM_TOPK = True
        COS_TEMP = 0.78
        CONS_ALPHA = 0.01
        LEAKY_SLOPE = 0.01
        EPS_COS = 1e-08

        def _leaky(x):
            return jnp.where(x >= 0, x, LEAKY_SLOPE * x)

        def _moe_forward(hidden_states, g, wt, wg, w_gate, w_up, w_down, sw_gate, sw_up, sw_down):
            b, s, h = hidden_states.shape
            x = hidden_states.reshape(-1, h)
            T = x.shape[0]
            logits_h = x @ wt.T
            logits_g = g @ wg.T
            logits_g = jnp.repeat(logits_g, s, axis=0)
            logits = (logits_h + logits_g / GE_TEMP) / (1.0 + 1.0 / GE_TEMP)
            scores = jax.nn.softmax(logits, axis=-1)
            topk_w, topk_idx = jax.lax.top_k(scores, K)
            if K > 1 and NORM_TOPK:
                topk_w = topk_w / (topk_w.sum(-1, keepdims=True) + 1e-20)
            onehot = jax.nn.one_hot(topk_idx.reshape(b, s * K), E, dtype=jnp.float32)
            ce = onehot.sum(1) / (s * K / E)
            aux_loss = (ce * scores.reshape(b, s, E).mean(1)).sum(1).mean() * ALPHA
            gp = _leaky(jnp.einsum('th,ehm->etm', x, w_gate))
            up = jnp.einsum('th,ehm->etm', x, w_up)
            y_all = jnp.einsum('etm,emh->eth', gp * up, w_down)
            y_sel = y_all[topk_idx, jnp.arange(T)[:, None], :]
            y = (y_sel * topk_w[..., None]).sum(1).reshape(b, s, h)
            p = _leaky(hidden_states @ sw_gate) * (hidden_states @ sw_up) @ sw_down
            y = y + p
            num = jnp.sum(y * p, -1)
            den = jnp.maximum(jnp.linalg.norm(y, axis=-1), EPS_COS) * jnp.maximum(jnp.linalg.norm(p, axis=-1), EPS_COS)
            closs = CONS_ALPHA * jnp.mean(num / den / (1.0 + COS_TEMP))
            return (y, aux_loss + closs)
        key = jax.random.key(seed)
        ks = jax.random.split(key, 12)
        sh = 1.0 / np.sqrt(H)
        sm = 1.0 / np.sqrt(M)
        ssm = 1.0 / np.sqrt(SM)
        sg = 1.0 / np.sqrt(G)
        return {'hidden_states': jax.random.normal(ks[0], (B, S, H), jnp.float32), 'g': jax.random.normal(ks[1], (B, G), jnp.float32), 'wt': jax.random.uniform(ks[2], (E, H), jnp.float32, -sh, sh), 'wg': jax.random.uniform(ks[3], (E, G), jnp.float32, -sg, sg), 'w_gate': jax.random.uniform(ks[4], (E, H, M), jnp.float32, -sh, sh), 'w_up': jax.random.uniform(ks[5], (E, H, M), jnp.float32, -sh, sh), 'w_down': jax.random.uniform(ks[6], (E, M, H), jnp.float32, -sm, sm), 'sw_gate': jax.random.uniform(ks[7], (H, SM), jnp.float32, -sh, sh), 'sw_up': jax.random.uniform(ks[8], (H, SM), jnp.float32, -sh, sh), 'sw_down': jax.random.uniform(ks[9], (SM, H), jnp.float32, -ssm, ssm)}
    _L0_cond_all = _L0_cond_setup()
    _L0_cond_in = {k: v for k, v in _L0_cond_all.items() if k in ('wt', 'wg', 'w_gate', 'w_up', 'w_down', 'sw_gate', 'sw_up', 'sw_down')}
    del _L0_cond_all

    def _L0_ffn_setup():
        import jax, jax.numpy as jnp
        import numpy as np
        H = 256
        I = 1024
        E = 4
        LN_EPS = 1e-12

        def _layer_norm(x, gamma, beta, eps=LN_EPS):
            mu = jnp.mean(x, axis=-1, keepdims=True)
            var = jnp.mean(jnp.square(x - mu), axis=-1, keepdims=True)
            return (x - mu) * jax.lax.rsqrt(var + eps) * gamma + beta
        key = jax.random.key(seed)
        ks = jax.random.split(key, 8)
        B, S = (4, 128)
        scale = 0.02
        return {'hidden_states': jax.random.normal(ks[0], (B, S, H), jnp.float32), 'W_router': jax.random.normal(ks[1], (H, E), jnp.float32) * scale, 'W1': jax.random.normal(ks[2], (E, H, I), jnp.float32) * scale, 'b1': jax.random.normal(ks[3], (E, I), jnp.float32) * scale, 'Wo': jax.random.normal(ks[4], (I, H), jnp.float32) * scale, 'bo': jax.random.normal(ks[5], (H,), jnp.float32) * scale, 'ln_gamma': jnp.ones((H,), jnp.float32), 'ln_beta': jnp.zeros((H,), jnp.float32)}
    _L0_ffn_all = _L0_ffn_setup()
    _L0_ffn_in = {k: v for k, v in _L0_ffn_all.items() if k in ('W_router', 'W1', 'b1', 'Wo', 'bo', 'ln_gamma', 'ln_beta')}
    del _L0_ffn_all

    def _L1_cond_setup():
        import jax, jax.numpy as jnp
        import numpy as np
        DIM = 256
        HEADS = 16
        DIM_HEAD = 64
        SCALE = 8.0

        def ln(x, g, eps=1e-05):
            mean = x.mean(axis=-1, keepdims=True)
            var = ((x - mean) ** 2).mean(axis=-1, keepdims=True)
            return (x - mean) * jax.lax.rsqrt(var + eps) * g

        def l2norm(t):
            n = jnp.maximum(jnp.linalg.norm(t, axis=-1, keepdims=True), 1e-12)
            return t / n

        def rel_pos_bias(n, w0, b0, g0, w1, b1, g1, w2, b2, dtype):
            pos = jnp.arange(-n + 1, n, dtype=dtype)[:, None]
            h = jax.nn.silu(ln(pos @ w0 + b0, g0))
            h = jax.nn.silu(ln(h @ w1 + b1, g1))
            h = h @ w2 + b2
            i = jnp.arange(n)
            idx = i[:, None] - i[None, :] + n - 1
            bias = h[idx]
            return jnp.transpose(bias, (2, 0, 1))
        key = jax.random.key(seed)
        ks = jax.random.split(key, 16)
        b, n = (2, 512)
        inner = HEADS * DIM_HEAD
        s = 0.02
        return {'x': jax.random.normal(ks[0], (b, n, DIM), jnp.float32), 'mask': jnp.ones((b, n), dtype=bool), 'g_norm': jnp.ones((DIM,), jnp.float32), 'Wq': jax.random.normal(ks[1], (DIM, inner), jnp.float32) * s, 'Wkv': jax.random.normal(ks[2], (DIM, 2 * DIM_HEAD), jnp.float32) * s, 'q_scale': jnp.ones((DIM_HEAD,), jnp.float32), 'k_scale': jnp.ones((DIM_HEAD,), jnp.float32), 'null_kv': jax.random.normal(ks[3], (2, DIM_HEAD), jnp.float32), 'null_attn_bias': jax.random.normal(ks[4], (HEADS,), jnp.float32), 'w0': jax.random.normal(ks[5], (1, DIM), jnp.float32) * s, 'b0': jnp.zeros((DIM,), jnp.float32), 'g0': jnp.ones((DIM,), jnp.float32), 'w1': jax.random.normal(ks[6], (DIM, DIM), jnp.float32) * s, 'b1': jnp.zeros((DIM,), jnp.float32), 'g1': jnp.ones((DIM,), jnp.float32), 'w2': jax.random.normal(ks[7], (DIM, HEADS), jnp.float32) * s, 'b2': jnp.zeros((HEADS,), jnp.float32), 'Wout': jax.random.normal(ks[8], (inner, DIM), jnp.float32) * s, 'g_out': jnp.ones((DIM,), jnp.float32)}
    _L1_cond_all = _L1_cond_setup()
    _L1_cond_in = {k: v for k, v in _L1_cond_all.items() if k in ('g_norm', 'Wq', 'Wkv', 'q_scale', 'k_scale', 'null_attn_bias', 'w0', 'b0', 'g0', 'w1', 'b1', 'g1', 'w2', 'b2', 'Wout', 'g_out')}
    del _L1_cond_all

    def _L1_ffn_setup():
        import jax, jax.numpy as jnp
        import numpy as np
        B, S, D, F, E, R = (4, 512, 256, 1024, 8, 4)
        key = jax.random.key(seed)
        ks = jax.random.split(key, 8)
        s_in = 1.0 / np.sqrt(D)
        s_ff = 1.0 / np.sqrt(F)
        return {'hidden_states': jax.random.normal(ks[0], (B, S, D), jnp.float32), 'gate_W': jax.random.normal(ks[1], (E, D), jnp.float32) * s_in, 'gate_b': jnp.zeros((E,), jnp.float32), 'wi_W': jax.random.normal(ks[2], (F, D), jnp.float32) * s_in, 'wi_b': jnp.zeros((F,), jnp.float32), 'wo_W': jax.random.normal(ks[3], (D, F), jnp.float32) * s_ff, 'wo_b': jnp.zeros((D,), jnp.float32), 'lora_A': jax.random.normal(ks[4], (E, R, D), jnp.float32) * s_in, 'lora_B': jax.random.normal(ks[5], (E, F, R), jnp.float32) * 0.02}
    _L1_ffn_all = _L1_ffn_setup()
    _L1_ffn_in = {k: v for k, v in _L1_ffn_all.items() if k in ('gate_W', 'gate_b', 'wi_W', 'wi_b', 'wo_W', 'wo_b', 'lora_A', 'lora_B')}
    del _L1_ffn_all

    def _L2_cond_setup():
        import jax, jax.numpy as jnp
        import numpy as np
        B, N, DIM, H, DH = (2, 512, 256, 16, 64)
        INNER = H * DH
        EPS = 1e-05

        def layernorm(x, g):
            mean = jnp.mean(x, axis=-1, keepdims=True)
            var = jnp.var(x, axis=-1, keepdims=True)
            return (x - mean) * jax.lax.rsqrt(var + EPS) * g
        key = jax.random.key(seed)
        ks = jax.random.split(key, 10)
        x = jax.random.normal(ks[0], (B, N, DIM), dtype=jnp.float32)
        attn_bias = jax.random.normal(ks[1], (H, N, N), dtype=jnp.float32)
        mask = jax.random.randint(ks[2], (B, N), 0, 2).astype(bool)
        g_in = jnp.ones((DIM,), dtype=jnp.float32)
        null_attn_bias = jax.random.normal(ks[3], (H,), dtype=jnp.float32)
        null_kv = jax.random.normal(ks[4], (2, DH), dtype=jnp.float32)
        Wq = jax.random.normal(ks[5], (DIM, INNER), dtype=jnp.float32) * 0.02
        Wkv = jax.random.normal(ks[6], (DIM, 2 * DH), dtype=jnp.float32) * 0.02
        Wo = jax.random.normal(ks[7], (INNER, DIM), dtype=jnp.float32) * 0.02
        g_out = jnp.ones((DIM,), dtype=jnp.float32)
        return {'x': x, 'attn_bias': attn_bias, 'mask': mask, 'g_in': g_in, 'null_attn_bias': null_attn_bias, 'null_kv': null_kv, 'Wq': Wq, 'Wkv': Wkv, 'Wo': Wo, 'g_out': g_out}
    _L2_cond_all = _L2_cond_setup()
    _L2_cond_in = {k: v for k, v in _L2_cond_all.items() if k in ('g_in', 'null_attn_bias', 'Wq', 'Wkv', 'Wo', 'g_out')}
    del _L2_cond_all

    def _L2_ffn_setup():
        import jax, jax.numpy as jnp
        import numpy as np
        FP8_MAX = 448.0
        key = jax.random.key(seed)
        k_x, k_w, k_b = jax.random.split(key, 3)
        B, S, IN, OUT = (4, 2048, 256, 256)
        x = jax.random.normal(k_x, (B, S, IN), dtype=jnp.float32)
        w_fp32 = jax.random.normal(k_w, (OUT, IN), dtype=jnp.float32)
        weight_fp8 = w_fp32.astype(jnp.float8_e4m3fn).astype(jnp.float32)
        bias = jax.random.normal(k_b, (OUT,), dtype=jnp.float32)
        input_scale = jnp.ones((1,), dtype=jnp.float32)
        weight_scale = jnp.ones((1,), dtype=jnp.float32)
        return {'x': x, 'weight_fp8': weight_fp8, 'bias': bias, 'input_scale': input_scale, 'weight_scale': weight_scale}
    _L2_ffn_all = _L2_ffn_setup()
    _L2_ffn_in = {k: v for k, v in _L2_ffn_all.items() if k in ('weight_fp8', 'bias', 'input_scale', 'weight_scale')}
    del _L2_ffn_all

    def _L3_cond_setup():
        import jax, jax.numpy as jnp
        import numpy as np
        B, N, DIM, H, DH = (2, 512, 256, 16, 64)
        INNER = H * DH
        EPS = 1e-05

        def layernorm(x, g):
            mean = jnp.mean(x, axis=-1, keepdims=True)
            var = jnp.var(x, axis=-1, keepdims=True)
            return (x - mean) * jax.lax.rsqrt(var + EPS) * g
        key = jax.random.key(seed)
        ks = jax.random.split(key, 10)
        x = jax.random.normal(ks[0], (B, N, DIM), dtype=jnp.float32)
        attn_bias = jax.random.normal(ks[1], (H, N, N), dtype=jnp.float32)
        mask = jax.random.randint(ks[2], (B, N), 0, 2).astype(bool)
        g_in = jnp.ones((DIM,), dtype=jnp.float32)
        null_attn_bias = jax.random.normal(ks[3], (H,), dtype=jnp.float32)
        null_kv = jax.random.normal(ks[4], (2, DH), dtype=jnp.float32)
        Wq = jax.random.normal(ks[5], (DIM, INNER), dtype=jnp.float32) * 0.02
        Wkv = jax.random.normal(ks[6], (DIM, 2 * DH), dtype=jnp.float32) * 0.02
        Wo = jax.random.normal(ks[7], (INNER, DIM), dtype=jnp.float32) * 0.02
        g_out = jnp.ones((DIM,), dtype=jnp.float32)
        return {'x': x, 'attn_bias': attn_bias, 'mask': mask, 'g_in': g_in, 'null_attn_bias': null_attn_bias, 'null_kv': null_kv, 'Wq': Wq, 'Wkv': Wkv, 'Wo': Wo, 'g_out': g_out}
    _L3_cond_all = _L3_cond_setup()
    _L3_cond_in = {k: v for k, v in _L3_cond_all.items() if k in ('g_in', 'null_attn_bias', 'Wq', 'Wkv', 'Wo', 'g_out')}
    del _L3_cond_all

    def _L3_ffn_setup():
        import jax, jax.numpy as jnp
        import numpy as np
        B, T = (2, 512)
        D_MODEL, D_HIDDEN = (256, 512)
        N_EXPERTS, TOP_K = (8, 2)
        N_TOKENS = B * T
        CAPACITY = 2 * N_TOKENS * TOP_K // N_EXPERTS
        key = jax.random.key(seed)
        k_x, k_rw, k_w, k_v, k_o = jax.random.split(key, 5)
        x = jax.random.normal(k_x, (B, T, D_MODEL), jnp.float32)
        router_w = jax.random.normal(k_rw, (N_EXPERTS, D_MODEL), jnp.float32) * D_MODEL ** (-0.5)
        router_b = jnp.zeros((N_EXPERTS,), jnp.float32)
        W = jax.random.normal(k_w, (N_EXPERTS, D_MODEL, D_HIDDEN), jnp.float32) * D_MODEL ** (-0.5)
        V = jax.random.normal(k_v, (N_EXPERTS, D_MODEL, D_HIDDEN), jnp.float32) * D_MODEL ** (-0.5)
        W_out = jax.random.normal(k_o, (N_EXPERTS, D_HIDDEN, D_MODEL), jnp.float32) * D_HIDDEN ** (-0.5)
        return {'x': x, 'router_w': router_w, 'router_b': router_b, 'W': W, 'V': V, 'W_out': W_out}
    _L3_ffn_all = _L3_ffn_setup()
    _L3_ffn_in = {k: v for k, v in _L3_ffn_all.items() if k in ('router_w', 'router_b', 'W', 'V', 'W_out')}
    del _L3_ffn_all
    return {'x': x, 'cond_64': cond_64, 'fside_16xSxS_0': fside_16xSxS_0, 'mask_BxS_bf1': mask_BxS_bf1, 'mask_BxS_bk0': mask_BxS_bk0, 'L0_cond_wt': _L0_cond_in['wt'], 'L0_cond_wg': _L0_cond_in['wg'], 'L0_cond_w_gate': _L0_cond_in['w_gate'], 'L0_cond_w_up': _L0_cond_in['w_up'], 'L0_cond_w_down': _L0_cond_in['w_down'], 'L0_cond_sw_gate': _L0_cond_in['sw_gate'], 'L0_cond_sw_up': _L0_cond_in['sw_up'], 'L0_cond_sw_down': _L0_cond_in['sw_down'], 'L0_ffn_W_router': _L0_ffn_in['W_router'], 'L0_ffn_W1': _L0_ffn_in['W1'], 'L0_ffn_b1': _L0_ffn_in['b1'], 'L0_ffn_Wo': _L0_ffn_in['Wo'], 'L0_ffn_bo': _L0_ffn_in['bo'], 'L0_ffn_ln_gamma': _L0_ffn_in['ln_gamma'], 'L0_ffn_ln_beta': _L0_ffn_in['ln_beta'], 'L1_cond_g_norm': _L1_cond_in['g_norm'], 'L1_cond_Wq': _L1_cond_in['Wq'], 'L1_cond_Wkv': _L1_cond_in['Wkv'], 'L1_cond_q_scale': _L1_cond_in['q_scale'], 'L1_cond_k_scale': _L1_cond_in['k_scale'], 'L1_cond_null_attn_bias': _L1_cond_in['null_attn_bias'], 'L1_cond_w0': _L1_cond_in['w0'], 'L1_cond_b0': _L1_cond_in['b0'], 'L1_cond_g0': _L1_cond_in['g0'], 'L1_cond_w1': _L1_cond_in['w1'], 'L1_cond_b1': _L1_cond_in['b1'], 'L1_cond_g1': _L1_cond_in['g1'], 'L1_cond_w2': _L1_cond_in['w2'], 'L1_cond_b2': _L1_cond_in['b2'], 'L1_cond_Wout': _L1_cond_in['Wout'], 'L1_cond_g_out': _L1_cond_in['g_out'], 'L1_ffn_gate_W': _L1_ffn_in['gate_W'], 'L1_ffn_gate_b': _L1_ffn_in['gate_b'], 'L1_ffn_wi_W': _L1_ffn_in['wi_W'], 'L1_ffn_wi_b': _L1_ffn_in['wi_b'], 'L1_ffn_wo_W': _L1_ffn_in['wo_W'], 'L1_ffn_wo_b': _L1_ffn_in['wo_b'], 'L1_ffn_lora_A': _L1_ffn_in['lora_A'], 'L1_ffn_lora_B': _L1_ffn_in['lora_B'], 'L2_cond_g_in': _L2_cond_in['g_in'], 'L2_cond_null_attn_bias': _L2_cond_in['null_attn_bias'], 'L2_cond_Wq': _L2_cond_in['Wq'], 'L2_cond_Wkv': _L2_cond_in['Wkv'], 'L2_cond_Wo': _L2_cond_in['Wo'], 'L2_cond_g_out': _L2_cond_in['g_out'], 'L2_ffn_weight_fp8': _L2_ffn_in['weight_fp8'], 'L2_ffn_bias': _L2_ffn_in['bias'], 'L2_ffn_input_scale': _L2_ffn_in['input_scale'], 'L2_ffn_weight_scale': _L2_ffn_in['weight_scale'], 'L3_cond_g_in': _L3_cond_in['g_in'], 'L3_cond_null_attn_bias': _L3_cond_in['null_attn_bias'], 'L3_cond_Wq': _L3_cond_in['Wq'], 'L3_cond_Wkv': _L3_cond_in['Wkv'], 'L3_cond_Wo': _L3_cond_in['Wo'], 'L3_cond_g_out': _L3_cond_in['g_out'], 'L3_ffn_router_w': _L3_ffn_in['router_w'], 'L3_ffn_router_b': _L3_ffn_in['router_b'], 'L3_ffn_W': _L3_ffn_in['W'], 'L3_ffn_V': _L3_ffn_in['V'], 'L3_ffn_W_out': _L3_ffn_in['W_out']}

def reference(x, cond_64, fside_16xSxS_0, mask_BxS_bf1, mask_BxS_bk0, L0_cond_wt, L0_cond_wg, L0_cond_w_gate, L0_cond_w_up, L0_cond_w_down, L0_cond_sw_gate, L0_cond_sw_up, L0_cond_sw_down, L0_ffn_W_router, L0_ffn_W1, L0_ffn_b1, L0_ffn_Wo, L0_ffn_bo, L0_ffn_ln_gamma, L0_ffn_ln_beta, L1_cond_g_norm, L1_cond_Wq, L1_cond_Wkv, L1_cond_q_scale, L1_cond_k_scale, L1_cond_null_attn_bias, L1_cond_w0, L1_cond_b0, L1_cond_g0, L1_cond_w1, L1_cond_b1, L1_cond_g1, L1_cond_w2, L1_cond_b2, L1_cond_Wout, L1_cond_g_out, L1_ffn_gate_W, L1_ffn_gate_b, L1_ffn_wi_W, L1_ffn_wi_b, L1_ffn_wo_W, L1_ffn_wo_b, L1_ffn_lora_A, L1_ffn_lora_B, L2_cond_g_in, L2_cond_null_attn_bias, L2_cond_Wq, L2_cond_Wkv, L2_cond_Wo, L2_cond_g_out, L2_ffn_weight_fp8, L2_ffn_bias, L2_ffn_input_scale, L2_ffn_weight_scale, L3_cond_g_in, L3_cond_null_attn_bias, L3_cond_Wq, L3_cond_Wkv, L3_cond_Wo, L3_cond_g_out, L3_ffn_router_w, L3_ffn_router_b, L3_ffn_W, L3_ffn_V, L3_ffn_W_out):
    import jax
    import jax.numpy as jnp

    def _L0_cond_ref(hidden_states, g, wt, wg, w_gate, w_up, w_down, sw_gate, sw_up, sw_down):
        import jax, jax.numpy as jnp
        import numpy as np
        B, S, H = (4, 512, 256)
        E = 8
        M = 128
        K = 2
        N_SHARED = 2
        SM = M * N_SHARED
        G = 64
        GE_TEMP = 1.0
        ALPHA = 0.001
        SEQ_AUX = True
        NORM_TOPK = True
        COS_TEMP = 0.78
        CONS_ALPHA = 0.01
        LEAKY_SLOPE = 0.01
        EPS_COS = 1e-08

        def _leaky(x):
            return jnp.where(x >= 0, x, LEAKY_SLOPE * x)

        def _moe_forward(hidden_states, g, wt, wg, w_gate, w_up, w_down, sw_gate, sw_up, sw_down):
            b, s, h = hidden_states.shape
            x = hidden_states.reshape(-1, h)
            T = x.shape[0]
            logits_h = x @ wt.T
            logits_g = g @ wg.T
            logits_g = jnp.repeat(logits_g, s, axis=0)
            logits = (logits_h + logits_g / GE_TEMP) / (1.0 + 1.0 / GE_TEMP)
            scores = jax.nn.softmax(logits, axis=-1)
            topk_w, topk_idx = jax.lax.top_k(scores, K)
            if K > 1 and NORM_TOPK:
                topk_w = topk_w / (topk_w.sum(-1, keepdims=True) + 1e-20)
            onehot = jax.nn.one_hot(topk_idx.reshape(b, s * K), E, dtype=jnp.float32)
            ce = onehot.sum(1) / (s * K / E)
            aux_loss = (ce * scores.reshape(b, s, E).mean(1)).sum(1).mean() * ALPHA
            gp = _leaky(jnp.einsum('th,ehm->etm', x, w_gate))
            up = jnp.einsum('th,ehm->etm', x, w_up)
            y_all = jnp.einsum('etm,emh->eth', gp * up, w_down)
            y_sel = y_all[topk_idx, jnp.arange(T)[:, None], :]
            y = (y_sel * topk_w[..., None]).sum(1).reshape(b, s, h)
            p = _leaky(hidden_states @ sw_gate) * (hidden_states @ sw_up) @ sw_down
            y = y + p
            num = jnp.sum(y * p, -1)
            den = jnp.maximum(jnp.linalg.norm(y, axis=-1), EPS_COS) * jnp.maximum(jnp.linalg.norm(p, axis=-1), EPS_COS)
            closs = CONS_ALPHA * jnp.mean(num / den / (1.0 + COS_TEMP))
            return (y, aux_loss + closs)
        y, _ = _moe_forward(hidden_states, g, wt, wg, w_gate, w_up, w_down, sw_gate, sw_up, sw_down)
        return y

    def _L0_ffn_ref(hidden_states, W_router, W1, b1, Wo, bo, ln_gamma, ln_beta):
        import jax, jax.numpy as jnp
        import numpy as np
        H = 256
        I = 1024
        E = 4
        LN_EPS = 1e-12

        def _layer_norm(x, gamma, beta, eps=LN_EPS):
            mu = jnp.mean(x, axis=-1, keepdims=True)
            var = jnp.mean(jnp.square(x - mu), axis=-1, keepdims=True)
            return (x - mu) * jax.lax.rsqrt(var + eps) * gamma + beta
        B, S, _ = hidden_states.shape
        x = hidden_states.reshape(-1, H)
        logits = x @ W_router
        expert_idx = jnp.argmax(logits, axis=-1)
        h = jnp.einsum('th,ehi->tei', x, W1) + b1
        h = jax.nn.gelu(h, approximate=False)
        onehot = jax.nn.one_hot(expert_idx, E, dtype=x.dtype)
        intermediate = jnp.einsum('te,tei->ti', onehot, h)
        y = intermediate @ Wo + bo + x
        y = _layer_norm(y, ln_gamma, ln_beta)
        return y.reshape(B, S, H)

    def _L1_cond_ref(x, mask, g_norm, Wq, Wkv, q_scale, k_scale, null_kv, null_attn_bias, w0, b0, g0, w1, b1, g1, w2, b2, Wout, g_out):
        import jax, jax.numpy as jnp
        import numpy as np
        DIM = 256
        HEADS = 16
        DIM_HEAD = 64
        SCALE = 8.0

        def ln(x, g, eps=1e-05):
            mean = x.mean(axis=-1, keepdims=True)
            var = ((x - mean) ** 2).mean(axis=-1, keepdims=True)
            return (x - mean) * jax.lax.rsqrt(var + eps) * g

        def l2norm(t):
            n = jnp.maximum(jnp.linalg.norm(t, axis=-1, keepdims=True), 1e-12)
            return t / n

        def rel_pos_bias(n, w0, b0, g0, w1, b1, g1, w2, b2, dtype):
            pos = jnp.arange(-n + 1, n, dtype=dtype)[:, None]
            h = jax.nn.silu(ln(pos @ w0 + b0, g0))
            h = jax.nn.silu(ln(h @ w1 + b1, g1))
            h = h @ w2 + b2
            i = jnp.arange(n)
            idx = i[:, None] - i[None, :] + n - 1
            bias = h[idx]
            return jnp.transpose(bias, (2, 0, 1))
        b, n, _ = x.shape
        xn = ln(x, g_norm)
        q = (xn @ Wq).reshape(b, n, HEADS, DIM_HEAD).transpose(0, 2, 1, 3)
        kv = xn @ Wkv
        k, v = (kv[..., :DIM_HEAD], kv[..., DIM_HEAD:])
        nk = jnp.broadcast_to(null_kv[0], (b, 1, DIM_HEAD))
        nv = jnp.broadcast_to(null_kv[1], (b, 1, DIM_HEAD))
        k = jnp.concatenate([nk, k], axis=1)
        v = jnp.concatenate([nv, v], axis=1)
        q = l2norm(q) * q_scale
        k = l2norm(k) * k_scale
        sim = jnp.einsum('bhid,bjd->bhij', q, k) * SCALE
        bias = rel_pos_bias(n, w0, b0, g0, w1, b1, g1, w2, b2, q.dtype)
        null_bias = jnp.broadcast_to(null_attn_bias[:, None, None], (HEADS, n, 1))
        attn_bias = jnp.concatenate([null_bias, bias], axis=-1)
        sim = sim + attn_bias
        neg = -jnp.finfo(sim.dtype).max
        causal = jnp.triu(jnp.ones((n, n + 1), dtype=bool), k=2)
        sim = jnp.where(causal, neg, sim)
        m = jnp.pad(mask, ((0, 0), (1, 0)), constant_values=True)[:, None, None, :]
        sim = jnp.where(m, sim, neg)
        attn = jax.nn.softmax(sim, axis=-1)
        out = jnp.einsum('bhij,bjd->bhid', attn, v)
        out = out.transpose(0, 2, 1, 3).reshape(b, n, HEADS * DIM_HEAD)
        return ln(out @ Wout, g_out)

    def _L1_ffn_ref(hidden_states, gate_W, gate_b, wi_W, wi_b, wo_W, wo_b, lora_A, lora_B):
        import jax, jax.numpy as jnp
        import numpy as np
        B, S, D, F, E, R = (4, 512, 256, 1024, 8, 4)
        x = hidden_states
        logits = jnp.einsum('bsd,ed->bse', x, gate_W) + gate_b
        top1 = jnp.argmax(jax.nn.softmax(logits, axis=-1), axis=-1)
        base = jnp.einsum('bsd,fd->bsf', x, wi_W) + wi_b
        out = jnp.zeros_like(x)
        for i in range(lora_A.shape[0]):
            lora = jnp.einsum('bsr,fr->bsf', jnp.einsum('bsd,rd->bsr', x, lora_A[i]), lora_B[i])
            inter = jax.nn.relu(base + lora)
            expert_out = jnp.einsum('bsf,df->bsd', inter, wo_W) + wo_b
            mask = (top1 == i).astype(x.dtype)[..., None]
            out = out + mask * expert_out
        return out

    def _L2_cond_ref(x, attn_bias, mask, g_in, null_attn_bias, null_kv, Wq, Wkv, Wo, g_out):
        import jax, jax.numpy as jnp
        import numpy as np
        B, N, DIM, H, DH = (2, 512, 256, 16, 64)
        INNER = H * DH
        EPS = 1e-05

        def layernorm(x, g):
            mean = jnp.mean(x, axis=-1, keepdims=True)
            var = jnp.var(x, axis=-1, keepdims=True)
            return (x - mean) * jax.lax.rsqrt(var + EPS) * g
        b, n, _ = x.shape
        scale = DH ** (-0.5)
        xn = layernorm(x, g_in)
        q = (xn @ Wq).reshape(b, n, H, DH).transpose(0, 2, 1, 3) * scale
        kv = xn @ Wkv
        k, v = (kv[..., :DH], kv[..., DH:])
        nk = jnp.broadcast_to(null_kv[0], (b, 1, DH))
        nv = jnp.broadcast_to(null_kv[1], (b, 1, DH))
        k = jnp.concatenate([nk, k], axis=1)
        v = jnp.concatenate([nv, v], axis=1)
        sim = jnp.einsum('bhid,bjd->bhij', q, k)
        null_col = jnp.broadcast_to(null_attn_bias[:, None, None], (H, n, 1))
        bias = jnp.concatenate([null_col, attn_bias], axis=-1)
        sim = sim + bias
        neg = -jnp.finfo(sim.dtype).max
        j = n + 1
        causal_mask = jnp.triu(jnp.ones((n, j), dtype=bool), k=j - n + 1)
        sim = jnp.where(causal_mask, neg, sim)
        mask_p = jnp.pad(mask, ((0, 0), (1, 0)), constant_values=True)
        sim = jnp.where(mask_p[:, None, None, :], sim, neg)
        attn = jax.nn.softmax(sim, axis=-1)
        out = jnp.einsum('bhij,bjd->bhid', attn, v)
        out = out.transpose(0, 2, 1, 3).reshape(b, n, INNER)
        out = out @ Wo
        return layernorm(out, g_out)

    def _L2_ffn_ref(x, weight_fp8, bias, input_scale, weight_scale):
        import jax, jax.numpy as jnp
        import numpy as np
        FP8_MAX = 448.0
        x_q = jnp.clip(x / input_scale, -FP8_MAX, FP8_MAX)
        x_dq = x_q.astype(jnp.float8_e4m3fn).astype(x.dtype) * input_scale
        w_dq = weight_fp8 * weight_scale
        out = jnp.einsum('bsi,oi->bso', x_dq, w_dq) + bias
        return out

    def _L3_cond_ref(x, attn_bias, mask, g_in, null_attn_bias, null_kv, Wq, Wkv, Wo, g_out):
        import jax, jax.numpy as jnp
        import numpy as np
        B, N, DIM, H, DH = (2, 512, 256, 16, 64)
        INNER = H * DH
        EPS = 1e-05

        def layernorm(x, g):
            mean = jnp.mean(x, axis=-1, keepdims=True)
            var = jnp.var(x, axis=-1, keepdims=True)
            return (x - mean) * jax.lax.rsqrt(var + EPS) * g
        b, n, _ = x.shape
        scale = DH ** (-0.5)
        xn = layernorm(x, g_in)
        q = (xn @ Wq).reshape(b, n, H, DH).transpose(0, 2, 1, 3) * scale
        kv = xn @ Wkv
        k, v = (kv[..., :DH], kv[..., DH:])
        nk = jnp.broadcast_to(null_kv[0], (b, 1, DH))
        nv = jnp.broadcast_to(null_kv[1], (b, 1, DH))
        k = jnp.concatenate([nk, k], axis=1)
        v = jnp.concatenate([nv, v], axis=1)
        sim = jnp.einsum('bhid,bjd->bhij', q, k)
        null_col = jnp.broadcast_to(null_attn_bias[:, None, None], (H, n, 1))
        bias = jnp.concatenate([null_col, attn_bias], axis=-1)
        sim = sim + bias
        neg = -jnp.finfo(sim.dtype).max
        j = n + 1
        causal_mask = jnp.triu(jnp.ones((n, j), dtype=bool), k=j - n + 1)
        sim = jnp.where(causal_mask, neg, sim)
        mask_p = jnp.pad(mask, ((0, 0), (1, 0)), constant_values=True)
        sim = jnp.where(mask_p[:, None, None, :], sim, neg)
        attn = jax.nn.softmax(sim, axis=-1)
        out = jnp.einsum('bhij,bjd->bhid', attn, v)
        out = out.transpose(0, 2, 1, 3).reshape(b, n, INNER)
        out = out @ Wo
        return layernorm(out, g_out)

    def _L3_ffn_ref(x, router_w, router_b, W, V, W_out):
        import jax, jax.numpy as jnp
        import numpy as np
        B, T = (2, 512)
        D_MODEL, D_HIDDEN = (256, 512)
        N_EXPERTS, TOP_K = (8, 2)
        N_TOKENS = B * T
        CAPACITY = 2 * N_TOKENS * TOP_K // N_EXPERTS
        Bq, Tq, D = x.shape
        N = Bq * Tq
        x_flat = x.reshape(N, D)
        router_logits = x_flat @ router_w.T + router_b
        top_vals, top_ids = jax.lax.top_k(router_logits, TOP_K)
        top_probs = jax.nn.softmax(top_vals, axis=-1)
        x_pad = jnp.concatenate([x_flat, jnp.zeros((1, D), x_flat.dtype)], axis=0)
        probs_pad = jnp.concatenate([top_probs, jnp.zeros((1, TOP_K), top_probs.dtype)], axis=0)
        out = jnp.zeros((N + 1, D), x_flat.dtype)
        for e in range(N_EXPERTS):
            tok, slot = jnp.nonzero(top_ids == e, size=CAPACITY, fill_value=(N, 0))
            w = probs_pad[tok, slot][:, None]
            xin = x_pad[tok]
            a = xin @ W[e]
            b = xin @ V[e]
            y = a * (b * jax.nn.sigmoid(b)) @ W_out[e]
            out = out.at[tok].add(y * w)
        return out[:N].reshape(Bq, Tq, D)
    x = x + _L0_ffn_ref(_L0_cond_ref(x, cond_64, L0_cond_wt, L0_cond_wg, L0_cond_w_gate, L0_cond_w_up, L0_cond_w_down, L0_cond_sw_gate, L0_cond_sw_up, L0_cond_sw_down), L0_ffn_W_router, L0_ffn_W1, L0_ffn_b1, L0_ffn_Wo, L0_ffn_bo, L0_ffn_ln_gamma, L0_ffn_ln_beta)
    x = x + _L1_ffn_ref(_L1_cond_ref(x, mask_BxS_bf1, L1_cond_g_norm, L1_cond_Wq, L1_cond_Wkv, L1_cond_q_scale, L1_cond_k_scale, cond_64, L1_cond_null_attn_bias, L1_cond_w0, L1_cond_b0, L1_cond_g0, L1_cond_w1, L1_cond_b1, L1_cond_g1, L1_cond_w2, L1_cond_b2, L1_cond_Wout, L1_cond_g_out), L1_ffn_gate_W, L1_ffn_gate_b, L1_ffn_wi_W, L1_ffn_wi_b, L1_ffn_wo_W, L1_ffn_wo_b, L1_ffn_lora_A, L1_ffn_lora_B)
    x = x + _L2_ffn_ref(_L2_cond_ref(x, fside_16xSxS_0, mask_BxS_bk0, L2_cond_g_in, L2_cond_null_attn_bias, cond_64, L2_cond_Wq, L2_cond_Wkv, L2_cond_Wo, L2_cond_g_out), L2_ffn_weight_fp8, L2_ffn_bias, L2_ffn_input_scale, L2_ffn_weight_scale)
    x = x + _L3_ffn_ref(_L3_cond_ref(x, fside_16xSxS_0, mask_BxS_bk0, L3_cond_g_in, L3_cond_null_attn_bias, cond_64, L3_cond_Wq, L3_cond_Wkv, L3_cond_Wo, L3_cond_g_out), L3_ffn_router_w, L3_ffn_router_b, L3_ffn_W, L3_ffn_V, L3_ffn_W_out)
    return x

_drawn_inputs = setup_inputs


def setup_inputs(seed=0):
    import zlib

    import numpy as np

    out = dict(_drawn_inputs(seed))
    spreads = {'L0_ffn_ln_gamma': (1.0, 0.2),
     'L0_ffn_ln_beta': (0.0, 0.1),
     'L1_cond_g_norm': (1.0, 0.2),
     'L1_cond_q_scale': (1.0, 0.6),
     'L1_cond_k_scale': (1.0, 0.6),
     'L1_cond_b0': (0.0, 0.8),
     'L1_cond_g0': (1.0, 0.6),
     'L1_cond_b1': (0.0, 0.8),
     'L1_cond_g1': (1.0, 0.6),
     'L1_cond_b2': (0.0, 0.8),
     'L1_cond_g_out': (1.0, 0.2),
     'L1_ffn_gate_b': (0.0, 0.8),
     'L1_ffn_wi_b': (0.0, 0.1),
     'L1_ffn_wo_b': (0.0, 0.1),
     'L2_cond_g_in': (1.0, 0.2),
     'L2_cond_g_out': (1.0, 0.2),
     'L3_cond_g_in': (1.0, 0.6),
     'L3_cond_g_out': (1.0, 0.6),
     'L3_ffn_router_b': (0.0, 2.0)}
    factors = {'L1_cond_null_attn_bias': 3.176,
     'L1_cond_w0': 8.0,
     'L1_cond_w1': 8.0,
     'L1_cond_w2': 7.135,
     'L1_ffn_gate_W': 8.0,
     'L1_ffn_lora_A': 6.373,
     'L1_ffn_lora_B': 5.883,
     'L3_cond_null_attn_bias': 8.0,
     'L3_cond_Wq': 8.0,
     'L3_cond_Wkv': 8.0,
     'L3_cond_Wo': 2.92,
     'L3_ffn_router_w': 3.266,
     'L3_ffn_W': 3.016,
     'L3_ffn_V': 3.615,
     'L3_ffn_W_out': 2.966}
    for name, (base, spread) in spreads.items():
        noise = np.random.default_rng([zlib.crc32(name.encode()), seed]).standard_normal(out[name].shape)
        drawn = base * np.exp(spread * noise) if base else spread * noise
        out[name] = jnp.asarray(drawn.astype(out[name].dtype))
    for name, factor in factors.items():
        out[name] = (out[name] * factor).astype(out[name].dtype)
    return out
```

```python
from contextlib import ExitStack, contextmanager

import concourse.bass as bass
from concourse import mybir

P = 128
B, S, D = 2, 1024, 256
TOK = B * S
NT = TOK // P
TB = S // P
KD = D // P
DH = 64
HEADS = 16
HG = 2
NG = HEADS // HG
CH = 512
NCH = TOK // CH
TPC = CH // P

ALU = mybir.AluOpType
ACT = mybir.ActivationFunctionType
AX = mybir.AxisListType
F32 = mybir.dt.float32
F32R = mybir.dt.float32r
U32 = mybir.dt.uint32
I32 = mybir.dt.int32
U8 = mybir.dt.uint8

FAR = -1.0e30


class Kit:

    def __init__(self, nc, ctx):
        self.nc, self.ctx = nc, ctx
        self.sem_ctx, self.sems = ctx, []

    @contextmanager
    def stage(self):
        before = self.sem_ctx, self.sems
        with ExitStack() as own:
            self.sem_ctx, self.sems = own, []
            yield
            with self.nc.Block() as block:
                @block.gpsimd
                def _(pool):
                    for s in self.sems:
                        pool.sem_clear(s)
        self.sem_ctx, self.sems = before

    def sb(self, name, shape, dtype=F32, ctx=None):
        return (ctx or self.ctx).enter_context(self.nc.sbuf_tensor(name, shape, dtype))

    def ps(self, name, shape, ctx):
        return ctx.enter_context(self.nc.psum_tensor(name, shape, F32))

    def sem(self, name):
        self.sems.append(self.sem_ctx.enter_context(self.nc.semaphore(name)))
        return self.sems[-1]


class Steps:

    def __init__(self, eng, sem):
        self.eng, self.sem, self.n = eng, sem, 0

    def did(self, instruction):
        instruction.then_inc(self.sem, 1)
        self.n += 1

    def settle(self):
        self.eng.wait_ge(self.sem, self.n)

    def then(self, instruction):
        self.did(instruction)
        self.settle()


def wait_apart(eng, sem, value, mark):
    eng.wait_ge(sem, value)
    eng.sem_inc(mark, 1)


def bc(ap, shape):
    return ap.broadcast_to(shape)


def to_feature_major(k, name, src, dst, ident):
    nc = k.nc
    NT = src.shape[1]
    turned, out_a, out_v = k.sem(name + "_turned"), k.sem(name + "_outa"), k.sem(name + "_outv")
    with ExitStack() as ctx:
        banks = [k.ps(f"{name}_ps{i}", [P, KD, 2 * P], ctx) for i in range(4)]
        with nc.Block() as block:
            @block.tensor
            def _(pe):
                for g in range(NT // 2):
                    if g >= 4:
                        pe.wait_ge(out_a if g % 2 == 0 else out_v, (g - 4) // 2 + 1)
                    for c in range(KD):
                        for t in range(2):
                            last = nc.tensor.transpose(banks[g % 4][:, c, t * P:(t + 1) * P],
                                                       src[:, 2 * g + t, c * P:(c + 1) * P], ident[:])
                    last.then_inc(turned, 1)

            @block.scalar
            def _(act):
                for g in range(0, NT // 2, 2):
                    act.wait_ge(turned, g + 1)
                    nc.scalar.activation(dst[:, :, 2 * g * P:(2 * g + 2) * P], banks[g % 4][:],
                                         ACT.Copy).then_inc(out_a, 1)

            @block.vector
            def _(dve):
                for g in range(1, NT // 2, 2):
                    dve.wait_ge(turned, g + 1)
                    nc.vector.tensor_copy(dst[:, :, 2 * g * P:(2 * g + 2) * P],
                                          banks[g % 4][:]).then_inc(out_v, 1)


def normalise(k, name, src, dst, gamma, eps, beta=None, add_to=None):
    nc = k.nc
    NT = src.shape[1]
    done, sd_ready, var_ready = k.sem(name + "_dve"), k.sem(name + "_sd"), k.sem(name + "_var")
    with ExitStack() as ctx:
        st = k.sb(name + "_st", [P, NT, 6], ctx=ctx)
        mv = k.sb(name + "_mv", [P, NT, 2], ctx=ctx)
        ve = k.sb(name + "_ve", [P, NT], ctx=ctx)
        sd = k.sb(name + "_sd_t", [P, NT], ctx=ctx)
        rs = k.sb(name + "_rs", [P, NT], ctx=ctx)
        tmp = k.sb(name + "_tmp", [P, NT, D], ctx=ctx)
        with nc.Block() as block:
            @block.vector
            def _(dve):
                s = Steps(dve, done)
                for t in range(NT):
                    s.did(nc.vector.bn_stats(st[:, t, :], src[:, t, :]))
                s.settle()
                for t in range(NT):
                    s.did(nc.vector.bn_aggr(mv[:, t, :], st[:, t, :]))
                s.settle()
                nc.vector.tensor_scalar(ve[:], mv[:, :, 1], eps, None, ALU.add).then_inc(var_ready, 1)
                dve.wait_ge(sd_ready, 1)
                s.then(nc.vector.reciprocal(rs[:], sd[:]))
                for t in range(NT):
                    s.did(nc.vector.tensor_scalar(tmp[:, t, :], src[:, t, :], mv[:, t, 0:1],
                                                  rs[:, t:t + 1], ALU.subtract, ALU.mult))
                s.settle()
                g = bc(gamma[:, None, :], [P, NT, D])
                more = [(add_to, ALU.add)] if add_to is not None else []
                if beta is not None:
                    more.insert(0, (bc(beta[:, None, :], [P, NT, D]), ALU.add))
                s.then(nc.vector.tensor_tensor(tmp[:] if more else dst[:], tmp[:], g, ALU.mult))
                for n, (other, op) in enumerate(more):
                    s.then(nc.vector.tensor_tensor(dst[:] if n == len(more) - 1 else tmp[:], tmp[:],
                                                   other[:] if other is add_to else other, op))

            @block.scalar
            def _(act):
                act.wait_ge(var_ready, 1)
                nc.scalar.activation(sd[:], ve[:], ACT.Sqrt).then_inc(sd_ready, 1)


def route(k, name, xT, w_dram, E, top, shares, bias=None, extra=None, scale=1.0, soft=None,
          ones=None):
    nc = k.nc
    EP = 8
    loaded, logit, dve_done, exped, iot = (k.sem(f"{name}_{s}") for s in
                                           ("loaded", "logit", "dve", "exp", "iota"))
    with ExitStack() as ctx:
        w = k.sb(name + "_w", [P, KD, E], ctx=ctx)
        bt = k.sb(name + "_b", [P, E], ctx=ctx)
        io = k.sb(name + "_io", [P, EP], ctx=ctx)
        L = k.sb(name + "_L", [P, NT, EP], ctx=ctx)
        M8 = k.sb(name + "_M8", [P, NT, 8], ctx=ctx)
        I8 = k.sb(name + "_I8", [P, NT, 8], U32, ctx=ctx)
        If = k.sb(name + "_If", [P, NT, 2], ctx=ctx)
        Ex = k.sb(name + "_E", [P, NT, EP], ctx=ctx)
        oh = k.sb(name + "_oh", [P, NT, EP], ctx=ctx)
        r1 = k.sb(name + "_r1", [P, NT], ctx=ctx)
        r2 = k.sb(name + "_r2", [P, NT], ctx=ctx)
        if extra is not None:
            condT_dram, wg_dram = extra
            cT = k.sb(name + "_cT", [DH, B], ctx=ctx)
            wg = k.sb(name + "_wg", [DH, E], ctx=ctx)
            cb = k.sb(name + "_cb", [DH, B, P], ctx=ctx)
        ps = k.ps(name + "_ps", [P, NT, E], ctx)
        n_loads = 1 + (bias is not None) + 2 * (extra is not None)
        with nc.Block() as block:
            @block.sync
            def _(sp):
                sp.dma_start(w[:], w_dram).then_inc(loaded, 16)
                if bias is not None:
                    sp.dma_start(bt[:], bias.partition_broadcast(P)).then_inc(loaded, 16)
                if extra is not None:
                    sp.dma_start(cT[:], condT_dram, allow_slow_non_contiguous=True).then_inc(loaded, 16)
                    sp.dma_start(wg[:], wg_dram).then_inc(loaded, 16)

            @block.gpsimd
            def _(pool):
                nc.gpsimd.iota(io[:], [[1, EP]], base=0, channel_multiplier=0,
                               allow_small_or_imprecise_dtypes=True).then_inc(iot, 1)

            @block.tensor
            def _(pe):
                pe.wait_ge(loaded, 16 * n_loads)
                if extra is not None:
                    pe.wait_ge(iot, 2)
                for t in range(NT):
                    for c in range(KD):
                        last = nc.tensor.matmul(ps[:, t, :], xT[:, c, t * P:(t + 1) * P], w[:, c, :],
                                                start=(c == 0), stop=(c == KD - 1 and extra is None))
                    if extra is not None:
                        last = nc.tensor.matmul(ps[:, t, :], cb[:, t // TB, :], wg[:],
                                                start=False, stop=True)
                last.then_inc(logit, 1)

            @block.scalar
            def _(act):
                if soft:
                    act.wait_ge(exped, 1)
                    nc.scalar.activation(Ex[:], Ex[:], ACT.Exp).then_inc(exped, 1)

            @block.vector
            def _(dve):
                s = Steps(dve, dve_done)
                if extra is not None:
                    dve.wait_ge(loaded, 16 * n_loads)
                    dve.wait_ge(iot, 1)
                    nc.vector.tensor_copy(cb[:], bc(cT[:, :, None], [DH, B, P])).then_inc(iot, 1)
                if E < EP:
                    s.then(nc.vector.memset(L[:], -3.0e38))
                dve.wait_ge(logit, 1)
                if bias is not None:
                    s.then(nc.vector.tensor_tensor(L[:, :, 0:E], ps[:], bc(bt[:, None, :], [P, NT, E]),
                                                   ALU.add))
                else:
                    s.then(nc.vector.tensor_scalar(L[:, :, 0:E], ps[:], scale, None, ALU.mult))
                for t in range(NT):
                    s.did(nc.vector.max(M8[:, t, :], L[:, t, :]))
                s.settle()
                for t in range(NT):
                    s.did(nc.vector.max_index(I8[:, t, :], M8[:, t, :], L[:, t, :]))
                s.settle()
                s.then(nc.vector.tensor_copy(If[:], I8[:, :, 0:2]))
                dve.wait_ge(iot, 1)
                iob = bc(io[:, None, 0:EP], [P, NT, EP])
                pick = ones if ones is not None else (shares if not soft else oh)
                s.then(nc.vector.tensor_tensor(pick[:], iob, bc(If[:, :, 0:1], [P, NT, EP]), ALU.is_equal))
                if top == 2:
                    s.then(nc.vector.tensor_tensor(Ex[:], iob, bc(If[:, :, 1:2], [P, NT, EP]),
                                                   ALU.is_equal))
                    s.then(nc.vector.tensor_tensor(pick[:], pick[:], Ex[:], ALU.add))
                if soft:
                    nc.vector.tensor_tensor(Ex[:], L[:], bc(M8[:, :, 0:1], [P, NT, EP]),
                                            ALU.subtract).then_inc(exped, 1)
                    dve.wait_ge(exped, 2)
                    if soft == "all":
                        s.then(nc.vector.reduce_sum(r1[:], Ex[:], AX.X))
                        s.then(nc.vector.reciprocal(r2[:], r1[:]))
                        s.then(nc.vector.tensor_tensor(Ex[:], Ex[:], bc(r2[:, :, None], [P, NT, EP]),
                                                       ALU.mult))
                    s.then(nc.vector.tensor_tensor(Ex[:], Ex[:], pick[:], ALU.mult))
                    s.then(nc.vector.reduce_sum(r1[:], Ex[:], AX.X))
                    if soft == "all":
                        s.then(nc.vector.tensor_scalar(r1[:], r1[:], 1e-20, None, ALU.add))
                    s.then(nc.vector.reciprocal(r2[:], r1[:]))
                    s.then(nc.vector.tensor_tensor(shares[:, :, 0:EP], Ex[:],
                                                   bc(r2[:, :, None], [P, NT, EP]), ALU.mult))


def gated_experts(k, name, xT, w_dram, n_experts, M, y, shares, kind):
    nc = k.nc
    MC = M // P
    per, groups_per = 2 * NCH * MC, 2 * NCH
    turns = n_experts // 2
    halves = TPC // 2
    WF = 2 * KD * M + MC * D
    gu_done, f_done, g_done, a_done, down_done, added, zeroed = (
        k.sem(f"{name}_{s}") for s in ("gu", "f", "g", "a", "down", "added", "zeroed"))
    w_loaded = [k.sem(f"{name}_wload{u}") for u in range(2)]
    with ExitStack() as ctx:
        w = [k.sb(f"{name}_w{u}", [P, WF], ctx=ctx) for u in range(2)]
        gate = [x[:, 0:KD * M].rearrange("p (c m) -> p c m", c=KD) for x in w]
        up = [x[:, KD * M:2 * KD * M].rearrange("p (c m) -> p c m", c=KD) for x in w]
        down = [x[:, 2 * KD * M:WF].rearrange("p (j d) -> p j d", j=MC) for x in w]
        fs = [k.sb(f"{name}_f{i}", [P, CH], ctx=ctx) for i in range(2)]
        gs = [k.sb(f"{name}_g{i}", [P, CH], ctx=ctx) for i in range(2)]
        hid = [k.sb(f"{name}_h{i}", [P, MC, CH], ctx=ctx) for i in range(2)]
        gps = [k.ps(f"{name}_gps{i}", [P, CH], ctx) for i in range(2)]
        ups = [k.ps(f"{name}_ups{i}", [P, CH], ctx) for i in range(2)]
        dps = [k.ps(f"{name}_dps{i}", [P, 2, D], ctx) for i in range(4)]
        steps = [(u, c, m) for u in range(2) for c in range(NCH) for m in range(MC)]
        with nc.Block() as block:
            @block.sync
            def _(sp):
                for u in range(2):
                    sp.dma_start(w[u][:], w_dram[u]).then_inc(w_loaded[u], 16)
                with sp.Fori(0, turns - 1) as i:
                    for u in range(2):
                        sp.wait_ge(down_done, halves * NCH * (2 * i + u + 1))
                        sp.dma_start(w[u][:], w_dram[2 * i + (2 + u)]).then_inc(w_loaded[u], 16)

            @block.gpsimd
            def _(pool):
                nc.gpsimd.memset(y[:], 0.0).then_inc(zeroed, 1)

            @block.tensor
            def _(pe):
                def gate_up(i, n):
                    u, c, m = steps[n]
                    if c == 0 and m == 0:
                        pe.wait_ge(w_loaded[u], 16 * i + 16)
                    pe.wait_ge(a_done, per * i + (n + 1))
                    for ps, wt in ((gps, gate), (ups, up)):
                        for c2 in range(KD):
                            last = nc.tensor.matmul(ps[n % 2][:], wt[u][:, c2, m * P:(m + 1) * P],
                                                    xT[:, c2, c * CH:(c + 1) * CH],
                                                    start=(c2 == 0), stop=(c2 == KD - 1))
                    last.then_inc(gu_done, 1)

                def down_projection(i, q):
                    pe.wait_ge(a_done, per * i + ((q + 1) * MC + 2))
                    for t2 in range(halves):
                        pe.wait_ge(added, halves * groups_per * i + (halves * q + t2 + 1))
                        for t in range(2):
                            for m in range(MC):
                                last = nc.tensor.matmul(
                                    dps[(halves * q + t2) % 4][:, t, :],
                                    hid[q % 2][:, m, (2 * t2 + t) * P:(2 * t2 + t + 1) * P],
                                    down[q // NCH][:, m, :], start=(m == 0), stop=(m == MC - 1))
                        last.then_inc(down_done, 1)

                with pe.Fori(0, turns) as i:
                    gate_up(i, 0)
                    for n in range(per):
                        if n + 1 < per:
                            gate_up(i, n + 1)
                        if n % MC == MC - 1:
                            down_projection(i, n // MC)

            @block.scalar
            def _(act):
                with act.Fori(0, turns) as i:
                    for n in range(per):
                        act.wait_ge(a_done, per * i + (n + 1))
                        act.wait_ge(gu_done, per * i + (n + 1))
                        if kind == "leaky":
                            nc.scalar.activation(fs[n % 2][:], gps[n % 2][:], ACT.Copy).then_inc(f_done, 1)
                        else:
                            nc.scalar.activation(fs[n % 2][:], ups[n % 2][:], ACT.Silu).then_inc(f_done, 1)

            @block.vector
            def _(dve):
                dve.sem_inc(a_done, 2)
                dve.sem_inc(added, 4)
                dve.wait_ge(zeroed, 1)

                def activate(i, n):
                    q, m = n // MC, n % MC
                    if m == 0 and q >= 2:
                        dve.wait_ge(down_done, halves * groups_per * i + halves * (q - 1))
                    dve.wait_ge(f_done, per * i + (n + 1))
                    h = hid[q % 2][:, m, :]
                    if kind == "leaky":
                        nc.vector.scalar_tensor_tensor(out=gs[n % 2][:], in0=fs[n % 2][:], scalar=0.01,
                                                       in1=gps[n % 2][:], op0=ALU.mult,
                                                       op1=ALU.max).then_inc(g_done, 1)
                        dve.wait_ge(g_done, per * i + (n + 1))
                        nc.vector.tensor_tensor(h, gs[n % 2][:], ups[n % 2][:], ALU.mult).then_inc(a_done, 1)
                    else:
                        nc.vector.tensor_tensor(h, fs[n % 2][:], gps[n % 2][:], ALU.mult).then_inc(a_done, 1)

                def accumulate(i, q):
                    u, c = q // NCH, q % NCH
                    for t2 in range(halves):
                        at = halves * groups_per * i + (halves * q + t2 + 1)
                        dve.wait_ge(added, at)
                        dve.wait_ge(down_done, at)
                        for t in range(2):
                            tt = c * TPC + 2 * t2 + t
                            last = nc.vector.scalar_tensor_tensor(
                                out=y[:, tt, :], in0=dps[(halves * q + t2) % 4][:, t, :],
                                scalar=shares[:, tt, bass.ds(2 * i + u, 1)], in1=y[:, tt, :],
                                op0=ALU.mult, op1=ALU.add)
                        last.then_inc(added, 1)

                with dve.Fori(0, turns) as i:
                    for n in range(per):
                        activate(i, n)
                        if n % MC == MC - 1 and n // MC >= 1:
                            accumulate(i, n // MC - 1)
                    accumulate(i, groups_per - 1)


def picked_ffn(k, name, src, picked, w1_dram, b1_dram, wo_dram, bo_dram, dst, ident, E):
    nc = k.nc
    FC = b1_dram.shape[1] // P
    loaded, masked, turned, taken, hps_done, gelu_done, out_done, out_sum, dve_done, ohT = (
        k.sem(f"{name}_{s}") for s in
        ("loaded", "masked", "turned", "taken", "hps", "gelu", "out", "sum", "dve", "ohT"))
    TG = E * TPC // 2
    with ExitStack() as ctx:
        w1 = k.sb(name + "_w1", [P, E, KD, FC * P], ctx=ctx)
        b1 = k.sb(name + "_b1", [E, FC * P], ctx=ctx)
        wo = k.sb(name + "_wo", [P, FC, D], ctx=ctx)
        bo = k.sb(name + "_bo", [P, D], ctx=ctx)
        ym = k.sb(name + "_ym", [P, E, TPC, D], ctx=ctx)
        ymT = k.sb(name + "_ymT", [P, E, KD, CH], ctx=ctx)
        pk = k.sb(name + "_pk", [P, TPC, E], ctx=ctx)
        pkT = k.sb(name + "_pkT", [E, CH], ctx=ctx)
        hid = k.sb(name + "_hid", [P, FC, CH], ctx=ctx)
        tmp = k.sb(name + "_tmp", [P, 2, 2, D], ctx=ctx)
        tps = [k.ps(f"{name}_tps{i}", [P, KD, 2 * P], ctx) for i in range(2)]
        hps = [k.ps(f"{name}_hps{i}", [P, CH], ctx) for i in range(2)]
        ops = [k.ps(f"{name}_ops{i}", [P, 2, D], ctx) for i in range(2)]
        kps = k.ps(name + "_kps", [E, CH], ctx)
        with nc.Block() as block:
            @block.sync
            def _(sp):
                sp.dma_start(w1[:], w1_dram).then_inc(loaded, 16)
                sp.dma_start(b1[:], b1_dram).then_inc(loaded, 16)
                sp.dma_start(wo[:], wo_dram).then_inc(loaded, 16)
                sp.dma_start(bo[:], bo_dram.partition_broadcast(P)).then_inc(loaded, 16)

            @block.tensor
            def _(pe):
                with pe.Fori(0, NCH) as c:
                    pe.wait_ge(masked, (E + 1) * c + (E + 1))
                    for t in range(TPC):
                        last = nc.tensor.transpose(kps[:, t * P:(t + 1) * P], pk[:, t, :], ident[:])
                    last.then_inc(ohT, 1)
                    for g in range(TG):
                        e, t2 = g // 2, g % 2
                        pe.wait_ge(taken, TG * c + (g + 1))
                        for c2 in range(KD):
                            for t in range(2):
                                last = nc.tensor.transpose(tps[g % 2][:, c2, t * P:(t + 1) * P],
                                                           ym[:, e, 2 * t2 + t, c2 * P:(c2 + 1) * P],
                                                           ident[:])
                        last.then_inc(turned, 1)
                    pe.wait_ge(loaded, 64)
                    pe.wait_ge(taken, TG * c + (TG + 2))
                    pe.wait_ge(ohT, 2 * c + 2)
                    for f in range(FC):
                        pe.wait_ge(gelu_done, FC * c + (f + 1))
                        for e in range(E):
                            for c2 in range(KD):
                                nc.tensor.matmul(hps[f % 2][:], w1[:, e, c2, f * P:(f + 1) * P],
                                                 ymT[:, e, c2, :], start=(e == 0 and c2 == 0), stop=False)
                        nc.tensor.matmul(hps[f % 2][:], b1[:, f * P:(f + 1) * P], pkT[:],
                                         start=False, stop=True).then_inc(hps_done, 1)
                    pe.wait_ge(gelu_done, FC * c + (FC + 2))
                    for t2 in range(2):
                        pe.wait_ge(out_sum, 2 * c + (t2 + 1))
                        for t in range(2):
                            for f in range(FC):
                                last = nc.tensor.matmul(ops[t2][:, t, :],
                                                        hid[:, f, (2 * t2 + t) * P:(2 * t2 + t + 1) * P],
                                                        wo[:, f, :], start=(f == 0), stop=(f == FC - 1))
                        last.then_inc(out_done, 1)

            @block.scalar
            def _(act):
                act.sem_inc(gelu_done, 2)
                with act.Fori(0, NCH) as c:
                    for f in range(FC):
                        if f == 0:
                            act.wait_ge(out_done, 2 * c + 1)
                        act.wait_ge(hps_done, FC * c + (f + 1))
                        nc.scalar.activation(hid[:, f, :], hps[f % 2][:], ACT.Gelu).then_inc(gelu_done, 1)

            @block.vector
            def _(dve):
                dve.sem_inc(out_done, 1)
                dve.sem_inc(taken, 2)
                dve.sem_inc(out_sum, 2)
                dve.wait_ge(loaded, 64)
                with dve.Fori(0, NCH) as c:
                    dve.wait_ge(out_done, 2 * c + 1)
                    nc.vector.tensor_copy(pk[:], picked[:, bass.ts(c, TPC), 0:E]).then_inc(masked, 1)
                    for e in range(E):
                        nc.vector.tensor_tensor(ym[:, e], src[:, bass.ts(c, TPC), :],
                                                bc(picked[:, bass.ts(c, TPC), e:e + 1], [P, TPC, D]),
                                                ALU.mult).then_inc(masked, 1)
                    dve.wait_ge(ohT, 2 * c + 1)
                    nc.vector.tensor_copy(pkT[:], kps[:]).then_inc(ohT, 1)
                    for g in range(TG):
                        e, t2 = g // 2, g % 2
                        dve.wait_ge(turned, TG * c + (g + 1))
                        nc.vector.tensor_copy(ymT[:, e, :, 2 * t2 * P:(2 * t2 + 2) * P],
                                              tps[g % 2][:]).then_inc(taken, 1)
                    for t2 in range(2):
                        dve.wait_ge(out_done, 2 * c + (t2 + 2))
                        dve.wait_ge(out_sum, 2 * c + (t2 + 1))
                        nc.vector.tensor_tensor(tmp[:, t2], ops[t2][:], bc(bo[:, None, :], [P, 2, D]),
                                                ALU.add).then_inc(dve_done, 1)
                        dve.wait_ge(dve_done, 2 * c + (t2 + 1))
                        nc.vector.tensor_tensor(dst[:, bass.ds(c * TPC + 2 * t2, 2), :], tmp[:, t2],
                                                src[:, bass.ds(c * TPC + 2 * t2, 2), :],
                                                ALU.add).then_inc(out_sum, 1)


def lora_ffn(k, name, xT, picked, w, x, ident):
    nc = k.nc
    wi_dram, bi_dram, wo_dram, bo_dram, la_dram, lb_dram = w
    R = la_dram.shape[2]
    E = 8
    FC = wi_dram.shape[2] // P
    loaded, spread, turned, pick_done, u_done, u_masked, hps_done, relu_done, out_done, out_sum, dve_done = (
        k.sem(f"{name}_{s}") for s in ("loaded", "spread", "turned", "pick", "u", "um", "hps", "relu",
                                       "out", "sum", "dve"))
    with ExitStack() as ctx:
        wi = k.sb(name + "_wi", [P, KD, FC * P], ctx=ctx)
        bi = k.sb(name + "_bi", [P, FC], ctx=ctx)
        wo = k.sb(name + "_wo", [P, FC, D], ctx=ctx)
        bo = k.sb(name + "_bo", [P, D], ctx=ctx)
        la = k.sb(name + "_la", [P, KD, R], ctx=ctx)
        lb = k.sb(name + "_lb", [R, FC * P], ctx=ctx)
        pk = k.sb(name + "_pk", [P, TPC, R], ctx=ctx)
        pkT = k.sb(name + "_pkT", [R, CH], ctx=ctx)
        um = k.sb(name + "_um", [R, CH], ctx=ctx)
        hid = k.sb(name + "_hid", [P, FC, CH], ctx=ctx)
        tmp = k.sb(name + "_tmp", [P, 2, 2, D], ctx=ctx)
        hps = [k.ps(f"{name}_hps{i}", [P, CH], ctx) for i in range(2)]
        ops = [k.ps(f"{name}_ops{i}", [P, 2, D], ctx) for i in range(2)]
        kps = k.ps(name + "_kps", [R, CH], ctx)
        ups = k.ps(name + "_ups", [R, CH], ctx)
        with nc.Block() as block:
            @block.sync
            def _(sp):
                for tile, dram in ((wi, wi_dram), (bi, bi_dram), (wo, wo_dram), (la, la_dram), (lb, lb_dram)):
                    sp.dma_start(tile[:], dram).then_inc(loaded, 16)
                sp.dma_start(bo[:], bo_dram.partition_broadcast(P)).then_inc(loaded, 16)

            @block.tensor
            def _(pe):
                pe.wait_ge(loaded, 6 * 16)
                with pe.Fori(0, NCH) as c:
                    pe.wait_ge(spread, c + 1)
                    for t in range(TPC):
                        last = nc.tensor.transpose(kps[:, t * P:(t + 1) * P], pk[:, t, :], ident[:])
                    last.then_inc(turned, 1)
                    for c2 in range(KD):
                        last = nc.tensor.matmul(ups[:], la[:, c2, :], xT[:, c2, bass.ts(c, CH)],
                                                start=(c2 == 0), stop=(c2 == KD - 1))
                    last.then_inc(u_done, 1)
                    pe.wait_ge(u_masked, c + 1)
                    for f in range(FC):
                        pe.wait_ge(relu_done, FC * c + (f + 1))
                        for c2 in range(KD):
                            nc.tensor.matmul(hps[f % 2][:], wi[:, c2, f * P:(f + 1) * P],
                                             xT[:, c2, bass.ts(c, CH)], start=(c2 == 0), stop=False)
                        nc.tensor.matmul(hps[f % 2][:], lb[:, f * P:(f + 1) * P], um[:],
                                         start=False, stop=True).then_inc(hps_done, 1)
                    pe.wait_ge(relu_done, FC * c + (FC + 2))
                    for t2 in range(2):
                        pe.wait_ge(out_sum, 2 * c + (t2 + 1))
                        for t in range(2):
                            for f in range(FC):
                                last = nc.tensor.matmul(ops[t2][:, t, :],
                                                        hid[:, f, (2 * t2 + t) * P:(2 * t2 + t + 1) * P],
                                                        wo[:, f, :], start=(f == 0), stop=(f == FC - 1))
                        last.then_inc(out_done, 1)

            @block.scalar
            def _(act):
                act.sem_inc(relu_done, 2)
                act.wait_ge(loaded, 6 * 16)
                with act.Fori(0, NCH) as c:
                    for f in range(FC):
                        if f == 0:
                            act.wait_ge(out_done, 2 * c + 1)
                        act.wait_ge(hps_done, FC * c + (f + 1))
                        nc.scalar.activation(hid[:, f, :], hps[f % 2][:], ACT.Relu,
                                             bias=bi[:, f:f + 1]).then_inc(relu_done, 1)

            @block.vector
            def _(dve):
                dve.sem_inc(out_done, 1)
                dve.sem_inc(out_sum, 2)
                dve.wait_ge(loaded, 6 * 16)
                with dve.Fori(0, NCH) as c:
                    dve.wait_ge(out_done, 2 * c + 1)
                    nc.vector.tensor_copy(pk[:].rearrange("p t (e r) -> p t e r", e=E),
                                          bc(picked[:, bass.ts(c, TPC), :, None], [P, TPC, E, R // E])
                                          ).then_inc(spread, 1)
                    dve.wait_ge(turned, c + 1)
                    nc.vector.tensor_copy(pkT[:], kps[:]).then_inc(pick_done, 1)
                    dve.wait_ge(u_done, c + 1)
                    dve.wait_ge(pick_done, c + 1)
                    nc.vector.tensor_tensor(um[:], ups[:], pkT[:], ALU.mult).then_inc(u_masked, 1)
                    for t2 in range(2):
                        rows = x[:, bass.ds(c * TPC + 2 * t2, 2), :]
                        dve.wait_ge(out_done, 2 * c + (t2 + 2))
                        dve.wait_ge(out_sum, 2 * c + (t2 + 1))
                        nc.vector.tensor_tensor(tmp[:, t2], ops[t2][:], bc(bo[:, None, :], [P, 2, D]),
                                                ALU.add).then_inc(dve_done, 1)
                        dve.wait_ge(dve_done, 2 * c + (t2 + 1))
                        nc.vector.tensor_tensor(rows, tmp[:, t2], rows, ALU.add).then_inc(out_sum, 1)


def round_to_e4m3(k, name, src, dst, in_scale_dram, scale_out):
    nc = k.nc
    loaded, done = k.sem(name + "_loaded"), k.sem(name + "_done")
    with ExitStack() as ctx:
        v = k.sb(name + "_v", [P, NT, D], ctx=ctx)
        m = k.sb(name + "_m", [P, NT, D], ctx=ctx)
        r = k.sb(name + "_r", [P, 1], ctx=ctx)
        with nc.Block() as block:
            @block.sync
            def _(sp):
                sp.dma_start(scale_out[:], in_scale_dram.partition_broadcast(P)).then_inc(loaded, 16)

            @block.vector
            def _(dve):
                s = Steps(dve, done)
                dve.wait_ge(loaded, 16)
                s.then(nc.vector.reciprocal(r[:], scale_out[:]))
                s.then(nc.vector.tensor_scalar(v[:], src[:], r[:, 0:1], 448.0, ALU.mult, ALU.min))
                s.then(nc.vector.tensor_scalar(v[:], v[:], -448.0, None, ALU.max))
                s.then(nc.vector.tensor_scalar(m[:].bitcast(U32), v[:].bitcast(U32), 0x7F800000, None,
                                               ALU.bitwise_and))
                s.then(nc.vector.tensor_scalar(m[:], m[:], 2.0 ** -6, 1.5 * 2.0 ** 20, ALU.max, ALU.mult))
                s.then(nc.vector.tensor_tensor(v[:], v[:], m[:], ALU.add))
                s.then(nc.vector.tensor_tensor(v[:], v[:], m[:], ALU.subtract))
                nc.vector.tensor_scalar(dst[:], v[:], scale_out[:, 0:1], None, ALU.mult)


def linear(k, name, xT, w_dram, scale_dram, bias_dram, x):
    nc = k.nc
    loaded, scaled, mm, tmp_done, added = (k.sem(f"{name}_{s}") for s in
                                           ("loaded", "scaled", "mm", "tmp", "added"))
    with ExitStack() as ctx:
        w = k.sb(name + "_w", [P, KD, D], ctx=ctx)
        ws = k.sb(name + "_ws", [P, KD, D], ctx=ctx)
        bo = k.sb(name + "_b", [P, D], ctx=ctx)
        sc = k.sb(name + "_sc", [P, 1], ctx=ctx)
        tmp = k.sb(name + "_tmp", [P, 4, 2, D], ctx=ctx)
        ps = [k.ps(f"{name}_ps{i}", [P, 2, D], ctx) for i in range(4)]
        with nc.Block() as block:
            @block.sync
            def _(sp):
                sp.dma_start(w[:], w_dram).then_inc(loaded, 16)
                sp.dma_start(bo[:], bias_dram.partition_broadcast(P)).then_inc(loaded, 16)
                sp.dma_start(sc[:], scale_dram.partition_broadcast(P)).then_inc(loaded, 16)

            @block.tensor
            def _(pe):
                pe.wait_ge(scaled, 1)
                for t2 in range(NT // 2):
                    if t2 >= 4:
                        pe.wait_ge(tmp_done, t2 - 3)
                    for t in range(2):
                        tt = 2 * t2 + t
                        for c in range(KD):
                            last = nc.tensor.matmul(ps[t2 % 4][:, t, :], xT[:, c, tt * P:(tt + 1) * P],
                                                    ws[:, c, :], start=(c == 0), stop=(c == KD - 1))
                    last.then_inc(mm, 1)

            @block.vector
            def _(dve):
                dve.wait_ge(loaded, 48)
                nc.vector.tensor_scalar(ws[:], w[:], sc[:, 0:1], None, ALU.mult).then_inc(scaled, 1)
                for t2 in range(NT // 2):
                    rows = x[:, 2 * t2:2 * t2 + 2, :]
                    dve.wait_ge(mm, t2 + 1)
                    nc.vector.tensor_tensor(tmp[:, t2 % 4], ps[t2 % 4][:], bc(bo[:, None, :], [P, 2, D]),
                                            ALU.add).then_inc(tmp_done, 1)
                    dve.wait_ge(tmp_done, t2 + 1)
                    nc.vector.tensor_tensor(rows, tmp[:, t2 % 4], rows, ALU.add).then_inc(added, 1)


CAPACITY = 2 * (2 * 512) * 2 // 8


def places(k, name, chosen, rank, upper):
    nc = k.nc
    EP = 8
    made, mm, done = k.sem(name + "_made"), k.sem(name + "_mm"), k.sem(name + "_done")
    with ExitStack() as ctx:
        ones = k.sb(name + "_ones", [P, P], ctx=ctx)
        before = k.sb(name + "_before", [P, NT, EP], ctx=ctx)
        cps = k.ps(name + "_cps", [P, NT, EP], ctx)
        tps = k.ps(name + "_tps", [P, NT, EP], ctx)
        with nc.Block() as block:
            @block.gpsimd
            def _(pool):
                nc.gpsimd.memset(ones[:], 1.0).then_inc(made, 1)

            @block.tensor
            def _(pe):
                pe.wait_ge(made, 1)
                nc.tensor.matmul(cps[:], upper[:], chosen[:], start=True, stop=True).then_inc(mm, 1)
                nc.tensor.matmul(tps[:], ones[:], chosen[:], start=True, stop=True).then_inc(mm, 1)

            @block.vector
            def _(dve):
                s = Steps(dve, done)
                s.then(nc.vector.memset(before[:], 0.0))
                dve.wait_ge(mm, 2)
                for t in range(1, NT):
                    s.then(nc.vector.tensor_tensor(before[:, t, :], tps[:, t - 1, :], before[:, t - 1, :],
                                                   ALU.add))
                s.then(nc.vector.tensor_tensor(rank[:], cps[:], before[:], ALU.add))


def drop_over_capacity(k, name, shares, rank):
    nc = k.nc
    done = k.sem(name)
    with nc.Block() as block:
        @block.vector
        def _(dve):
            s = Steps(dve, done)
            s.then(nc.vector.tensor_scalar(rank[:], rank[:], float(CAPACITY), None, ALU.is_le))
            s.then(nc.vector.tensor_tensor(shares[:], shares[:], rank[:], ALU.mult))


TABLE = S + P - 1


def position_table(k, a, table_dram, ident):
    nc = k.nc
    NPT = S // P
    with ExitStack() as ctx:
        w0, b0, g0, b1, g1 = (k.sb("pt_" + n, [P, D], ctx=ctx) for n in ("w0", "b0", "g0", "b1", "g1"))
        w1 = k.sb("pt_w1", [P, KD, D], ctx=ctx)
        w2 = k.sb("pt_w2", [P, KD, HEADS], ctx=ctx)
        b2 = k.sb("pt_b2", [HEADS, 1], ctx=ctx)
        pos = k.sb("pt_pos", [P, NPT], ctx=ctx)
        h = k.sb("pt_h", [P, NPT, D], ctx=ctx)
        hn = k.sb("pt_hn", [P, NPT, D], ctx=ctx)
        hT = k.sb("pt_hT", [P, KD, S], ctx=ctx)
        tab = k.sb("pt_tab", [HEADS, TABLE], ctx=ctx)
        loaded, posd, made = k.sem("pt_loaded"), k.sem("pt_posd"), k.sem("pt_made")
        mm, stored, act_done = k.sem("pt_mm"), k.sem("pt_stored"), k.sem("pt_act")
        with nc.Block() as block:
            @block.sync
            def _(sp):
                for tile, n in ((w0, "w0"), (b0, "b0"), (g0, "g0"), (b1, "b1"), (g1, "g1")):
                    sp.dma_start(tile[:], a["l1_" + n].partition_broadcast(P)).then_inc(loaded, 16)
                sp.dma_start(w1[:], a["l1_w1"]).then_inc(loaded, 16)
                sp.dma_start(w2[:], a["l1_w2"]).then_inc(loaded, 16)
                sp.dma_start(b2[:], a["l1_b2"].rearrange("(h o) -> h o", o=1),
                             allow_slow_non_contiguous=True).then_inc(loaded, 16)
                sp.wait_ge(loaded, 8 * 16)

            @block.gpsimd
            def _(pool):
                nc.gpsimd.iota(pos[:], [[P, NPT]], base=0, channel_multiplier=1,
                               allow_small_or_imprecise_dtypes=True).then_inc(posd, 1)

            @block.vector
            def _(dve):
                dve.wait_ge(loaded, 8 * 16)
                dve.wait_ge(posd, 1)
                for t in range(NPT):
                    nc.vector.scalar_tensor_tensor(out=h[:, t, :], in0=w0[:], scalar=pos[:, t:t + 1],
                                                   in1=b0[:], op0=ALU.mult, op1=ALU.add)
        normalise(k, "pt_n0", h, hn, g0, 1e-5)
        with nc.Block() as block:
            @block.scalar
            def _(act):
                nc.scalar.activation(h[:], hn[:], ACT.Silu)
        to_feature_major(k, "pt_t0", h, hT, ident)
        with ExitStack() as inner:
            ps = [k.ps(f"pt_ps{i}", [P, 2, D], inner) for i in range(4)]
            with nc.Block() as block:
                @block.tensor
                def _(pe):
                    for t in range(NPT):
                        for c in range(KD):
                            last = nc.tensor.matmul(ps[t // 2][:, t % 2, :], hT[:, c, t * P:(t + 1) * P],
                                                    w1[:, c, :], start=(c == 0), stop=(c == KD - 1))
                        last.then_inc(mm, 1)

                @block.vector
                def _(dve):
                    for t2 in range(NPT // 2):
                        dve.wait_ge(mm, 2 * t2 + 2)
                        nc.vector.tensor_tensor(h[:, 2 * t2:2 * t2 + 2, :], ps[t2][:],
                                                bc(b1[:, None, :], [P, 2, D]), ALU.add)
        normalise(k, "pt_n1", h, hn, g1, 1e-5)
        with nc.Block() as block:
            @block.scalar
            def _(act):
                nc.scalar.activation(h[:], hn[:], ACT.Silu)
        to_feature_major(k, "pt_t1", h, hT, ident)
        with ExitStack() as inner:
            ps = [k.ps(f"pt_qs{i}", [HEADS, CH], inner) for i in range(2)]
            with nc.Block() as block:
                @block.tensor
                def _(pe):
                    for i in range(2):
                        for c in range(KD):
                            last = nc.tensor.matmul(ps[i][:], w2[:, c, :], hT[:, c, i * CH:(i + 1) * CH],
                                                    start=(c == 0), stop=(c == KD - 1))
                        last.then_inc(mm, 1)

                @block.vector
                def _(dve):
                    nc.vector.memset(tab[:, 0:P - 1], FAR).then_inc(made, 1)
                    for i in range(2):
                        dve.wait_ge(mm, NPT + i + 1)
                        nc.vector.tensor_scalar(tab[:, P - 1 + i * CH:P - 1 + (i + 1) * CH], ps[i][:],
                                                b2[:, 0:1], None, ALU.add).then_inc(made, 1)

                @block.sync
                def _(sp):
                    sp.wait_ge(made, 3)
                    sp.dma_start(table_dram, tab[:]).then_inc(stored, 16)
                    sp.wait_ge(stored, 16)


def attention(k, name, xT, w, cond_dram, mask_dram, acc, ident, bias_dram, table=False, l2=None):
    nc = k.nc
    wq_dram, wkv_dram, wo_dram, nb_dram = w
    s8 = lambda n: k.sem(f"{name}_{n}")
    ctx = ExitStack()
    with ctx:
        kA = k.sb(name + "_kA", [P, B, S], F32R, ctx=ctx)
        kB = k.sb(name + "_kB", [P, B, S], F32R, ctx=ctx)
        V = k.sb(name + "_V", [P, B, TB, 2 * DH], F32R, ctx=ctx)
        SN = k.sb(name + "_SN", [P, NT, HEADS], ctx=ctx)
        cond = k.sb(name + "_cond", [P, 2, DH], ctx=ctx)
        nb = k.sb(name + "_nb", [P, HEADS], ctx=ctx)
        keys_and_values(k, name + "_kv", xT, wq_dram, wkv_dram, cond_dram, nb_dram, mask_dram, ident,
                        kA, kB, V, SN, cond, nb, table, l2)
        heads_loop(k, name, xT, wq_dram, wo_dram, acc, ident, bias_dram, table, l2 is not None,
                   kA, kB, V, SN, cond, nb)


def keys_and_values(k, name, xT, wq_dram, wkv_dram, cond_dram, nb_dram, mask_dram, ident,
                    kA, kB, V, SN, cond, nb, table, l2):
    nc = k.nc
    scale = 8.0 if l2 else DH ** -0.5
    NB = B * TB
    loaded, dve_done, act_done, mm, pool_done = (k.sem(f"{name}_{s}") for s in
                                                 ("loaded", "dve", "act", "mm", "pool"))
    with ExitStack() as ctx:
        wq = k.sb(name + "_wq", [P, KD, HEADS * DH], ctx=ctx)
        wkv = k.sb(name + "_wkv", [P, KD, 2 * DH], ctx=ctx)
        prod = k.sb(name + "_prod", [P, KD, HEADS * DH], ctx=ctx)
        U = k.sb(name + "_U", [P, KD * HEADS], ctx=ctx)
        kn = k.sb(name + "_kn", [P, DH], ctx=ctx)
        qk = k.sb(name + "_qk", [P, 2, DH], ctx=ctx)
        sq = k.sb(name + "_sq", [P, NB, DH], ctx=ctx)
        n1 = k.sb(name + "_n1", [P, NB], ctx=ctx)
        n2 = k.sb(name + "_n2", [P, NB], ctx=ctx)
        kf = k.sb(name + "_kf", [P, NB, DH], ctx=ctx)
        sA = k.sb(name + "_sA", [P, NB, 2 * DH], F32R, ctx=ctx)
        sB = k.sb(name + "_sB", [P, NB, 2 * DH], F32R, ctx=ctx)
        mrow = k.sb(name + "_mrow", [P, B, S], mask_dram.dtype, ctx=ctx)
        kvps = [k.ps(f"{name}_kvps{i}", [P, 4, 2 * DH], ctx) for i in range(4)]
        snps = k.ps(name + "_snps", [P, NT, HEADS], ctx)
        tps = [k.ps(f"{name}_tps{i}", [P, 4, P], ctx) for i in range(2)]
        n_loads = 5 + 2 * bool(l2)

        xk = k.sb(name + "_xk", [P, KD, TOK], ctx=ctx) if table else xT
        turned_round = k.sem(name + "_turned_round")

        with nc.Block() as block:
            @block.sync
            def _(sp):
                sp.dma_start(cond[:], cond_dram.partition_broadcast(P)).then_inc(loaded, 16)
                sp.dma_start(nb[:], nb_dram.partition_broadcast(P)).then_inc(loaded, 16)
                sp.dma_start(wkv[:], wkv_dram).then_inc(loaded, 16)
                sp.dma_start(wq[:], wq_dram).then_inc(loaded, 16)
                sp.dma_start(mrow[DH:DH + 1, :, :], mask_dram[None, :, :]).then_inc(loaded, 16)
                if l2:
                    for n in range(2):
                        sp.dma_start(qk[:, n, :], l2[n].partition_broadcast(P)).then_inc(loaded, 16)

            @block.gpsimd
            def _(pool):
                nc.gpsimd.memset(sB[:].bitcast(F32), 0.0).then_inc(pool_done, 1)

            @block.tensor
            def _(pe):
                pe.wait_ge(loaded, 16 * n_loads)
                if table:
                    pe.wait_ge(turned_round, KD * B)
                for n in range(NB):
                    for c in range(KD):
                        last = nc.tensor.matmul(kvps[n // 4][:, n % 4, :], xk[:, c, n * P:(n + 1) * P],
                                                wkv[:, c, :], start=(c == 0), stop=(c == KD - 1))
                last.then_inc(mm, 1)
                pe.wait_ge(pool_done, 2)
                for t in range(NT):
                    for c in range(KD):
                        last = nc.tensor.matmul(snps[:, t, :], xT[:, c, t * P:(t + 1) * P],
                                                U[:, c * HEADS:(c + 1) * HEADS],
                                                start=(c == 0), stop=(c == KD - 1))
                last.then_inc(mm, 1)
                pe.wait_ge(pool_done, 3)
                for g in range(2 * NB // 4):
                    src = (sA if g < NB // 4 else sB)[:].bitcast(F32)
                    if g >= 2:
                        pe.wait_ge(act_done, g - 1)
                    for j in range(4):
                        last = nc.tensor.transpose(tps[g % 2][:, j, :], src[:, (g % (NB // 4)) * 4 + j, :],
                                                   ident[:])
                    last.then_inc(mm, 1)

            squares, roots = k.sem(name + "_squares"), k.sem(name + "_roots")

            @block.scalar
            def _(act):
                if table:
                    for c in range(KD):
                        for b in range(B):
                            row = xT[:, c, :].rearrange("p (b s) -> p b s", b=B)[:, b, ::-1]
                            nc.scalar.activation(xk[:, c, b * S:(b + 1) * S], row,
                                                 ACT.Copy).then_inc(turned_round, 1)
                if l2:
                    act.wait_ge(mm, 1)
                    for i in range(4):
                        nc.scalar.activation(sq[:, 4 * i:4 * i + 4, :], kvps[i][:, :, 0:DH],
                                             ACT.Square).then_inc(squares, 1)
                    act.wait_ge(roots, 1)
                    nc.scalar.activation(n2[:, 0:1], n1[:, 0:1], ACT.Sqrt).then_inc(roots, 1)
                    act.wait_ge(roots, 3)
                    nc.scalar.activation(n2[:], n1[:], ACT.Sqrt).then_inc(roots, 1)
                for g in range(2 * NB // 4):
                    act.wait_ge(mm, g + 3)
                    dst = (kA if g < NB // 4 else kB)[:].rearrange("p b s -> p (b s)")
                    at = (g % (NB // 4)) * 4 * P
                    nc.scalar.activation(dst[:, at:at + 4 * P].rearrange("p (j n) -> p j n", j=4),
                                         tps[g % 2][:], ACT.Copy).then_inc(act_done, 1)

            @block.vector
            def _(dve):
                s = Steps(dve, dve_done)
                dve.wait_ge(loaded, 16 * n_loads)
                if l2:
                    s.then(nc.vector.tensor_tensor(kn[:], cond[:, 0, :], cond[:, 0, :], ALU.mult))
                    nc.vector.reduce_sum(n1[:, 0:1], kn[:], AX.X).then_inc(roots, 1)
                    dve.wait_ge(roots, 2)
                    s.then(nc.vector.tensor_scalar(n1[:, 0:1], n2[:, 0:1], 1e-12, None, ALU.max))
                    s.then(nc.vector.reciprocal(n2[:, 0:1], n1[:, 0:1]))
                    s.then(nc.vector.tensor_tensor(qk[:, 0, :], qk[:, 0, :], qk[:, 1, :], ALU.mult))
                    s.then(nc.vector.tensor_scalar(qk[:, 0, :], qk[:, 0, :], scale, None, ALU.mult))
                    s.then(nc.vector.tensor_scalar(kn[:], cond[:, 0, :], n2[:, 0:1], None, ALU.mult))
                    s.then(nc.vector.tensor_tensor(kn[:], kn[:], qk[:, 0, :], ALU.mult))
                else:
                    s.then(nc.vector.tensor_scalar(kn[:], cond[:, 0, :], scale, None, ALU.mult))
                knb = bc(kn[:, None, :], [P, KD * HEADS, DH])
                s.then(nc.vector.tensor_tensor(prod[:].rearrange("p c (h d) -> p (c h) d", d=DH),
                                               wq[:].rearrange("p c (h d) -> p (c h) d", d=DH),
                                               knb, ALU.mult))
                s.then(nc.vector.reduce_sum(U[:], prod[:].rearrange("p c (h d) -> p (c h) d", d=DH), AX.X))
                dve.wait_ge(pool_done, 1)
                dve.sem_inc(pool_done, 1)
                dve.wait_ge(mm, 1)
                if l2:
                    dve.wait_ge(squares, 4)
                    nc.vector.reduce_sum(n1[:], sq[:], AX.X).then_inc(roots, 1)
                    dve.wait_ge(roots, 4)
                    s.then(nc.vector.tensor_scalar(n1[:], n2[:], 1e-12, None, ALU.max))
                    s.then(nc.vector.reciprocal(n2[:], n1[:]))
                for i in range(4):
                    if l2:
                        s.did(nc.vector.tensor_tensor(kf[:, 4 * i:4 * i + 4, :], kvps[i][:, :, 0:DH],
                                                      bc(n2[:, 4 * i:4 * i + 4, None], [P, 4, DH]), ALU.mult))
                    else:
                        s.did(nc.vector.tensor_scalar(kf[:, 4 * i:4 * i + 4, :], kvps[i][:, :, 0:DH],
                                                      scale, None, ALU.mult))
                    s.did(nc.vector.tensor_copy(V[:, i // 2, 4 * (i % 2):4 * (i % 2) + 4, 0:DH],
                                                kvps[i][:, :, DH:2 * DH]))
                s.settle()
                if l2:
                    s.then(nc.vector.tensor_tensor(kf[:], kf[:], bc(qk[:, 0:1, :], [P, NB, DH]), ALU.mult))
                s.did(nc.vector.tensor_copy(sA[:, :, 0:DH], kf[:]))
                s.did(nc.vector.tensor_copy(sA[:, :, DH:2 * DH], kf[:]))
                for i in range(4):
                    v = V[:, i // 2, 4 * (i % 2):4 * (i % 2) + 4, :]
                    s.did(nc.vector.tensor_tensor(v[:, :, DH:2 * DH], kvps[i][:, :, DH:2 * DH],
                                                  v[:, :, 0:DH].bitcast(F32), ALU.subtract))
                s.settle()
                nc.vector.tensor_tensor(sB[:, :, 0:DH], kf[:], sA[:, :, 0:DH].bitcast(F32),
                                        ALU.subtract).then_inc(pool_done, 1)
                dve.wait_ge(mm, 2)
                nc.vector.tensor_copy(SN[:], snps[:])
                dve.wait_ge(act_done, 2 * NB // 4)
                for b in range(B):
                    row = mrow[DH:DH + 1, b, ::-1] if table else mrow[DH:DH + 1, b, :]
                    nc.vector.tensor_scalar(kB[DH:DH + 1, b, :], row, 1.0, -FAR, ALU.subtract, ALU.mult)


def heads_loop(k, name, xT, wq_dram, wo_dram, acc, ident, bias_dram, table, norm_q,
               kA, kB, V, SN, cond, nb):
    nc = k.nc
    s8 = lambda n: k.sem(f"{name}_{n}")
    RQ = 4
    DUOS, UNITS = TB * B, TB * B * HG
    pairs = {i: (i + 2) // 2 for i in range(TB)}
    first = []
    for d in range(DUOS):
        first.append(first[-1] + pairs[(d - 1) // B] if d else 0)
    BANKS = first[-1] + pairs[TB - 1]

    group_end, wq_loaded, wo_loaded = s8("group_end"), s8("wq_loaded"), s8("wo_loaded")
    bias_loaded = [s8(f"bias_loaded{i}") for i in range(2)]
    diag_done, q_done, q_sq, q_norm, q_hi, q_lo = (s8(n) for n in
                                                  ("diag", "q", "q_sq", "q_norm", "q_hi", "q_lo"))
    qt_done, a_taken0, a_taken1, b_done = s8("qt"), s8("a0"), s8("a1"), s8("b")
    s_done, ttr_done, exp_done, sn_done = s8("s"), s8("ttr"), s8("exp"), s8("sn")
    t_done, hi_done, lo_done, pv_done = s8("t"), s8("hi"), s8("lo"), s8("pv")
    dn_done, pn_done, pnv_done, o_taken, tb_done = s8("dn"), s8("pn"), s8("pnv"), s8("o"), s8("tb")
    z_steps, zt_done, zt_taken, proj_done, proj_added, dve_small, ready, small_ones, dve_mark, pool_mark = (
        s8(n) for n in ("z", "zt", "ztt", "proj", "added", "small", "ready", "acc_zero",
                        "dve_mark", "pool_mark"))
    a_taken = [a_taken0, a_taken1]

    with ExitStack() as ctx:
        wq = k.sb(name + "_wqg", [P, KD, HG * DH], ctx=ctx)
        wo = k.sb(name + "_wog", [P, D], ctx=ctx)
        qs = [k.sb(f"{name}_qs{i}", [P, 4, HG, 2 * DH], F32R, ctx=ctx) for i in range(2)]
        A = [k.sb(f"{name}_A{i}", [P, TOK], F32R, ctx=ctx) for i in range(HG)]
        Bq = [k.sb(f"{name}_B{i}", [P, TOK], F32R, ctx=ctx) for i in range(HG)]
        bt = [k.sb(f"{name}_bt{i}", [P, HG, S], ctx=ctx) for i in range(1 if table else 2)]
        pr = [k.sb(f"{name}_p{i}", [P, HG, S], ctx=ctx) for i in range(2)]
        ph = [k.sb(f"{name}_ph{i}", [P, 2, HG * P], F32R, ctx=ctx) for i in range(2)]
        pl = [k.sb(f"{name}_pl{i}", [P, 2, HG * P], F32R, ctx=ctx) for i in range(2)]
        sng = k.sb(name + "_sng", [P, NT, HG], ctx=ctx)
        NM = k.sb(name + "_NM", [P, UNITS], ctx=ctx)
        RS = k.sb(name + "_RS", [P, UNITS], ctx=ctx)
        DN = k.sb(name + "_DN", [P, UNITS], ctx=ctx)
        PN = k.sb(name + "_PN", [P, UNITS], ctx=ctx)
        TT = k.sb(name + "_TT", [P, UNITS], ctx=ctx)
        RI = k.sb(name + "_RI", [P, UNITS], ctx=ctx)
        pnv = [k.sb(f"{name}_pnv{i}", [P, B * HG, DH], ctx=ctx) for i in range(2)]
        os_ = k.sb(name + "_os", [P, B * HG * P], ctx=ctx)
        u1 = k.sb(name + "_u1", [P, B * HG, DH], ctx=ctx)
        u2 = k.sb(name + "_u2", [P, B * HG, DH], ctx=ctx)
        Z = k.sb(name + "_Z", [P, B * HG, DH], ctx=ctx)
        ZT = k.sb(name + "_ZT", [P, B, P], ctx=ctx)
        if norm_q:
            qf = k.sb(name + "_qf", [P, RQ, 4 * HG * DH], ctx=ctx)
            ssq = k.sb(name + "_ssq", [P, NT, HG], ctx=ctx)
            rq = k.sb(name + "_rq", [P, NT, HG], ctx=ctx)
        Sps = [k.ps(f"{name}_S{i}", [P, 2, CH], ctx) for i in range(2)]
        Tps = [k.ps(f"{name}_T{i}", [P, 2, HG * P], ctx) for i in range(2)]
        Ops = k.ps(name + "_O", [P, B, HG * P], ctx)
        Mps = k.ps(name + "_M", [P, CH], ctx)
        qb = [Sps[r // 2][:, r % 2, :] for r in range(RQ)]

        def widths(i):
            W = (i + 1) * P
            return W, (1 if W <= CH else 2), max(2 * P, W) if W <= CH else W // 2

        def score_cols(i, j):
            W, chunks, n = widths(i)
            lo = S - max(W, 2 * P) if table else 0
            return slice(lo + j * n, lo + (j + 1) * n)

        def chunked(ap, i):
            W, chunks, n = widths(i)
            return ap.rearrange("p (j n) -> p j n", j=chunks)

        def begin(eng, g):
            eng.wait_ge(group_end, 4 * g + 4)

        with nc.Block() as block:
            @block.sync
            def _(sp):
                with sp.Fori(0, NG) as g:
                    begin(sp, g)
                    sp.dma_start(wq[:], wq_dram[:, :, bass.ts(g, HG * DH)]).then_inc(wq_loaded, 16)
                    if table:
                        sp.dma_start(bt[0][:], bias_dram[g]).then_inc(bias_loaded[0], 16)
                    sp.dma_start(wo[:], wo_dram[:, g, :]).then_inc(wo_loaded, 16)
                    if not table:
                        for i in range(TB):
                            if i >= 2:
                                sp.wait_ge(ttr_done, UNITS * g + B * HG * (i - 1))
                            W = (i + 1) * P
                            sp.dma_start(bt[i % 2][:, :, 0:W],
                                         bias_dram[bass.ts(g, HG), i * P:(i + 1) * P, 0:W]
                                         .rearrange("h p s -> p h s")).then_inc(bias_loaded[i % 2], 16)

            @block.gpsimd
            def _(pool):
                for h in range(HG):
                    nc.gpsimd.memset(Bq[h][DH:P, :].bitcast(F32), 0.0).then_inc(ready, 1)
                pool.wait_ge(ready, 2)
                for h in range(HG):
                    nc.gpsimd.memset(Bq[h][DH:DH + 1, :].bitcast(F32), 1.0).then_inc(ready, 1)
                pool.wait_ge(ready, 4)
                far = pool.to_reg(FAR)
                with pool.Fori(0, NG) as g:
                    begin(pool, g)

                    def hide_later_keys(i):
                        wait_apart(pool, bias_loaded[i % 2], 16 * (TB // 2) * g + 16 * (i // 2 + 1),
                                   pool_mark)
                        d = bt[i % 2][:, :, i * P:(i + 1) * P]
                        nc.gpsimd.affine_select(out=d, in_=d, compare_op=ALU.is_ge, fill=far, base=0,
                                                pattern=[[0, HG], [-1, P]],
                                                channel_multiplier=1).then_inc(diag_done, 1)

                    if not table:
                        hide_later_keys(0)
                        hide_later_keys(1)
                    for r in range(RQ):
                        for h in range(HG):
                            wait_apart(pool, a_taken[h], RQ * g + (r + 1), pool_mark)
                            nc.gpsimd.tensor_copy(Bq[h][0:DH, r * CH:(r + 1) * CH],
                                                  A[h][0:DH, r * CH:(r + 1) * CH].bitcast(F32)).then_inc(b_done, 1)
                    for i in range(TB):
                        if i + 2 < TB and not table:
                            hide_later_keys(i + 2)
                        pool.wait_ge(pn_done, TB * g + (i + 1))
                        if i >= 2:
                            pool.wait_ge(z_steps, 3 * TB * g + 3 * (i - 1))
                        nc.gpsimd.tensor_tensor(pnv[i % 2][:], bc(cond[:, 1:2, :], [P, B * HG, DH]),
                                                bc(PN[:, 4 * i:4 * i + 4, None], [P, B * HG, DH]),
                                                ALU.mult).then_inc(pnv_done, 1)
                    pool.wait_ge(pnv_done, TB * g + TB)
                    pool.sem_inc(group_end, 1)

            @block.tensor
            def _(pe):
                pe.sem_inc(group_end, 4)

                def scores(g, d):
                    i, b = d // B, d % B
                    W, chunks, n = widths(i)
                    t = b * TB + i
                    for h in range(HG):
                        u = HG * d + h
                        if u >= 2:
                            pe.wait_ge(ttr_done, UNITS * g + (u - 1))
                        for j in range(chunks):
                            cols = score_cols(i, j)
                            out = Sps[u % 2][:, j, 0:n]
                            nc.tensor.matmul(out, A[h][:, t * P:(t + 1) * P], kA[:, b, cols],
                                             start=True, stop=False)
                            last = nc.tensor.matmul(out, Bq[h][:, t * P:(t + 1) * P], kB[:, b, cols],
                                                    start=False, stop=True)
                        last.then_inc(s_done, 1)

                def turn(g, d, n):
                    i = d // B
                    at = first[d] + n
                    if n == 0:
                        pe.wait_ge(exp_done, UNITS * g + HG * (d + 1))
                    if at >= 2:
                        pe.wait_ge(lo_done, BANKS * g + (at - 1))
                    for jj in range(2):
                        j = 2 * n + jj
                        if j > i:
                            break
                        for h in range(HG):
                            last = nc.tensor.transpose(Tps[at % 2][:, jj, h * P:(h + 1) * P],
                                                       pr[d % 2][:, h, j * P:(j + 1) * P], ident[:])
                    last.then_inc(t_done, 1)

                def values(g, d, n):
                    i, b = d // B, d % B
                    at = first[d] + n
                    if n == 0 and b == 0 and i >= 1:
                        pe.wait_ge(o_taken, TB * g + i)
                    pe.wait_ge(lo_done, BANKS * g + (at + 1))
                    for jj in range(2):
                        j = 2 * n + jj
                        if j > i:
                            break
                        vj = V[:, b, (TB - 1 - i + j) if table else j, :]
                        nc.tensor.matmul(Ops[:, b, :], vj, ph[at % 2][:, jj, :], start=(j == 0), stop=False)
                        last = nc.tensor.matmul(Ops[:, b, :], vj, pl[at % 2][:, jj, :], start=False,
                                                stop=(j == i))
                    last.then_inc(pv_done, 1)

                def tail_turn(g, i):
                    pe.wait_ge(o_taken, TB * g + (i + 1))
                    if i >= 1:
                        pe.wait_ge(proj_added, TB * g + i)
                    for q in range(B * HG):
                        last = nc.tensor.transpose(Mps[:, q * P:(q + 1) * P], os_[:, q * P:(q + 1) * P],
                                                   ident[:])
                    last.then_inc(tb_done, 1)

                def tail_back(g, i):
                    pe.wait_ge(z_steps, 3 * TB * g + 3 * (i + 1))
                    for b in range(B):
                        last = nc.tensor.transpose(Mps[:, b * P:(b + 1) * P],
                                                   Z[:, HG * b:HG * b + HG, :].rearrange("p h d -> p (h d)"),
                                                   ident[:])
                    last.then_inc(zt_done, 1)

                def tail_project(g, i):
                    pe.wait_ge(wo_loaded, 16 * g + 16)
                    pe.wait_ge(zt_taken, TB * g + (i + 1))
                    for b in range(B):
                        last = nc.tensor.matmul(Mps[:, b * D:(b + 1) * D], ZT[:, b, :], wo[:],
                                                start=True, stop=True)
                    last.then_inc(proj_done, 1)

                with pe.Fori(0, NG) as g:
                    begin(pe, g)
                    pe.wait_ge(wq_loaded, 16 * g + 16)
                    for r in range(RQ):
                        for t in range(4):
                            tt = 4 * r + t
                            for c in range(KD):
                                last = nc.tensor.matmul(qb[r][:, t * P:(t + 1) * P],
                                                        xT[:, c, tt * P:(tt + 1) * P], wq[:, c, :],
                                                        start=(c == 0), stop=(c == KD - 1))
                        last.then_inc(q_done, 1)
                    for r in range(RQ):
                        pe.wait_ge(q_lo, RQ * g + (r + 1))
                        for h in range(HG):
                            if r >= 1:
                                pe.wait_ge(a_taken[h], RQ * g + r)
                            for t in range(4):
                                last = nc.tensor.transpose(
                                    Tps[h][:].rearrange("p a b -> p (a b)")[:, t * P:(t + 1) * P],
                                    qs[r % 2][:, t, h, :].bitcast(F32), ident[:])
                            last.then_inc(qt_done, 1)
                    pe.wait_ge(ready, 4)
                    pe.wait_ge(a_taken[0], RQ * g + RQ)
                    pe.wait_ge(a_taken[1], RQ * g + RQ)
                    pe.wait_ge(b_done, HG * RQ * g + HG * RQ)
                    scores(g, 0)
                    for d in range(DUOS):
                        i, b = d // B, d % B
                        if d + 1 < DUOS:
                            scores(g, d + 1)
                        if b == 0 and i >= 1:
                            tail_turn(g, i - 1)
                        if b == 1 and i >= 1:
                            tail_project(g, i - 1)
                        turn(g, d, 0)
                        for n in range(pairs[i]):
                            if n + 1 < pairs[i]:
                                turn(g, d, n + 1)
                            values(g, d, n)
                            if n == 0 and b == 0 and i >= 1:
                                tail_back(g, i - 1)
                    tail_turn(g, TB - 1)
                    tail_back(g, TB - 1)
                    tail_project(g, TB - 1)
                    pe.wait_ge(proj_done, TB * g + TB)
                    pe.sem_inc(group_end, 1)

            @block.scalar
            def _(act):
                def exponentials(g, u):
                    act.wait_ge(ttr_done, UNITS * g + (u + 1))
                    d, h = u // HG, u % HG
                    W = (d // B + 1) * P
                    p = pr[d % 2][:, h, 0:W]
                    nc.scalar.activation(p, p, ACT.Exp, bias=NM[:, u:u + 1], scale=-1.0,
                                         accum_out=RS[:, u:u + 1]).then_inc(exp_done, 1)

                def high_part(g, d, n):
                    at = first[d] + n
                    js = min(2, d // B + 1 - 2 * n)
                    if at >= 2:
                        act.wait_ge(pv_done, BANKS * g + (at - 1))
                    act.wait_ge(t_done, BANKS * g + (at + 1))
                    nc.scalar.activation(ph[at % 2][:, 0:js, :], Tps[at % 2][:, 0:js, :],
                                         ACT.Copy).then_inc(hi_done, 1)

                def null_exponential(g, i):
                    act.wait_ge(dn_done, TB * g + (i + 1))
                    nc.scalar.activation(PN[:, 4 * i:4 * i + 4], DN[:, 4 * i:4 * i + 4],
                                         ACT.Exp).then_inc(pn_done, 1)

                def take_outputs(g, i):
                    if i >= 1:
                        act.wait_ge(tb_done, TB * g + i)
                    act.wait_ge(pv_done, BANKS * g + first[B * i + 1] + pairs[i])
                    nc.scalar.activation(os_[:], Ops[:].rearrange("p a b -> p (a b)"),
                                         ACT.Copy).then_inc(o_taken, 1)

                def take_back(g, i):
                    act.wait_ge(zt_done, TB * g + (i + 1))
                    nc.scalar.activation(ZT[:], Mps[:, 0:B * P].rearrange("p (b n) -> p b n", b=B),
                                         ACT.Copy).then_inc(zt_taken, 1)

                with act.Fori(0, NG) as g:
                    begin(act, g)
                    if norm_q:
                        for r in range(RQ):
                            act.wait_ge(q_done, RQ * g + (r + 1))
                            nc.scalar.activation(qf[:, r, :], qb[r], ACT.Square).then_inc(q_sq, 1)
                        act.wait_ge(q_norm, 2 * g + 1)
                        nc.scalar.activation(rq[:], ssq[:], ACT.Sqrt).then_inc(q_norm, 1)
                    for r in range(RQ):
                        if r >= 2:
                            act.wait_ge(qt_done, HG * RQ * g + HG * (r - 1))
                        if norm_q:
                            act.wait_ge(q_sq, 2 * RQ * g + RQ + (r + 1))
                            src = qf[:, r, :]
                        else:
                            act.wait_ge(q_done, RQ * g + (r + 1))
                            src = qb[r]
                        nc.scalar.activation(qs[r % 2][:, :, :, 0:DH],
                                             src.rearrange("p (t h d) -> p t h d", t=4, h=HG),
                                             ACT.Copy).then_inc(q_hi, 1)
                        if r >= 1:
                            act.wait_ge(qt_done, HG * RQ * g + (HG * (r - 1) + 1))
                            nc.scalar.activation(A[0][:, (r - 1) * CH:r * CH],
                                                 Tps[0][:].rearrange("p a b -> p (a b)"),
                                                 ACT.Copy).then_inc(a_taken[0], 1)
                    act.wait_ge(qt_done, HG * RQ * g + (HG * (RQ - 1) + 1))
                    nc.scalar.activation(A[0][:, (RQ - 1) * CH:RQ * CH],
                                         Tps[0][:].rearrange("p a b -> p (a b)"),
                                         ACT.Copy).then_inc(a_taken[0], 1)
                    exponentials(g, 0)
                    exponentials(g, 1)
                    for d in range(DUOS):
                        i, b = d // B, d % B
                        if b == 1:
                            null_exponential(g, i)
                        if b == 0 and i >= 1:
                            take_outputs(g, i - 1)
                        for n in range(pairs[i]):
                            high_part(g, d, n)
                            if n < 2 and d + 1 < DUOS:
                                exponentials(g, HG * (d + 1) + n)
                        if pairs[i] < 2 and d + 1 < DUOS:
                            exponentials(g, HG * (d + 1) + 1)
                        if b == 0 and i >= 1:
                            take_back(g, i - 1)
                    take_outputs(g, TB - 1)
                    take_back(g, TB - 1)
                    act.wait_ge(zt_taken, TB * g + TB)
                    act.sem_inc(group_end, 1)

            @block.vector
            def _(dve):
                def add_bias_and_max(g, u):
                    d, h = u // HG, u % HG
                    i, b = d // B, d % B
                    t = b * TB + i
                    W, chunks, n = widths(i)
                    if d >= 2 and h == 0:
                        dve.wait_ge(t_done, BANKS * g + first[d - 1])
                    if h == 0 and b == 0:
                        if not table:
                            dve.wait_ge(diag_done, TB * g + (i + 1))
                        elif i == 0:
                            dve.wait_ge(bias_loaded[0], 16 * g + 16)
                    wait_apart(dve, s_done, UNITS * g + (u + 1), dve_mark)
                    off = P if (table and i == 0) else 0
                    nn = min(n, W)
                    nc.vector.tensor_tensor_reduce(
                        out=chunked(pr[d % 2][:, h, 0:W], i), in0=Sps[u % 2][:, 0:chunks, off:off + nn],
                        in1=chunked(bt[0 if table else i % 2][:, h, 0:W], i), scale=-1.0,
                        scalar=sng[:, t, h:h + 1], op0=ALU.add, op1=ALU.min,
                        accum_out=NM[:, u:u + 1]).then_inc(ttr_done, 1)

                def low_part(g, d, n):
                    at = first[d] + n
                    js = min(2, d // B + 1 - 2 * n)
                    dve.wait_ge(hi_done, BANKS * g + (at + 1))
                    nc.vector.tensor_tensor(pl[at % 2][:, 0:js, :], Tps[at % 2][:, 0:js, :],
                                            ph[at % 2][:, 0:js, :].bitcast(F32),
                                            ALU.subtract).then_inc(lo_done, 1)

                def null_difference(g, i):
                    dve.wait_ge(ttr_done, UNITS * g + 4 * (i + 1))
                    nc.vector.tensor_tensor(
                        DN[:, 4 * i:4 * i + 4].rearrange("p (b h) -> p b h", b=B),
                        NM[:, 4 * i:4 * i + 4].rearrange("p (b h) -> p b h", b=B),
                        sng[:].rearrange("p (b t) h -> p b t h", b=B)[:, :, i, :],
                        ALU.subtract).then_inc(dn_done, 1)

                def outputs(g, i):
                    c = slice(4 * i, 4 * i + 4)
                    dve.wait_ge(exp_done, UNITS * g + 4 * (i + 1))
                    dve.wait_ge(pn_done, TB * g + (i + 1))
                    nc.vector.tensor_tensor(TT[:, c], RS[:, c], PN[:, c], ALU.add).then_inc(dve_small, 1)
                    dve.wait_ge(dve_small, 2 * TB * g + (2 * i + 1))
                    nc.vector.reciprocal(RI[:, c], TT[:, c]).then_inc(dve_small, 1)
                    halves = Mps[:].rearrange("p (q e) -> p q e", e=2 * DH)
                    dve.wait_ge(pnv_done, TB * g + (i + 1))
                    dve.wait_ge(tb_done, TB * g + (i + 1))
                    nc.vector.tensor_tensor(u1[:], halves[:, :, DH:2 * DH], pnv[i % 2][:],
                                            ALU.add).then_inc(z_steps, 1)
                    dve.wait_ge(z_steps, 3 * TB * g + (3 * i + 1))
                    nc.vector.tensor_tensor(u2[:], halves[:, :, 0:DH], u1[:], ALU.add).then_inc(z_steps, 1)
                    dve.wait_ge(dve_small, 2 * TB * g + (2 * i + 2))
                    dve.wait_ge(z_steps, 3 * TB * g + (3 * i + 2))
                    if i >= 1:
                        dve.wait_ge(zt_done, TB * g + i)
                    nc.vector.tensor_tensor(Z[:], u2[:], bc(RI[:, c, None], [P, B * HG, DH]),
                                            ALU.mult).then_inc(z_steps, 1)

                def accumulate(g, i):
                    dve.wait_ge(proj_done, TB * g + (i + 1))
                    rows = acc[:].rearrange("p (b t) d -> p b t d", b=B)[:, :, i, :]
                    nc.vector.tensor_tensor(rows, Mps[:].rearrange("p (b d) -> p b d", b=B), rows,
                                            ALU.add).then_inc(proj_added, 1)

                nc.vector.memset(acc[:], 0.0).then_inc(small_ones, 1)
                dve.wait_ge(small_ones, 1)
                with dve.Fori(0, NG) as g:
                    begin(dve, g)
                    heads = bass.ts(g, HG)
                    if norm_q:
                        for r in range(RQ):
                            dve.wait_ge(q_sq, 2 * RQ * g + (r + 1))
                            nc.vector.reduce_sum(
                                ssq[:, 4 * r:4 * r + 4, :].rearrange("p t h -> p (t h)"),
                                qf[:, r, :].rearrange("p (n d) -> p n d", d=DH), AX.X).then_inc(sn_done, 1)
                        dve.wait_ge(sn_done, (RQ + 6) * g + RQ)
                        dve.sem_inc(q_norm, 1)
                        dve.wait_ge(q_norm, 2 * g + 2)
                        nc.vector.tensor_scalar(ssq[:], rq[:], 1e-12, None, ALU.max).then_inc(sn_done, 1)
                        dve.wait_ge(sn_done, (RQ + 6) * g + (RQ + 1))
                        nc.vector.reciprocal(rq[:], ssq[:]).then_inc(sn_done, 1)
                        dve.wait_ge(sn_done, (RQ + 6) * g + (RQ + 2))
                        nc.vector.tensor_tensor(sng[:], SN[:, :, heads], rq[:], ALU.mult).then_inc(sn_done, 1)
                        dve.wait_ge(sn_done, (RQ + 6) * g + (RQ + 3))
                        base, n_sn = RQ + 3, RQ + 6
                        src = sng[:]
                    else:
                        base, n_sn = 0, 3
                        src = SN[:, :, heads]
                    nc.vector.tensor_copy(DN[:, 0:HG], nb[:, heads]).then_inc(sn_done, 1)
                    dve.wait_ge(sn_done, n_sn * g + (base + 1))
                    nc.vector.tensor_tensor(sng[:], src, bc(DN[:, None, 0:HG], [P, NT, HG]),
                                            ALU.add).then_inc(sn_done, 1)
                    dve.wait_ge(sn_done, n_sn * g + (base + 2))
                    nc.vector.tensor_scalar(sng[:], sng[:], -1.0, None, ALU.mult).then_inc(sn_done, 1)
                    if norm_q:
                        for r in range(RQ):
                            nc.vector.tensor_tensor(
                                qf[:, r, :].rearrange("p (t h d) -> p t h d", t=4, h=HG),
                                qb[r].rearrange("p (t h d) -> p t h d", t=4, h=HG),
                                bc(rq[:, 4 * r:4 * r + 4, :, None], [P, 4, HG, DH]),
                                ALU.mult).then_inc(q_sq, 1)
                        dve.wait_ge(q_sq, 2 * RQ * g + 2 * RQ)
                    for r in range(RQ):
                        dve.wait_ge(q_hi, RQ * g + (r + 1))
                        src = qf[:, r, :] if norm_q else qb[r]
                        nc.vector.tensor_tensor(qs[r % 2][:, :, :, DH:2 * DH],
                                                src.rearrange("p (t h d) -> p t h d", t=4, h=HG),
                                                qs[r % 2][:, :, :, 0:DH].bitcast(F32),
                                                ALU.subtract).then_inc(q_lo, 1)
                        if r >= 1:
                            dve.wait_ge(qt_done, HG * RQ * g + HG * r)
                            nc.vector.tensor_copy(A[1][:, (r - 1) * CH:r * CH],
                                                  Tps[1][:].rearrange("p a b -> p (a b)")).then_inc(a_taken[1], 1)
                    dve.wait_ge(qt_done, HG * RQ * g + HG * RQ)
                    nc.vector.tensor_copy(A[1][:, (RQ - 1) * CH:RQ * CH],
                                          Tps[1][:].rearrange("p a b -> p (a b)")).then_inc(a_taken[1], 1)
                    dve.wait_ge(sn_done, n_sn * g + n_sn)
                    add_bias_and_max(g, 0)
                    add_bias_and_max(g, 1)
                    for d in range(DUOS):
                        i, b = d // B, d % B
                        if d + 1 < DUOS:
                            add_bias_and_max(g, HG * (d + 1))
                        if b == 0 and i >= 1:
                            outputs(g, i - 1)
                        for n in range(pairs[i]):
                            low_part(g, d, n)
                            if n == 0 and d + 1 < DUOS:
                                add_bias_and_max(g, HG * (d + 1) + 1)
                        if b == 0:
                            null_difference(g, i)
                        if b == 1 and i >= 1:
                            accumulate(g, i - 1)
                    outputs(g, TB - 1)
                    accumulate(g, TB - 1)
                    dve.wait_ge(proj_added, TB * g + TB)
                    dve.sem_inc(group_end, 1)


def load_constants(k, ident, X, x_dram, upper):
    nc = k.nc
    made, loaded = k.sem("const_made"), k.sem("const_loaded")
    with nc.Block() as block:
        @block.sync
        def _(sp):
            sp.dma_start(X[:], x_dram.rearrange("b (i p) d -> p (b i) d", p=P)).then_inc(loaded, 16)
            sp.wait_ge(loaded, 16)

        @block.gpsimd
        def _(pool):
            nc.gpsimd.memset(ident[:], 0.0).then_inc(made, 1)
            nc.gpsimd.memset(upper[:], 1.0).then_inc(made, 1)
            pool.wait_ge(made, 2)
            nc.gpsimd.affine_select(out=ident[:], in_=ident[:], compare_op=ALU.not_equal, fill=1.0,
                                    base=0, pattern=[[-1, P]], channel_multiplier=1)
            nc.gpsimd.affine_select(out=upper[:], in_=upper[:], compare_op=ALU.is_ge, fill=0.0,
                                    base=0, pattern=[[1, P]], channel_multiplier=-1)


def load_vector(k, name, ctx, dram, block_sems):
    t = k.sb(name, [P, dram.shape[0]], ctx=ctx)
    return t


def load_broadcast(k, name, pairs):
    nc = k.nc
    loaded = k.sem(name + "_loaded")
    with nc.Block() as block:
        @block.sync
        def _(sp):
            for tile, dram in pairs:
                sp.dma_start(tile[:], dram.partition_broadcast(P)).then_inc(loaded, 16)
            sp.wait_ge(loaded, 16 * len(pairs))


def fill(k, name, tile, value):
    nc = k.nc
    with nc.Block() as block:
        @block.gpsimd
        def _(pool):
            nc.gpsimd.memset(tile, value)


def store_rows(k, name, src, out_dram):
    nc = k.nc
    stored = k.sem(name)
    with nc.Block() as block:
        @block.sync
        def _(sp):
            sp.dma_start(out_dram.rearrange("b (i p) d -> p (b i) d", p=P), src[:]).then_inc(stored, 16)
            sp.wait_ge(stored, 16)


def layer0(k, a, X, Y, XT, ident):
    with ExitStack() as ctx:
        shares = k.sb("l0_shares", [P, NT, 10], ctx=ctx)
        fill(k, "l0_ones", shares[:, :, 8:10], 1.0)
        to_feature_major(k, "l0_t", X, XT, ident)
        route(k, "l0_r", XT, a["l0_router"], 8, 2, shares, extra=(a["condT"], a["l0_router_cond"]),
              scale=0.5, soft="all")
        gated_experts(k, "l0_e", XT, a["l0_experts"], 10, P, Y, shares, "leaky")
    with ExitStack() as ctx:
        picked = k.sb("l0_picked", [P, NT, 8], ctx=ctx)
        Z = k.sb("l0_z", [P, NT, D], ctx=ctx)
        gamma, beta = k.sb("l0_gamma", [P, D], ctx=ctx), k.sb("l0_beta", [P, D], ctx=ctx)
        load_broadcast(k, "l0_v", [(gamma, a["l0_ln_gamma"]), (beta, a["l0_ln_beta"])])
        to_feature_major(k, "l0_t2", Y, XT, ident)
        route(k, "l0_r2", XT, a["l0_ffn_router"], 4, 1, picked)
        with ExitStack() as inner:
            picked_ffn(k, "l0_f", Y, picked, a["l0_w1"], a["l0_b1"], a["l0_wo"], a["l0_bo"], Z, ident, 4)
        normalise(k, "l0_ln", Z, X, gamma, 1e-12, beta=beta, add_to=X)


def window_views(table_dram):
    return bass.AP(tensor=table_dram.tensor, offset=0,
                   ap=[[HG * TABLE, NG], [1, P], [TABLE, HG], [1, S]])


def layer1_attention(k, a, X, Y, XT, ident, table_dram):
    position_table(k, a, table_dram, ident)
    with ExitStack() as ctx:
        g_in = k.sb("l1_gin", [P, D], ctx=ctx)
        load_broadcast(k, "l1_v", [(g_in, a["l1_g_norm"])])
        normalise(k, "l1_n", X, Y, g_in, 1e-5)
        to_feature_major(k, "l1_t", Y, XT, ident)
    attention(k, "l1_a", XT, (a["l1_wq"], a["l1_wkv"], a["l1_wout"], a["l1_null_attn_bias"]), a["cond"],
              a["mask1"], Y, ident, window_views(table_dram), table=True, l2=(a["l1_q_scale"], a["l1_k_scale"]))
    with ExitStack() as ctx:
        g_out = k.sb("l1_gout", [P, D], ctx=ctx)
        load_broadcast(k, "l1_v2", [(g_out, a["l1_g_out"])])
        normalise(k, "l1_no", Y, Y, g_out, 1e-5)


def biased_attention(k, a, layer, X, Y, XT, ident):
    n = f"l{layer}"
    with ExitStack() as ctx:
        g_in = k.sb(n + "_gin", [P, D], ctx=ctx)
        load_broadcast(k, n + "_v", [(g_in, a[n + "_g_in"])])
        normalise(k, n + "_n", X, Y, g_in, 1e-5)
        to_feature_major(k, n + "_t", Y, XT, ident)
    attention(k, n + "_a", XT, (a[n + "_wq"], a[n + "_wkv"], a[n + "_wout"], a[n + "_null_attn_bias"]),
              a["cond"], a["mask0"], Y, ident, a["bias"])
    with ExitStack() as ctx:
        g_out = k.sb(n + "_gout", [P, D], ctx=ctx)
        load_broadcast(k, n + "_v2", [(g_out, a[n + "_g_out"])])
        normalise(k, n + "_no", Y, Y, g_out, 1e-5)


def layer1_ffn(k, a, X, Y, XT, ident):
    with ExitStack() as ctx:
        picked = k.sb("l1_picked", [P, NT, 8], ctx=ctx)
        to_feature_major(k, "l1_t2", Y, XT, ident)
        route(k, "l1_r", XT, a["l1_router"], 8, 1, picked, bias=a["l1_router_b"])
        lora_ffn(k, "l1_f", XT, picked, (a["l1_wi"], a["l1_wi_b"], a["l1_wo"], a["l1_wo_b"],
                                         a["l1_lora_a"], a["l1_lora_b"]), X, ident)


def layer2_ffn(k, a, X, Y, XT, ident):
    with ExitStack() as ctx:
        scale = k.sb("l2_scale", [P, 1], ctx=ctx)
        round_to_e4m3(k, "l2_q", Y, Y, a["l2_input_scale"], scale)
        to_feature_major(k, "l2_t2", Y, XT, ident)
        linear(k, "l2_f", XT, a["l2_w"], a["l2_weight_scale"], a["l2_bias"], X)


def layer3_ffn(k, a, X, Y, XT, ident, upper):
    with ExitStack() as ctx:
        shares = k.sb("l3_shares", [P, NT, 8], ctx=ctx)
        chosen = k.sb("l3_chosen", [P, NT, 8], ctx=ctx)
        rank = k.sb("l3_rank", [P, NT, 8], ctx=ctx)
        to_feature_major(k, "l3_t2", Y, XT, ident)
        route(k, "l3_r", XT, a["l3_router"], 8, 2, shares, bias=a["l3_router_b"], soft="chosen",
              ones=chosen)
        places(k, "l3_p", chosen, rank, upper)
        drop_over_capacity(k, "l3_d", shares, rank)
        gated_experts(k, "l3_e", XT, a["l3_experts"], 8, 4 * P, Y, shares, "silu")
        nc = k.nc
        with nc.Block() as block:
            @block.vector
            def _(dve):
                nc.vector.tensor_tensor(X[:], X[:], Y[:], ALU.add)


def four_layers(nc, a, out):
    with ExitStack() as ctx:
        k = Kit(nc, ctx)
        X = k.sb("X", [P, NT, D])
        Y = k.sb("Y", [P, NT, D])
        XT = k.sb("XT", [P, KD, TOK])
        ident, upper = k.sb("ident", [P, P]), k.sb("upper", [P, P])
        table_dram = nc.dram_tensor("position_table", [HEADS, TABLE], F32, kind="Internal").ap()
        load_constants(k, ident, X, a["x"], upper)
        with k.stage():
            layer0(k, a, X, Y, XT, ident)
        with k.stage():
            layer1_attention(k, a, X, Y, XT, ident, table_dram)
        with k.stage():
            layer1_ffn(k, a, X, Y, XT, ident)
        with k.stage():
            biased_attention(k, a, 2, X, Y, XT, ident)
        with k.stage():
            layer2_ffn(k, a, X, Y, XT, ident)
        with k.stage():
            biased_attention(k, a, 3, X, Y, XT, ident)
        with k.stage():
            layer3_ffn(k, a, X, Y, XT, ident, upper)
        store_rows(k, "stored", X, out)


def lay_out(inputs):
    import numpy as np

    def rows(w):
        w = np.asarray(w)
        return np.ascontiguousarray(w.reshape(w.shape[0] // 128, 128, -1).transpose(1, 0, 2))

    g = {n: np.asarray(a) for n, a in inputs.items()}

    def experts(gate, up, down):
        out = []
        for a, b, c in zip(gate, up, down):
            out.append(np.concatenate([rows(x).reshape(128, -1) for x in (a, b, c)], axis=1))
        return np.ascontiguousarray(np.stack(out))

    def halves(w):
        return [w[:, :w.shape[1] // 2], w[:, w.shape[1] // 2:]]

    a = {"x": g["x"], "cond": g["cond_64"], "condT": g["cond_64"].T, "bias": g["fside_16xSxS_0"],
         "mask1": g["mask_BxS_bf1"], "mask0": g["mask_BxS_bk0"]}
    down = g["L0_cond_sw_down"]
    a["l0_router"] = rows(g["L0_cond_wt"].T)
    a["l0_router_cond"] = g["L0_cond_wg"].T
    a["l0_experts"] = experts(list(g["L0_cond_w_gate"]) + halves(g["L0_cond_sw_gate"]),
                              list(g["L0_cond_w_up"]) + halves(g["L0_cond_sw_up"]),
                              list(g["L0_cond_w_down"]) + [down[:128], down[128:]])
    a["l0_ffn_router"] = rows(g["L0_ffn_W_router"])
    a["l0_w1"] = g["L0_ffn_W1"].reshape(4, 2, 128, 1024).transpose(2, 0, 1, 3)
    a["l0_b1"] = g["L0_ffn_b1"]
    a["l0_wo"] = rows(g["L0_ffn_Wo"])
    for n in ("bo", "ln_gamma", "ln_beta"):
        a["l0_" + n] = g["L0_ffn_" + n]
    for n in ("g_norm", "q_scale", "k_scale", "null_attn_bias", "b0", "g0", "b1", "g1", "b2", "g_out"):
        a["l1_" + n] = g["L1_cond_" + n]
    a["l1_w0"] = g["L1_cond_w0"][0]
    a["l1_w1"] = rows(g["L1_cond_w1"])
    a["l1_w2"] = rows(g["L1_cond_w2"])
    for layer, wo in ((1, "L1_cond_Wout"), (2, "L2_cond_Wo"), (3, "L3_cond_Wo")):
        a[f"l{layer}_wq"] = rows(g[f"L{layer}_cond_Wq"])
        a[f"l{layer}_wkv"] = rows(g[f"L{layer}_cond_Wkv"])
        a[f"l{layer}_wout"] = rows(g[wo])
    a["l1_router"] = rows(g["L1_ffn_gate_W"].T)
    a["l1_router_b"] = g["L1_ffn_gate_b"]
    a["l1_wi"] = rows(g["L1_ffn_wi_W"].T)
    a["l1_wi_b"] = g["L1_ffn_wi_b"].reshape(8, 128).T
    a["l1_wo"] = rows(g["L1_ffn_wo_W"].T)
    a["l1_wo_b"] = g["L1_ffn_wo_b"]
    a["l1_lora_a"] = rows(g["L1_ffn_lora_A"].reshape(32, 256).T)
    a["l1_lora_b"] = g["L1_ffn_lora_B"].transpose(0, 2, 1).reshape(32, 1024)
    for layer in (2, 3):
        for n in ("g_in", "null_attn_bias", "g_out"):
            a[f"l{layer}_{n}"] = g[f"L{layer}_cond_{n}"]
    a["l2_w"] = rows(g["L2_ffn_weight_fp8"].T)
    for n in ("bias", "input_scale", "weight_scale"):
        a["l2_" + n] = g["L2_ffn_" + n]
    a["l3_router"] = rows(g["L3_ffn_router_w"].T)
    a["l3_router_b"] = g["L3_ffn_router_b"]
    a["l3_experts"] = experts(g["L3_ffn_W"], g["L3_ffn_V"], g["L3_ffn_W_out"])
    return {n: np.ascontiguousarray(v) for n, v in a.items()}


_OUT = ((2, 1024, 256), "float32")


def kernel(**inputs):
    import numpy as _np
    import concourse.bacc as _bacc
    from concourse import mybir as _mybir
    from concourse.bass_utils import run_bass_kernel_spmd as _run

    nc = _bacc.Bacc("TRN2", target_bir_lowering=False, num_devices=1)
    laid = lay_out(inputs)
    arrays = {f"in_{n}": a for n, a in laid.items()}
    dram = {n: nc.dram_tensor(f"in_{n}", a.shape, _mybir.dt.from_np(a.dtype), kind="ExternalInput").ap()
            for n, a in laid.items()}
    out = nc.dram_tensor("out_0", _OUT[0], _mybir.dt.from_np(_np.dtype(_OUT[1])), kind="ExternalOutput").ap()
    four_layers(nc, dram, out)
    return _run(nc, [arrays], core_ids=[0]).results[0]["out_0"]
```

```python
from contextlib import ExitStack, contextmanager

import concourse.bass as bass
from concourse import mybir

P = 128
B, S, D = 2, 1024, 256
TOK = B * S
NT = TOK // P
TB = S // P
KD = D // P
DH = 64
HEADS = 16
HG = 2
NG = HEADS // HG
CH = 512
NCH = TOK // CH
TPC = CH // P

ALU = mybir.AluOpType
ACT = mybir.ActivationFunctionType
AX = mybir.AxisListType
F32 = mybir.dt.float32
F32R = mybir.dt.float32r
U32 = mybir.dt.uint32
I32 = mybir.dt.int32
U8 = mybir.dt.uint8

FAR = -1.0e30


class Kit:

    def __init__(self, nc, ctx):
        self.nc, self.ctx = nc, ctx
        self.sem_ctx, self.sems = ctx, []

    @contextmanager
    def stage(self):
        before = self.sem_ctx, self.sems
        with ExitStack() as own:
            self.sem_ctx, self.sems = own, []
            yield
            with self.nc.Block() as block:
                @block.gpsimd
                def _(pool):
                    for s in self.sems:
                        pool.sem_clear(s)
        self.sem_ctx, self.sems = before

    def sb(self, name, shape, dtype=F32, ctx=None):
        return (ctx or self.ctx).enter_context(self.nc.sbuf_tensor(name, shape, dtype))

    def ps(self, name, shape, ctx):
        return ctx.enter_context(self.nc.psum_tensor(name, shape, F32))

    def sem(self, name):
        self.sems.append(self.sem_ctx.enter_context(self.nc.semaphore(name)))
        return self.sems[-1]


class Steps:

    def __init__(self, eng, sem):
        self.eng, self.sem, self.n = eng, sem, 0

    def did(self, instruction):
        instruction.then_inc(self.sem, 1)
        self.n += 1

    def settle(self):
        self.eng.wait_ge(self.sem, self.n)

    def then(self, instruction):
        self.did(instruction)
        self.settle()


def wait_apart(eng, sem, value, mark):
    eng.wait_ge(sem, value)
    eng.sem_inc(mark, 1)


def bc(ap, shape):
    return ap.broadcast_to(shape)


def to_feature_major(k, name, src, dst, ident):
    nc = k.nc
    NT = src.shape[1]
    turned, out_a, out_v = k.sem(name + "_turned"), k.sem(name + "_outa"), k.sem(name + "_outv")
    with ExitStack() as ctx:
        banks = [k.ps(f"{name}_ps{i}", [P, KD, 2 * P], ctx) for i in range(4)]
        with nc.Block() as block:
            @block.tensor
            def _(pe):
                for g in range(NT // 2):
                    if g >= 4:
                        pe.wait_ge(out_a if g % 2 == 0 else out_v, (g - 4) // 2 + 1)
                    for c in range(KD):
                        for t in range(2):
                            last = nc.tensor.transpose(banks[g % 4][:, c, t * P:(t + 1) * P],
                                                       src[:, 2 * g + t, c * P:(c + 1) * P], ident[:])
                    last.then_inc(turned, 1)

            @block.scalar
            def _(act):
                for g in range(0, NT // 2, 2):
                    act.wait_ge(turned, g + 1)
                    nc.scalar.activation(dst[:, :, 2 * g * P:(2 * g + 2) * P], banks[g % 4][:],
                                         ACT.Copy).then_inc(out_a, 1)

            @block.vector
            def _(dve):
                for g in range(1, NT // 2, 2):
                    dve.wait_ge(turned, g + 1)
                    nc.vector.tensor_copy(dst[:, :, 2 * g * P:(2 * g + 2) * P],
                                          banks[g % 4][:]).then_inc(out_v, 1)


def normalise(k, name, src, dst, gamma, eps, beta=None, add_to=None):
    nc = k.nc
    NT = src.shape[1]
    done, sd_ready, var_ready = k.sem(name + "_dve"), k.sem(name + "_sd"), k.sem(name + "_var")
    with ExitStack() as ctx:
        st = k.sb(name + "_st", [P, NT, 6], ctx=ctx)
        mv = k.sb(name + "_mv", [P, NT, 2], ctx=ctx)
        ve = k.sb(name + "_ve", [P, NT], ctx=ctx)
        sd = k.sb(name + "_sd_t", [P, NT], ctx=ctx)
        rs = k.sb(name + "_rs", [P, NT], ctx=ctx)
        tmp = k.sb(name + "_tmp", [P, NT, D], ctx=ctx)
        with nc.Block() as block:
            @block.vector
            def _(dve):
                s = Steps(dve, done)
                for t in range(NT):
                    s.did(nc.vector.bn_stats(st[:, t, :], src[:, t, :]))
                s.settle()
                for t in range(NT):
                    s.did(nc.vector.bn_aggr(mv[:, t, :], st[:, t, :]))
                s.settle()
                nc.vector.tensor_scalar(ve[:], mv[:, :, 1], eps, None, ALU.add).then_inc(var_ready, 1)
                dve.wait_ge(sd_ready, 1)
                s.then(nc.vector.reciprocal(rs[:], sd[:]))
                for t in range(NT):
                    s.did(nc.vector.tensor_scalar(tmp[:, t, :], src[:, t, :], mv[:, t, 0:1],
                                                  rs[:, t:t + 1], ALU.subtract, ALU.mult))
                s.settle()
                g = bc(gamma[:, None, :], [P, NT, D])
                more = [(add_to, ALU.add)] if add_to is not None else []
                if beta is not None:
                    more.insert(0, (bc(beta[:, None, :], [P, NT, D]), ALU.add))
                s.then(nc.vector.tensor_tensor(tmp[:] if more else dst[:], tmp[:], g, ALU.mult))
                for n, (other, op) in enumerate(more):
                    s.then(nc.vector.tensor_tensor(dst[:] if n == len(more) - 1 else tmp[:], tmp[:],
                                                   other[:] if other is add_to else other, op))

            @block.scalar
            def _(act):
                act.wait_ge(var_ready, 1)
                nc.scalar.activation(sd[:], ve[:], ACT.Sqrt).then_inc(sd_ready, 1)


def route(k, name, xT, w_dram, E, top, shares, bias=None, extra=None, scale=1.0, soft=None,
          ones=None):
    nc = k.nc
    EP = 8
    loaded, logit, dve_done, exped, iot = (k.sem(f"{name}_{s}") for s in
                                           ("loaded", "logit", "dve", "exp", "iota"))
    with ExitStack() as ctx:
        w = k.sb(name + "_w", [P, KD, E], ctx=ctx)
        bt = k.sb(name + "_b", [P, E], ctx=ctx)
        io = k.sb(name + "_io", [P, EP], ctx=ctx)
        L = k.sb(name + "_L", [P, NT, EP], ctx=ctx)
        M8 = k.sb(name + "_M8", [P, NT, 8], ctx=ctx)
        I8 = k.sb(name + "_I8", [P, NT, 8], U32, ctx=ctx)
        If = k.sb(name + "_If", [P, NT, 2], ctx=ctx)
        Ex = k.sb(name + "_E", [P, NT, EP], ctx=ctx)
        oh = k.sb(name + "_oh", [P, NT, EP], ctx=ctx)
        r1 = k.sb(name + "_r1", [P, NT], ctx=ctx)
        r2 = k.sb(name + "_r2", [P, NT], ctx=ctx)
        if extra is not None:
            condT_dram, wg_dram = extra
            cT = k.sb(name + "_cT", [DH, B], ctx=ctx)
            wg = k.sb(name + "_wg", [DH, E], ctx=ctx)
            cb = k.sb(name + "_cb", [DH, B, P], ctx=ctx)
        ps = k.ps(name + "_ps", [P, NT, E], ctx)
        n_loads = 1 + (bias is not None) + 2 * (extra is not None)
        with nc.Block() as block:
            @block.sync
            def _(sp):
                sp.dma_start(w[:], w_dram).then_inc(loaded, 16)
                if bias is not None:
                    sp.dma_start(bt[:], bias.partition_broadcast(P)).then_inc(loaded, 16)
                if extra is not None:
                    sp.dma_start(cT[:], condT_dram, allow_slow_non_contiguous=True).then_inc(loaded, 16)
                    sp.dma_start(wg[:], wg_dram).then_inc(loaded, 16)

            @block.gpsimd
            def _(pool):
                nc.gpsimd.iota(io[:], [[1, EP]], base=0, channel_multiplier=0,
                               allow_small_or_imprecise_dtypes=True).then_inc(iot, 1)

            @block.tensor
            def _(pe):
                pe.wait_ge(loaded, 16 * n_loads)
                if extra is not None:
                    pe.wait_ge(iot, 2)
                for t in range(NT):
                    for c in range(KD):
                        last = nc.tensor.matmul(ps[:, t, :], xT[:, c, t * P:(t + 1) * P], w[:, c, :],
                                                start=(c == 0), stop=(c == KD - 1 and extra is None))
                    if extra is not None:
                        last = nc.tensor.matmul(ps[:, t, :], cb[:, t // TB, :], wg[:],
                                                start=False, stop=True)
                last.then_inc(logit, 1)

            @block.scalar
            def _(act):
                if soft:
                    act.wait_ge(exped, 1)
                    nc.scalar.activation(Ex[:], Ex[:], ACT.Exp).then_inc(exped, 1)

            @block.vector
            def _(dve):
                s = Steps(dve, dve_done)
                if extra is not None:
                    dve.wait_ge(loaded, 16 * n_loads)
                    dve.wait_ge(iot, 1)
                    nc.vector.tensor_copy(cb[:], bc(cT[:, :, None], [DH, B, P])).then_inc(iot, 1)
                if E < EP:
                    s.then(nc.vector.memset(L[:], -3.0e38))
                dve.wait_ge(logit, 1)
                if bias is not None:
                    s.then(nc.vector.tensor_tensor(L[:, :, 0:E], ps[:], bc(bt[:, None, :], [P, NT, E]),
                                                   ALU.add))
                else:
                    s.then(nc.vector.tensor_scalar(L[:, :, 0:E], ps[:], scale, None, ALU.mult))
                for t in range(NT):
                    s.did(nc.vector.max(M8[:, t, :], L[:, t, :]))
                s.settle()
                for t in range(NT):
                    s.did(nc.vector.max_index(I8[:, t, :], M8[:, t, :], L[:, t, :]))
                s.settle()
                s.then(nc.vector.tensor_copy(If[:], I8[:, :, 0:2]))
                dve.wait_ge(iot, 1)
                iob = bc(io[:, None, 0:EP], [P, NT, EP])
                pick = ones if ones is not None else (shares if not soft else oh)
                s.then(nc.vector.tensor_tensor(pick[:], iob, bc(If[:, :, 0:1], [P, NT, EP]), ALU.is_equal))
                if top == 2:
                    s.then(nc.vector.tensor_tensor(Ex[:], iob, bc(If[:, :, 1:2], [P, NT, EP]),
                                                   ALU.is_equal))
                    s.then(nc.vector.tensor_tensor(pick[:], pick[:], Ex[:], ALU.add))
                if soft:
                    nc.vector.tensor_tensor(Ex[:], L[:], bc(M8[:, :, 0:1], [P, NT, EP]),
                                            ALU.subtract).then_inc(exped, 1)
                    dve.wait_ge(exped, 2)
                    if soft == "all":
                        s.then(nc.vector.reduce_sum(r1[:], Ex[:], AX.X))
                        s.then(nc.vector.reciprocal(r2[:], r1[:]))
                        s.then(nc.vector.tensor_tensor(Ex[:], Ex[:], bc(r2[:, :, None], [P, NT, EP]),
                                                       ALU.mult))
                    s.then(nc.vector.tensor_tensor(Ex[:], Ex[:], pick[:], ALU.mult))
                    s.then(nc.vector.reduce_sum(r1[:], Ex[:], AX.X))
                    if soft == "all":
                        s.then(nc.vector.tensor_scalar(r1[:], r1[:], 1e-20, None, ALU.add))
                    s.then(nc.vector.reciprocal(r2[:], r1[:]))
                    s.then(nc.vector.tensor_tensor(shares[:, :, 0:EP], Ex[:],
                                                   bc(r2[:, :, None], [P, NT, EP]), ALU.mult))


def gated_experts(k, name, xT, w_dram, n_experts, M, y, shares, kind):
    nc = k.nc
    MC = M // P
    per, groups_per = 2 * NCH * MC, 2 * NCH
    turns = n_experts // 2
    halves = TPC // 2
    WF = 2 * KD * M + MC * D
    gu_done, f_done, g_done, a_done, down_done, added, zeroed = (
        k.sem(f"{name}_{s}") for s in ("gu", "f", "g", "a", "down", "added", "zeroed"))
    w_loaded = [k.sem(f"{name}_wload{u}") for u in range(2)]
    with ExitStack() as ctx:
        w = [k.sb(f"{name}_w{u}", [P, WF], ctx=ctx) for u in range(2)]
        gate = [x[:, 0:KD * M].rearrange("p (c m) -> p c m", c=KD) for x in w]
        up = [x[:, KD * M:2 * KD * M].rearrange("p (c m) -> p c m", c=KD) for x in w]
        down = [x[:, 2 * KD * M:WF].rearrange("p (j d) -> p j d", j=MC) for x in w]
        fs = [k.sb(f"{name}_f{i}", [P, CH], ctx=ctx) for i in range(2)]
        gs = [k.sb(f"{name}_g{i}", [P, CH], ctx=ctx) for i in range(2)]
        hid = [k.sb(f"{name}_h{i}", [P, MC, CH], ctx=ctx) for i in range(2)]
        gps = [k.ps(f"{name}_gps{i}", [P, CH], ctx) for i in range(2)]
        ups = [k.ps(f"{name}_ups{i}", [P, CH], ctx) for i in range(2)]
        dps = [k.ps(f"{name}_dps{i}", [P, 2, D], ctx) for i in range(4)]
        steps = [(u, c, m) for u in range(2) for c in range(NCH) for m in range(MC)]
        with nc.Block() as block:
            @block.sync
            def _(sp):
                for u in range(2):
                    sp.dma_start(w[u][:], w_dram[u]).then_inc(w_loaded[u], 16)
                with sp.Fori(0, turns - 1) as i:
                    for u in range(2):
                        sp.wait_ge(down_done, halves * NCH * (2 * i + u + 1))
                        sp.dma_start(w[u][:], w_dram[2 * i + (2 + u)]).then_inc(w_loaded[u], 16)

            @block.gpsimd
            def _(pool):
                nc.gpsimd.memset(y[:], 0.0).then_inc(zeroed, 1)

            @block.tensor
            def _(pe):
                def gate_up(i, n):
                    u, c, m = steps[n]
                    if c == 0 and m == 0:
                        pe.wait_ge(w_loaded[u], 16 * i + 16)
                    pe.wait_ge(a_done, per * i + (n + 1))
                    for ps, wt in ((gps, gate), (ups, up)):
                        for c2 in range(KD):
                            last = nc.tensor.matmul(ps[n % 2][:], wt[u][:, c2, m * P:(m + 1) * P],
                                                    xT[:, c2, c * CH:(c + 1) * CH],
                                                    start=(c2 == 0), stop=(c2 == KD - 1))
                    last.then_inc(gu_done, 1)

                def down_projection(i, q):
                    pe.wait_ge(a_done, per * i + ((q + 1) * MC + 2))
                    for t2 in range(halves):
                        pe.wait_ge(added, halves * groups_per * i + (halves * q + t2 + 1))
                        for t in range(2):
                            for m in range(MC):
                                last = nc.tensor.matmul(
                                    dps[(halves * q + t2) % 4][:, t, :],
                                    hid[q % 2][:, m, (2 * t2 + t) * P:(2 * t2 + t + 1) * P],
                                    down[q // NCH][:, m, :], start=(m == 0), stop=(m == MC - 1))
                        last.then_inc(down_done, 1)

                with pe.Fori(0, turns) as i:
                    gate_up(i, 0)
                    for n in range(per):
                        if n + 1 < per:
                            gate_up(i, n + 1)
                        if n % MC == MC - 1:
                            down_projection(i, n // MC)

            @block.scalar
            def _(act):
                with act.Fori(0, turns) as i:
                    for n in range(per):
                        act.wait_ge(a_done, per * i + (n + 1))
                        act.wait_ge(gu_done, per * i + (n + 1))
                        if kind == "leaky":
                            nc.scalar.activation(fs[n % 2][:], gps[n % 2][:], ACT.Copy).then_inc(f_done, 1)
                        else:
                            nc.scalar.activation(fs[n % 2][:], ups[n % 2][:], ACT.Silu).then_inc(f_done, 1)

            @block.vector
            def _(dve):
                dve.sem_inc(a_done, 2)
                dve.sem_inc(added, 4)
                dve.wait_ge(zeroed, 1)

                def activate(i, n):
                    q, m = n // MC, n % MC
                    if m == 0 and q >= 2:
                        dve.wait_ge(down_done, halves * groups_per * i + halves * (q - 1))
                    dve.wait_ge(f_done, per * i + (n + 1))
                    h = hid[q % 2][:, m, :]
                    if kind == "leaky":
                        nc.vector.scalar_tensor_tensor(out=gs[n % 2][:], in0=fs[n % 2][:], scalar=0.01,
                                                       in1=gps[n % 2][:], op0=ALU.mult,
                                                       op1=ALU.max).then_inc(g_done, 1)
                        dve.wait_ge(g_done, per * i + (n + 1))
                        nc.vector.tensor_tensor(h, gs[n % 2][:], ups[n % 2][:], ALU.mult).then_inc(a_done, 1)
                    else:
                        nc.vector.tensor_tensor(h, fs[n % 2][:], gps[n % 2][:], ALU.mult).then_inc(a_done, 1)

                def accumulate(i, q):
                    u, c = q // NCH, q % NCH
                    for t2 in range(halves):
                        at = halves * groups_per * i + (halves * q + t2 + 1)
                        dve.wait_ge(added, at)
                        dve.wait_ge(down_done, at)
                        for t in range(2):
                            tt = c * TPC + 2 * t2 + t
                            last = nc.vector.scalar_tensor_tensor(
                                out=y[:, tt, :], in0=dps[(halves * q + t2) % 4][:, t, :],
                                scalar=shares[:, tt, bass.ds(2 * i + u, 1)], in1=y[:, tt, :],
                                op0=ALU.mult, op1=ALU.add)
                        last.then_inc(added, 1)

                with dve.Fori(0, turns) as i:
                    for n in range(per):
                        activate(i, n)
                        if n % MC == MC - 1 and n // MC >= 1:
                            accumulate(i, n // MC - 1)
                    accumulate(i, groups_per - 1)


def picked_ffn(k, name, src, picked, w1_dram, b1_dram, wo_dram, bo_dram, dst, ident, E):
    nc = k.nc
    FC = b1_dram.shape[1] // P
    loaded, masked, turned, taken, hps_done, gelu_done, out_done, out_sum, dve_done, ohT = (
        k.sem(f"{name}_{s}") for s in
        ("loaded", "masked", "turned", "taken", "hps", "gelu", "out", "sum", "dve", "ohT"))
    TG = E * TPC // 2
    with ExitStack() as ctx:
        w1 = k.sb(name + "_w1", [P, E, KD, FC * P], ctx=ctx)
        b1 = k.sb(name + "_b1", [E, FC * P], ctx=ctx)
        wo = k.sb(name + "_wo", [P, FC, D], ctx=ctx)
        bo = k.sb(name + "_bo", [P, D], ctx=ctx)
        ym = k.sb(name + "_ym", [P, E, TPC, D], ctx=ctx)
        ymT = k.sb(name + "_ymT", [P, E, KD, CH], ctx=ctx)
        pk = k.sb(name + "_pk", [P, TPC, E], ctx=ctx)
        pkT = k.sb(name + "_pkT", [E, CH], ctx=ctx)
        hid = k.sb(name + "_hid", [P, FC, CH], ctx=ctx)
        tmp = k.sb(name + "_tmp", [P, 2, 2, D], ctx=ctx)
        tps = [k.ps(f"{name}_tps{i}", [P, KD, 2 * P], ctx) for i in range(2)]
        hps = [k.ps(f"{name}_hps{i}", [P, CH], ctx) for i in range(2)]
        ops = [k.ps(f"{name}_ops{i}", [P, 2, D], ctx) for i in range(2)]
        kps = k.ps(name + "_kps", [E, CH], ctx)
        with nc.Block() as block:
            @block.sync
            def _(sp):
                sp.dma_start(w1[:], w1_dram).then_inc(loaded, 16)
                sp.dma_start(b1[:], b1_dram).then_inc(loaded, 16)
                sp.dma_start(wo[:], wo_dram).then_inc(loaded, 16)
                sp.dma_start(bo[:], bo_dram.partition_broadcast(P)).then_inc(loaded, 16)

            @block.tensor
            def _(pe):
                with pe.Fori(0, NCH) as c:
                    pe.wait_ge(masked, (E + 1) * c + (E + 1))
                    for t in range(TPC):
                        last = nc.tensor.transpose(kps[:, t * P:(t + 1) * P], pk[:, t, :], ident[:])
                    last.then_inc(ohT, 1)
                    for g in range(TG):
                        e, t2 = g // 2, g % 2
                        pe.wait_ge(taken, TG * c + (g + 1))
                        for c2 in range(KD):
                            for t in range(2):
                                last = nc.tensor.transpose(tps[g % 2][:, c2, t * P:(t + 1) * P],
                                                           ym[:, e, 2 * t2 + t, c2 * P:(c2 + 1) * P],
                                                           ident[:])
                        last.then_inc(turned, 1)
                    pe.wait_ge(loaded, 64)
                    pe.wait_ge(taken, TG * c + (TG + 2))
                    pe.wait_ge(ohT, 2 * c + 2)
                    for f in range(FC):
                        pe.wait_ge(gelu_done, FC * c + (f + 1))
                        for e in range(E):
                            for c2 in range(KD):
                                nc.tensor.matmul(hps[f % 2][:], w1[:, e, c2, f * P:(f + 1) * P],
                                                 ymT[:, e, c2, :], start=(e == 0 and c2 == 0), stop=False)
                        nc.tensor.matmul(hps[f % 2][:], b1[:, f * P:(f + 1) * P], pkT[:],
                                         start=False, stop=True).then_inc(hps_done, 1)
                    pe.wait_ge(gelu_done, FC * c + (FC + 2))
                    for t2 in range(2):
                        pe.wait_ge(out_sum, 2 * c + (t2 + 1))
                        for t in range(2):
                            for f in range(FC):
                                last = nc.tensor.matmul(ops[t2][:, t, :],
                                                        hid[:, f, (2 * t2 + t) * P:(2 * t2 + t + 1) * P],
                                                        wo[:, f, :], start=(f == 0), stop=(f == FC - 1))
                        last.then_inc(out_done, 1)

            @block.scalar
            def _(act):
                act.sem_inc(gelu_done, 2)
                with act.Fori(0, NCH) as c:
                    for f in range(FC):
                        if f == 0:
                            act.wait_ge(out_done, 2 * c + 1)
                        act.wait_ge(hps_done, FC * c + (f + 1))
                        nc.scalar.activation(hid[:, f, :], hps[f % 2][:], ACT.Gelu).then_inc(gelu_done, 1)

            @block.vector
            def _(dve):
                dve.sem_inc(out_done, 1)
                dve.sem_inc(taken, 2)
                dve.sem_inc(out_sum, 2)
                dve.wait_ge(loaded, 64)
                with dve.Fori(0, NCH) as c:
                    dve.wait_ge(out_done, 2 * c + 1)
                    nc.vector.tensor_copy(pk[:], picked[:, bass.ts(c, TPC), 0:E]).then_inc(masked, 1)
                    for e in range(E):
                        nc.vector.tensor_tensor(ym[:, e], src[:, bass.ts(c, TPC), :],
                                                bc(picked[:, bass.ts(c, TPC), e:e + 1], [P, TPC, D]),
                                                ALU.mult).then_inc(masked, 1)
                    dve.wait_ge(ohT, 2 * c + 1)
                    nc.vector.tensor_copy(pkT[:], kps[:]).then_inc(ohT, 1)
                    for g in range(TG):
                        e, t2 = g // 2, g % 2
                        dve.wait_ge(turned, TG * c + (g + 1))
                        nc.vector.tensor_copy(ymT[:, e, :, 2 * t2 * P:(2 * t2 + 2) * P],
                                              tps[g % 2][:]).then_inc(taken, 1)
                    for t2 in range(2):
                        dve.wait_ge(out_done, 2 * c + (t2 + 2))
                        dve.wait_ge(out_sum, 2 * c + (t2 + 1))
                        nc.vector.tensor_tensor(tmp[:, t2], ops[t2][:], bc(bo[:, None, :], [P, 2, D]),
                                                ALU.add).then_inc(dve_done, 1)
                        dve.wait_ge(dve_done, 2 * c + (t2 + 1))
                        nc.vector.tensor_tensor(dst[:, bass.ds(c * TPC + 2 * t2, 2), :], tmp[:, t2],
                                                src[:, bass.ds(c * TPC + 2 * t2, 2), :],
                                                ALU.add).then_inc(out_sum, 1)


def lora_ffn(k, name, xT, picked, w, x, ident):
    nc = k.nc
    wi_dram, bi_dram, wo_dram, bo_dram, la_dram, lb_dram = w
    R = la_dram.shape[2]
    E = 8
    FC = wi_dram.shape[2] // P
    loaded, spread, turned, pick_done, u_done, u_masked, hps_done, relu_done, out_done, out_sum, dve_done = (
        k.sem(f"{name}_{s}") for s in ("loaded", "spread", "turned", "pick", "u", "um", "hps", "relu",
                                       "out", "sum", "dve"))
    with ExitStack() as ctx:
        wi = k.sb(name + "_wi", [P, KD, FC * P], ctx=ctx)
        bi = k.sb(name + "_bi", [P, FC], ctx=ctx)
        wo = k.sb(name + "_wo", [P, FC, D], ctx=ctx)
        bo = k.sb(name + "_bo", [P, D], ctx=ctx)
        la = k.sb(name + "_la", [P, KD, R], ctx=ctx)
        lb = k.sb(name + "_lb", [R, FC * P], ctx=ctx)
        pk = k.sb(name + "_pk", [P, TPC, R], ctx=ctx)
        pkT = k.sb(name + "_pkT", [R, CH], ctx=ctx)
        um = k.sb(name + "_um", [R, CH], ctx=ctx)
        hid = k.sb(name + "_hid", [P, FC, CH], ctx=ctx)
        tmp = k.sb(name + "_tmp", [P, 2, 2, D], ctx=ctx)
        hps = [k.ps(f"{name}_hps{i}", [P, CH], ctx) for i in range(2)]
        ops = [k.ps(f"{name}_ops{i}", [P, 2, D], ctx) for i in range(2)]
        kps = k.ps(name + "_kps", [R, CH], ctx)
        ups = k.ps(name + "_ups", [R, CH], ctx)
        with nc.Block() as block:
            @block.sync
            def _(sp):
                for tile, dram in ((wi, wi_dram), (bi, bi_dram), (wo, wo_dram), (la, la_dram), (lb, lb_dram)):
                    sp.dma_start(tile[:], dram).then_inc(loaded, 16)
                sp.dma_start(bo[:], bo_dram.partition_broadcast(P)).then_inc(loaded, 16)

            @block.tensor
            def _(pe):
                pe.wait_ge(loaded, 6 * 16)
                with pe.Fori(0, NCH) as c:
                    pe.wait_ge(spread, c + 1)
                    for t in range(TPC):
                        last = nc.tensor.transpose(kps[:, t * P:(t + 1) * P], pk[:, t, :], ident[:])
                    last.then_inc(turned, 1)
                    for c2 in range(KD):
                        last = nc.tensor.matmul(ups[:], la[:, c2, :], xT[:, c2, bass.ts(c, CH)],
                                                start=(c2 == 0), stop=(c2 == KD - 1))
                    last.then_inc(u_done, 1)
                    pe.wait_ge(u_masked, c + 1)
                    for f in range(FC):
                        pe.wait_ge(relu_done, FC * c + (f + 1))
                        for c2 in range(KD):
                            nc.tensor.matmul(hps[f % 2][:], wi[:, c2, f * P:(f + 1) * P],
                                             xT[:, c2, bass.ts(c, CH)], start=(c2 == 0), stop=False)
                        nc.tensor.matmul(hps[f % 2][:], lb[:, f * P:(f + 1) * P], um[:],
                                         start=False, stop=True).then_inc(hps_done, 1)
                    pe.wait_ge(relu_done, FC * c + (FC + 2))
                    for t2 in range(2):
                        pe.wait_ge(out_sum, 2 * c + (t2 + 1))
                        for t in range(2):
                            for f in range(FC):
                                last = nc.tensor.matmul(ops[t2][:, t, :],
                                                        hid[:, f, (2 * t2 + t) * P:(2 * t2 + t + 1) * P],
                                                        wo[:, f, :], start=(f == 0), stop=(f == FC - 1))
                        last.then_inc(out_done, 1)

            @block.scalar
            def _(act):
                act.sem_inc(relu_done, 2)
                act.wait_ge(loaded, 6 * 16)
                with act.Fori(0, NCH) as c:
                    for f in range(FC):
                        if f == 0:
                            act.wait_ge(out_done, 2 * c + 1)
                        act.wait_ge(hps_done, FC * c + (f + 1))
                        nc.scalar.activation(hid[:, f, :], hps[f % 2][:], ACT.Relu,
                                             bias=bi[:, f:f + 1]).then_inc(relu_done, 1)

            @block.vector
            def _(dve):
                dve.sem_inc(out_done, 1)
                dve.sem_inc(out_sum, 2)
                dve.wait_ge(loaded, 6 * 16)
                with dve.Fori(0, NCH) as c:
                    dve.wait_ge(out_done, 2 * c + 1)
                    nc.vector.tensor_copy(pk[:].rearrange("p t (e r) -> p t e r", e=E),
                                          bc(picked[:, bass.ts(c, TPC), :, None], [P, TPC, E, R // E])
                                          ).then_inc(spread, 1)
                    dve.wait_ge(turned, c + 1)
                    nc.vector.tensor_copy(pkT[:], kps[:]).then_inc(pick_done, 1)
                    dve.wait_ge(u_done, c + 1)
                    dve.wait_ge(pick_done, c + 1)
                    nc.vector.tensor_tensor(um[:], ups[:], pkT[:], ALU.mult).then_inc(u_masked, 1)
                    for t2 in range(2):
                        rows = x[:, bass.ds(c * TPC + 2 * t2, 2), :]
                        dve.wait_ge(out_done, 2 * c + (t2 + 2))
                        dve.wait_ge(out_sum, 2 * c + (t2 + 1))
                        nc.vector.tensor_tensor(tmp[:, t2], ops[t2][:], bc(bo[:, None, :], [P, 2, D]),
                                                ALU.add).then_inc(dve_done, 1)
                        dve.wait_ge(dve_done, 2 * c + (t2 + 1))
                        nc.vector.tensor_tensor(rows, tmp[:, t2], rows, ALU.add).then_inc(out_sum, 1)


def round_to_e4m3(k, name, src, dst, in_scale_dram, scale_out):
    nc = k.nc
    loaded, done = k.sem(name + "_loaded"), k.sem(name + "_done")
    with ExitStack() as ctx:
        v = k.sb(name + "_v", [P, NT, D], ctx=ctx)
        m = k.sb(name + "_m", [P, NT, D], ctx=ctx)
        r = k.sb(name + "_r", [P, 1], ctx=ctx)
        with nc.Block() as block:
            @block.sync
            def _(sp):
                sp.dma_start(scale_out[:], in_scale_dram.partition_broadcast(P)).then_inc(loaded, 16)

            @block.vector
            def _(dve):
                s = Steps(dve, done)
                dve.wait_ge(loaded, 16)
                s.then(nc.vector.reciprocal(r[:], scale_out[:]))
                s.then(nc.vector.tensor_scalar(v[:], src[:], r[:, 0:1], 448.0, ALU.mult, ALU.min))
                s.then(nc.vector.tensor_scalar(v[:], v[:], -448.0, None, ALU.max))
                s.then(nc.vector.tensor_scalar(m[:].bitcast(U32), v[:].bitcast(U32), 0x7F800000, None,
                                               ALU.bitwise_and))
                s.then(nc.vector.tensor_scalar(m[:], m[:], 2.0 ** -6, 1.5 * 2.0 ** 20, ALU.max, ALU.mult))
                s.then(nc.vector.tensor_tensor(v[:], v[:], m[:], ALU.add))
                s.then(nc.vector.tensor_tensor(v[:], v[:], m[:], ALU.subtract))
                nc.vector.tensor_scalar(dst[:], v[:], scale_out[:, 0:1], None, ALU.mult)


def linear(k, name, xT, w_dram, scale_dram, bias_dram, x):
    nc = k.nc
    loaded, scaled, mm, tmp_done, added = (k.sem(f"{name}_{s}") for s in
                                           ("loaded", "scaled", "mm", "tmp", "added"))
    with ExitStack() as ctx:
        w = k.sb(name + "_w", [P, KD, D], ctx=ctx)
        ws = k.sb(name + "_ws", [P, KD, D], ctx=ctx)
        bo = k.sb(name + "_b", [P, D], ctx=ctx)
        sc = k.sb(name + "_sc", [P, 1], ctx=ctx)
        tmp = k.sb(name + "_tmp", [P, 4, 2, D], ctx=ctx)
        ps = [k.ps(f"{name}_ps{i}", [P, 2, D], ctx) for i in range(4)]
        with nc.Block() as block:
            @block.sync
            def _(sp):
                sp.dma_start(w[:], w_dram).then_inc(loaded, 16)
                sp.dma_start(bo[:], bias_dram.partition_broadcast(P)).then_inc(loaded, 16)
                sp.dma_start(sc[:], scale_dram.partition_broadcast(P)).then_inc(loaded, 16)

            @block.tensor
            def _(pe):
                pe.wait_ge(scaled, 1)
                for t2 in range(NT // 2):
                    if t2 >= 4:
                        pe.wait_ge(tmp_done, t2 - 3)
                    for t in range(2):
                        tt = 2 * t2 + t
                        for c in range(KD):
                            last = nc.tensor.matmul(ps[t2 % 4][:, t, :], xT[:, c, tt * P:(tt + 1) * P],
                                                    ws[:, c, :], start=(c == 0), stop=(c == KD - 1))
                    last.then_inc(mm, 1)

            @block.vector
            def _(dve):
                dve.wait_ge(loaded, 48)
                nc.vector.tensor_scalar(ws[:], w[:], sc[:, 0:1], None, ALU.mult).then_inc(scaled, 1)
                for t2 in range(NT // 2):
                    rows = x[:, 2 * t2:2 * t2 + 2, :]
                    dve.wait_ge(mm, t2 + 1)
                    nc.vector.tensor_tensor(tmp[:, t2 % 4], ps[t2 % 4][:], bc(bo[:, None, :], [P, 2, D]),
                                            ALU.add).then_inc(tmp_done, 1)
                    dve.wait_ge(tmp_done, t2 + 1)
                    nc.vector.tensor_tensor(rows, tmp[:, t2 % 4], rows, ALU.add).then_inc(added, 1)


CAPACITY = 2 * (2 * 512) * 2 // 8


def places(k, name, chosen, rank, upper):
    nc = k.nc
    EP = 8
    made, mm, done = k.sem(name + "_made"), k.sem(name + "_mm"), k.sem(name + "_done")
    with ExitStack() as ctx:
        ones = k.sb(name + "_ones", [P, P], ctx=ctx)
        before = k.sb(name + "_before", [P, NT, EP], ctx=ctx)
        cps = k.ps(name + "_cps", [P, NT, EP], ctx)
        tps = k.ps(name + "_tps", [P, NT, EP], ctx)
        with nc.Block() as block:
            @block.gpsimd
            def _(pool):
                nc.gpsimd.memset(ones[:], 1.0).then_inc(made, 1)

            @block.tensor
            def _(pe):
                pe.wait_ge(made, 1)
                nc.tensor.matmul(cps[:], upper[:], chosen[:], start=True, stop=True).then_inc(mm, 1)
                nc.tensor.matmul(tps[:], ones[:], chosen[:], start=True, stop=True).then_inc(mm, 1)

            @block.vector
            def _(dve):
                s = Steps(dve, done)
                s.then(nc.vector.memset(before[:], 0.0))
                dve.wait_ge(mm, 2)
                for t in range(1, NT):
                    s.then(nc.vector.tensor_tensor(before[:, t, :], tps[:, t - 1, :], before[:, t - 1, :],
                                                   ALU.add))
                s.then(nc.vector.tensor_tensor(rank[:], cps[:], before[:], ALU.add))


def drop_over_capacity(k, name, shares, rank):
    nc = k.nc
    done = k.sem(name)
    with nc.Block() as block:
        @block.vector
        def _(dve):
            nc.vector.scalar_tensor_tensor(out=shares[:], in0=rank[:], scalar=float(CAPACITY), in1=shares[:],
                                           op0=ALU.is_le, op1=ALU.mult)


def sent_experts(k, name, src, shares, chosen, rank, w_dram, M, E, x, rows_dram, out_dram, ident):
    nc = k.nc
    MC = M // P
    CT = CAPACITY // P
    SLOTS = E * CAPACITY
    OVER, OTHER = float(2 ** 20), float(2 ** 22)
    WF = 2 * KD * M + MC * D
    per, turns = 2 * MC, E // 2
    names = ("zeroed", "blank", "index_ready", "base", "dve", "sent", "x_turned", "x_act", "x_dve", "gu",
             "f", "hidden", "down", "y_act", "y_dve", "stored", "stored_ahead", "added")
    (zeroed, blank, index_ready, base_made, dve_done, sent, x_turned, x_act, x_dve, gu_done, f_done, hid_done,
     down_done, y_act, y_dve, stored, stored_ahead, added) = (k.sem(f"{name}_{n}") for n in names)
    w_loaded = [k.sem(f"{name}_w_loaded{u}") for u in range(2)]
    x_loaded = [k.sem(f"{name}_x_loaded{u}") for u in range(2)]
    BACK = 4
    fetched = [k.sem(f"{name}_fetched{u}") for u in range(BACK)]
    slots_of = lambda dram: dram.rearrange("(e t p) d -> e p t d", e=E, t=CT)
    with ExitStack() as ctx:
        zero = k.sb(name + "_zero", [P, 8, D], ctx=ctx)
        base = k.sb(name + "_base", [P, E], ctx=ctx)
        v, pick, other = (k.sb(f"{name}_{n}", [P, NT, E], ctx=ctx) for n in ("v", "pick", "other"))
        slot = [k.sb(f"{name}_slot{n}", [P, NT], ctx=ctx) for n in range(2)]
        total = k.sb(name + "_total", [P, NT], ctx=ctx)
        near = k.sb(name + "_near", [P, 2, NT], ctx=ctx)
        send = k.sb(name + "_send", [P, 2, NT], U32, ctx=ctx)
        fetch = k.sb(name + "_fetch", [P, 2, NT], U32, ctx=ctx)
        share = k.sb(name + "_share", [P, 2, NT], ctx=ctx)
        w = [k.sb(f"{name}_w{u}", [P, WF], ctx=ctx) for u in range(2)]
        gate = [t[:, 0:KD * M].rearrange("p (c m) -> p c m", c=KD) for t in w]
        up = [t[:, KD * M:2 * KD * M].rearrange("p (c m) -> p c m", c=KD) for t in w]
        down = [t[:, 2 * KD * M:WF].rearrange("p (j d) -> p j d", j=MC) for t in w]
        xg = [k.sb(f"{name}_xg{u}", [P, CT, D], ctx=ctx) for u in range(2)]
        xgT = [k.sb(f"{name}_xgT{u}", [P, KD, CAPACITY], ctx=ctx) for u in range(2)]
        yg = [k.sb(f"{name}_yg{u}", [P, CT, D], ctx=ctx) for u in range(2)]
        fs = [k.sb(f"{name}_f{i}", [P, CAPACITY], ctx=ctx) for i in range(2)]
        hid = [k.sb(f"{name}_h{i}", [P, MC, CAPACITY], ctx=ctx) for i in range(2)]
        back = [k.sb(f"{name}_back{i}", [P, D], ctx=ctx) for i in range(BACK)]
        tps = [k.ps(f"{name}_tps{i}", [P, KD, 2 * P], ctx) for i in range(2)]
        gps = [k.ps(f"{name}_gps{i}", [P, CAPACITY], ctx) for i in range(2)]
        ups = [k.ps(f"{name}_ups{i}", [P, CAPACITY], ctx) for i in range(2)]
        dps = [k.ps(f"{name}_dps{i}", [P, 2, D], ctx) for i in range(2)]
        with nc.Block() as block:
            @block.sync
            def _(sp):
                for u in range(2):
                    sp.dma_start(w[u][:], w_dram[u]).then_inc(w_loaded[u], 16)
                sp.wait_ge(zeroed, 1)
                for n in range(SLOTS // P // 8):
                    sp.dma_start(rows_dram[n * 8 * P:(n + 1) * 8 * P, :].rearrange("(p t) d -> p t d", t=8),
                                 zero[:]).then_inc(blank, 16)
                sp.wait_ge(blank, 16 * (SLOTS // P // 8))
                sp.sem_inc(stored_ahead, 2)
                sp.wait_ge(sent, 16 * 2 * NT)
                for u in range(2):
                    sp.dma_start(xg[u][:], slots_of(rows_dram)[u]).then_inc(x_loaded[u], 16)

                def store(i, u):
                    sp.wait_ge(y_act, 2 * i + (u + 2))
                    sp.wait_ge(y_dve, 2 * i + (u + 2))
                    sp.dma_start(slots_of(out_dram)[2 * i + u], yg[u][:]).then_inc(stored, 16)
                    sp.wait_ge(stored, 32 * i + 16 * (u + 1))
                    sp.sem_inc(stored_ahead, 1)

                with sp.Fori(0, turns - 1) as i:
                    for u in range(2):
                        sp.wait_ge(x_turned, 4 * i + 2 * (u + 1))
                        sp.dma_start(xg[u][:], slots_of(rows_dram)[2 * i + (2 + u)]).then_inc(x_loaded[u], 16)
                        sp.wait_ge(down_done, 4 * i + 2 * (u + 1))
                        sp.dma_start(w[u][:], w_dram[2 * i + (2 + u)]).then_inc(w_loaded[u], 16)
                        store(i, u)
                for u in range(2):
                    store(turns - 1, u)
                sp.wait_ge(stored, 16 * E)

            @block.gpsimd
            def _(pool):
                nc.gpsimd.memset(zero[:], 0.0).then_inc(zeroed, 1)
                nc.gpsimd.iota(base[:], [[CAPACITY, E]], base=-1, channel_multiplier=0,
                               allow_small_or_imprecise_dtypes=True).then_inc(base_made, 1)
                pool.wait_ge(index_ready, 2)
                pool.wait_ge(blank, 16 * (SLOTS // P // 8))
                for n in range(2):
                    for t in range(NT):
                        pool.indirect_dma_start(
                            rows_dram, bass.IndirectOffsetOnAxis(ap=send[:, n, t:t + 1], axis=0),
                            src[:, t, :], None, bounds_check=SLOTS - 1, oob_is_err=False).then_inc(sent, 16)
                pool.wait_ge(index_ready, 4)
                pool.wait_ge(stored, 16 * E)
                for n in range(2):
                    for t in range(NT):
                        at = n * NT + t
                        if at >= BACK:
                            pool.wait_ge(added, at - BACK + 1)
                        pool.indirect_dma_start(
                            back[at % BACK][:], None, out_dram,
                            bass.IndirectOffsetOnAxis(ap=fetch[:, n, t:t + 1], axis=0),
                            bounds_check=SLOTS - 1, oob_is_err=False).then_inc(fetched[at % BACK], 16)

            @block.tensor
            def _(pe):
                def turn(i, u):
                    pe.wait_ge(x_loaded[u], 16 * i + 16)
                    for half in range(CT // 2):
                        pe.wait_ge((x_act, x_dve)[half], 2 * i + (u + 1))
                        for c in range(KD):
                            for t in range(2):
                                last = nc.tensor.transpose(tps[half][:, c, t * P:(t + 1) * P],
                                                           xg[u][:, 2 * half + t, c * P:(c + 1) * P], ident[:])
                        last.then_inc(x_turned, 1)

                def gate_up(i, u, m):
                    n = u * MC + m
                    if m == 0:
                        pe.wait_ge(w_loaded[u], 16 * i + 16)
                        pe.wait_ge(x_act, 2 * i + (u + 2))
                        pe.wait_ge(x_dve, 2 * i + (u + 2))
                    pe.wait_ge(hid_done, per * i + (n + 1))
                    for ps, wt in ((gps, gate), (ups, up)):
                        for c in range(KD):
                            last = nc.tensor.matmul(ps[n % 2][:], wt[u][:, c, m * P:(m + 1) * P],
                                                    xgT[u][:, c, :], start=(c == 0), stop=(c == KD - 1))
                    last.then_inc(gu_done, 1)

                def down_projection(i, u):
                    pe.wait_ge(hid_done, per * i + ((u + 1) * MC + 2))
                    for half in range(CT // 2):
                        pe.wait_ge((y_act, y_dve)[half], 2 * i + (u + 1))
                        for t in range(2):
                            for m in range(MC):
                                last = nc.tensor.matmul(
                                    dps[half][:, t, :], hid[u][:, m, (2 * half + t) * P:(2 * half + t + 1) * P],
                                    down[u][:, m, :], start=(m == 0), stop=(m == MC - 1))
                        last.then_inc(down_done, 1)

                with pe.Fori(0, turns) as i:
                    turn(i, 0)
                    for m in range(MC):
                        gate_up(i, 0, m)
                    turn(i, 1)
                    down_projection(i, 0)
                    for m in range(MC):
                        gate_up(i, 1, m)
                    down_projection(i, 1)

            @block.scalar
            def _(act):
                act.sem_inc(x_act, 1)
                act.sem_inc(y_act, 1)

                def take_columns(i, u):
                    act.wait_ge(x_turned, 4 * i + (2 * u + 1))
                    nc.scalar.activation(xgT[u][:, :, 0:2 * P], tps[0][:], ACT.Copy).then_inc(x_act, 1)

                def silu(i, u, m):
                    n = u * MC + m
                    act.wait_ge(hid_done, per * i + (n + 1))
                    act.wait_ge(gu_done, per * i + (n + 1))
                    nc.scalar.activation(fs[n % 2][:], ups[n % 2][:], ACT.Silu).then_inc(f_done, 1)

                def take_output(i, u):
                    act.wait_ge(down_done, 4 * i + (2 * u + 1))
                    act.wait_ge(stored_ahead, 2 * i + (u + 1))
                    nc.scalar.activation(yg[u][:, 0:2, :], dps[0][:], ACT.Copy).then_inc(y_act, 1)

                with act.Fori(0, turns) as i:
                    take_columns(i, 0)
                    for m in range(MC):
                        silu(i, 0, m)
                    take_columns(i, 1)
                    take_output(i, 0)
                    for m in range(MC):
                        silu(i, 1, m)
                    take_output(i, 1)

            @block.vector
            def _(dve):
                s = Steps(dve, dve_done)
                dve.sem_inc(x_dve, 1)
                dve.sem_inc(y_dve, 1)
                dve.sem_inc(hid_done, 2)
                dve.wait_ge(base_made, 1)
                s.then(nc.vector.tensor_scalar(v[:], rank[:], float(CAPACITY), OVER, ALU.is_gt, ALU.mult))
                s.then(nc.vector.tensor_tensor(v[:], v[:], rank[:], ALU.add))
                s.then(nc.vector.tensor_tensor(v[:], v[:], bc(base[:, None, :], [P, NT, E]), ALU.add))
                s.then(nc.vector.tensor_scalar(other[:], chosen[:], 1.0, -OTHER, ALU.subtract, ALU.mult))
                s.then(nc.vector.tensor_tensor(other[:], other[:], v[:], ALU.add))
                s.then(nc.vector.tensor_reduce(slot[0][:], other[:], AX.X, ALU.min))
                s.then(nc.vector.tensor_tensor(pick[:], v[:], chosen[:], ALU.mult))
                s.then(nc.vector.reduce_sum(total[:], pick[:], AX.X))
                s.then(nc.vector.tensor_tensor(slot[1][:], total[:], slot[0][:], ALU.subtract))
                for n in range(2):
                    nc.vector.tensor_copy(send[:, n, :], slot[n][:]).then_inc(index_ready, 1)
                for n in range(2):
                    s.then(nc.vector.tensor_scalar(near[:, n, :], slot[n][:], float(SLOTS - 1), None, ALU.min))
                    nc.vector.tensor_copy(fetch[:, n, :], near[:, n, :]).then_inc(index_ready, 1)
                    s.then(nc.vector.tensor_tensor(pick[:], v[:], bc(slot[n][:, :, None], [P, NT, E]),
                                                   ALU.is_equal))
                    s.then(nc.vector.tensor_tensor(pick[:], pick[:], shares[:], ALU.mult))
                    s.then(nc.vector.reduce_sum(share[:, n, :], pick[:], AX.X))

                def take_columns(i, u):
                    dve.wait_ge(x_turned, 4 * i + (2 * u + 2))
                    nc.vector.tensor_copy(xgT[u][:, :, 2 * P:4 * P], tps[1][:]).then_inc(x_dve, 1)

                def multiply(i, u, m):
                    n = u * MC + m
                    dve.wait_ge(f_done, per * i + (n + 1))
                    nc.vector.tensor_tensor(hid[u][:, m, :], fs[n % 2][:], gps[n % 2][:],
                                            ALU.mult).then_inc(hid_done, 1)

                def take_output(i, u):
                    dve.wait_ge(down_done, 4 * i + (2 * u + 2))
                    dve.wait_ge(stored_ahead, 2 * i + (u + 1))
                    nc.vector.tensor_copy(yg[u][:, 2:4, :], dps[1][:]).then_inc(y_dve, 1)

                with dve.Fori(0, turns) as i:
                    take_columns(i, 0)
                    for m in range(MC):
                        multiply(i, 0, m)
                    take_columns(i, 1)
                    take_output(i, 0)
                    for m in range(MC):
                        multiply(i, 1, m)
                    take_output(i, 1)
                for n in range(2):
                    for t in range(NT):
                        at = n * NT + t
                        dve.wait_ge(fetched[at % BACK], 16 * (at // BACK + 1))
                        if n:
                            dve.wait_ge(added, at - NT + 1)
                        nc.vector.scalar_tensor_tensor(out=x[:, t, :], in0=back[at % BACK][:],
                                                       scalar=share[:, n, t:t + 1], in1=x[:, t, :],
                                                       op0=ALU.mult, op1=ALU.add).then_inc(added, 1)


TABLE = S + P - 1


def position_table(k, a, table_dram, ident):
    nc = k.nc
    NPT = S // P
    with ExitStack() as ctx:
        w0, b0, g0, b1, g1 = (k.sb("pt_" + n, [P, D], ctx=ctx) for n in ("w0", "b0", "g0", "b1", "g1"))
        w1 = k.sb("pt_w1", [P, KD, D], ctx=ctx)
        w2 = k.sb("pt_w2", [P, KD, HEADS], ctx=ctx)
        b2 = k.sb("pt_b2", [HEADS, 1], ctx=ctx)
        pos = k.sb("pt_pos", [P, NPT], ctx=ctx)
        h = k.sb("pt_h", [P, NPT, D], ctx=ctx)
        hn = k.sb("pt_hn", [P, NPT, D], ctx=ctx)
        hT = k.sb("pt_hT", [P, KD, S], ctx=ctx)
        tab = k.sb("pt_tab", [HEADS, TABLE], ctx=ctx)
        loaded, posd, made = k.sem("pt_loaded"), k.sem("pt_posd"), k.sem("pt_made")
        mm, stored, act_done = k.sem("pt_mm"), k.sem("pt_stored"), k.sem("pt_act")
        with nc.Block() as block:
            @block.sync
            def _(sp):
                for tile, n in ((w0, "w0"), (b0, "b0"), (g0, "g0"), (b1, "b1"), (g1, "g1")):
                    sp.dma_start(tile[:], a["l1_" + n].partition_broadcast(P)).then_inc(loaded, 16)
                sp.dma_start(w1[:], a["l1_w1"]).then_inc(loaded, 16)
                sp.dma_start(w2[:], a["l1_w2"]).then_inc(loaded, 16)
                sp.dma_start(b2[:], a["l1_b2"].rearrange("(h o) -> h o", o=1),
                             allow_slow_non_contiguous=True).then_inc(loaded, 16)
                sp.wait_ge(loaded, 8 * 16)

            @block.gpsimd
            def _(pool):
                nc.gpsimd.iota(pos[:], [[P, NPT]], base=0, channel_multiplier=1,
                               allow_small_or_imprecise_dtypes=True).then_inc(posd, 1)

            @block.vector
            def _(dve):
                dve.wait_ge(loaded, 8 * 16)
                dve.wait_ge(posd, 1)
                for t in range(NPT):
                    nc.vector.scalar_tensor_tensor(out=h[:, t, :], in0=w0[:], scalar=pos[:, t:t + 1],
                                                   in1=b0[:], op0=ALU.mult, op1=ALU.add)
        normalise(k, "pt_n0", h, hn, g0, 1e-5)
        with nc.Block() as block:
            @block.scalar
            def _(act):
                nc.scalar.activation(h[:], hn[:], ACT.Silu)
        to_feature_major(k, "pt_t0", h, hT, ident)
        with ExitStack() as inner:
            ps = [k.ps(f"pt_ps{i}", [P, 2, D], inner) for i in range(4)]
            with nc.Block() as block:
                @block.tensor
                def _(pe):
                    for t in range(NPT):
                        for c in range(KD):
                            last = nc.tensor.matmul(ps[t // 2][:, t % 2, :], hT[:, c, t * P:(t + 1) * P],
                                                    w1[:, c, :], start=(c == 0), stop=(c == KD - 1))
                        last.then_inc(mm, 1)

                @block.vector
                def _(dve):
                    for t2 in range(NPT // 2):
                        dve.wait_ge(mm, 2 * t2 + 2)
                        nc.vector.tensor_tensor(h[:, 2 * t2:2 * t2 + 2, :], ps[t2][:],
                                                bc(b1[:, None, :], [P, 2, D]), ALU.add)
        normalise(k, "pt_n1", h, hn, g1, 1e-5)
        with nc.Block() as block:
            @block.scalar
            def _(act):
                nc.scalar.activation(h[:], hn[:], ACT.Silu)
        to_feature_major(k, "pt_t1", h, hT, ident)
        with ExitStack() as inner:
            ps = [k.ps(f"pt_qs{i}", [HEADS, CH], inner) for i in range(2)]
            with nc.Block() as block:
                @block.tensor
                def _(pe):
                    for i in range(2):
                        for c in range(KD):
                            last = nc.tensor.matmul(ps[i][:], w2[:, c, :], hT[:, c, i * CH:(i + 1) * CH],
                                                    start=(c == 0), stop=(c == KD - 1))
                        last.then_inc(mm, 1)

                @block.vector
                def _(dve):
                    nc.vector.memset(tab[:, 0:P - 1], FAR).then_inc(made, 1)
                    for i in range(2):
                        dve.wait_ge(mm, NPT + i + 1)
                        nc.vector.tensor_scalar(tab[:, P - 1 + i * CH:P - 1 + (i + 1) * CH], ps[i][:],
                                                b2[:, 0:1], None, ALU.add).then_inc(made, 1)

                @block.sync
                def _(sp):
                    sp.wait_ge(made, 3)
                    sp.dma_start(table_dram, tab[:]).then_inc(stored, 16)
                    sp.wait_ge(stored, 16)


def attention(k, name, xT, w, cond_dram, condT_dram, mask_dram, acc, ident, bias_dram, table=False,
              l2=None, rq_dram=None):
    wq_dram, wkv_dram, wo_dram, nb_dram = w
    with ExitStack() as ctx:
        kA = k.sb(name + "_kA", [P, B, S], F32R, ctx=ctx)
        kB = k.sb(name + "_kB", [P, B, S], F32R, ctx=ctx)
        V = k.sb(name + "_V", [P, B, TB, 2 * DH], F32R, ctx=ctx)
        SNG = k.sb(name + "_SNG", [P, NT, HEADS], ctx=ctx)
        RN = k.sb(name + "_RN", [P, NT, HEADS], ctx=ctx)
        WO = k.sb(name + "_WO", [P, HEADS * D], ctx=ctx)
        with ExitStack() as inner:
            rq = None
            if l2:
                rq = k.sb(name + "_rq", [P, NT, HEADS], ctx=inner)
                query_norms(k, name + "_qn", xT, wq_dram, rq, rq_dram, ident)
            keys_and_values(k, name + "_kv", xT, wq_dram, wkv_dram, cond_dram, nb_dram, mask_dram, wo_dram,
                            ident, kA, kB, V, SNG, WO, rq, table, l2)
        heads_loop(k, name, xT, wq_dram, acc, ident, bias_dram, table, rq_dram, kA, kB, V, SNG, WO, RN)
        null_values(k, name + "_nv", acc, condT_dram, RN, WO, ident)


def query_norms(k, name, xT, wq_dram, rq, rq_dram, ident):
    nc = k.nc
    loaded, made, squared, summed, small, turned, taken, stored = (
        k.sem(f"{name}_{n}") for n in ("loaded", "made", "squared", "summed", "small", "turned", "taken",
                                       "stored"))
    HALF = HEADS // 2
    UNITS = 2 * NT
    with ExitStack() as ctx:
        wq = k.sb(name + "_wq", [P, KD, HEADS * DH], ctx=ctx)
        sq = [k.sb(f"{name}_sq{i}", [P, HALF, DH], ctx=ctx) for i in range(2)]
        norm = k.sb(name + "_norm", [P, NT, HEADS], ctx=ctx)
        rqT = k.sb(name + "_rqT", [HEADS, TOK], ctx=ctx)
        qps = [k.ps(f"{name}_q{i}", [P, HALF, DH], ctx) for i in range(4)]
        tps = [k.ps(f"{name}_t{i}", [HEADS, CH], ctx) for i in range(4)]
        with nc.Block() as block:
            @block.sync
            def _(sp):
                sp.dma_start(wq[:], wq_dram).then_inc(loaded, 16)
                for n in range(NCH):
                    sp.wait_ge(taken, n + 1)
                    sp.dma_start(rq_dram[:, n * CH:(n + 1) * CH], rqT[:, n * CH:(n + 1) * CH]).then_inc(stored, 16)
                sp.wait_ge(stored, 16 * NCH)

            @block.tensor
            def _(pe):
                pe.wait_ge(loaded, 16)
                for n in range(UNITS):
                    if n >= 4:
                        pe.wait_ge(squared, n - 3)
                    for c in range(KD):
                        last = nc.tensor.matmul(qps[n % 4][:], xT[:, c, (n // 2) * P:(n // 2 + 1) * P],
                                                wq[:, c, (n % 2) * CH:(n % 2 + 1) * CH],
                                                start=(c == 0), stop=(c == KD - 1))
                    last.then_inc(made, 1)
                pe.wait_ge(small, 3)
                for t in range(NT):
                    last = nc.tensor.transpose(tps[t // 4][:, (t % 4) * P:(t % 4 + 1) * P], rq[:, t, :],
                                               ident[:])
                    if t % 4 == 3:
                        last.then_inc(turned, 1)

            @block.scalar
            def _(act):
                for n in range(UNITS):
                    act.wait_ge(made, n + 1)
                    if n >= 2:
                        act.wait_ge(summed, n - 1)
                    nc.scalar.activation(sq[n % 2][:], qps[n % 4][:], ACT.Square).then_inc(squared, 1)
                act.wait_ge(summed, UNITS)
                nc.scalar.activation(rq[:], norm[:], ACT.Sqrt).then_inc(small, 1)
                for n in range(NCH):
                    act.wait_ge(turned, n + 1)
                    nc.scalar.activation(rqT[:, n * CH:(n + 1) * CH], tps[n][:], ACT.Copy).then_inc(taken, 1)

            @block.vector
            def _(dve):
                for n in range(UNITS):
                    dve.wait_ge(squared, n + 1)
                    nc.vector.reduce_sum(norm[:, n // 2, (n % 2) * HALF:(n % 2 + 1) * HALF], sq[n % 2][:],
                                         AX.X).then_inc(summed, 1)
                dve.wait_ge(small, 1)
                nc.vector.tensor_scalar(norm[:], rq[:], 1e-12, None, ALU.max).then_inc(small, 1)
                dve.wait_ge(small, 2)
                nc.vector.reciprocal(rq[:], norm[:]).then_inc(small, 1)


def null_values(k, name, acc, condT_dram, RN, WO, ident):
    nc = k.nc
    loaded, zeroed, placed, nv_made, nv_taken, turned, taken, made, added = (
        k.sem(f"{name}_{n}") for n in ("loaded", "zeroed", "placed", "nv_made", "nv_taken", "turned", "taken",
                                       "made", "added"))
    with ExitStack() as ctx:
        column = k.sb(name + "_column", [DH, 1], ctx=ctx)
        VN = k.sb(name + "_VN", [P, HEADS, HEADS], ctx=ctx)
        nv = k.sb(name + "_nvs", [P, D], ctx=ctx)
        RNT = k.sb(name + "_RNT", [P, TOK], ctx=ctx)
        nvps = k.ps(name + "_nvps", [HEADS, D], ctx)
        tps = [k.ps(f"{name}_t{i}", [HEADS, CH], ctx) for i in range(3)]
        out = [k.ps(f"{name}_out{i}", [P, 2, D], ctx) for i in range(4)]
        with nc.Block() as block:
            @block.sync
            def _(sp):
                sp.dma_start(column[:], condT_dram[:, 1:2], allow_slow_non_contiguous=True).then_inc(loaded, 16)

            @block.gpsimd
            def _(pool):
                nc.gpsimd.memset(VN[:], 0.0).then_inc(zeroed, 1)
                nc.gpsimd.memset(nv[:], 0.0).then_inc(zeroed, 1)
                nc.gpsimd.memset(RNT[:], 0.0).then_inc(zeroed, 1)

            @block.tensor
            def _(pe):
                def turn(n):
                    if n >= 3:
                        pe.wait_ge(taken, n - 2)
                    for t in range(4):
                        last = nc.tensor.transpose(tps[n % 3][:, t * P:(t + 1) * P], RN[:, 4 * n + t, :],
                                                   ident[:])
                    last.then_inc(turned, 1)

                turn(0)
                turn(1)
                pe.wait_ge(placed, 1)
                for h in range(HEADS):
                    last = nc.tensor.matmul(nvps[:], VN[:, h, :], WO[:, h * D:(h + 1) * D],
                                            start=(h == 0), stop=(h == HEADS - 1))
                last.then_inc(nv_made, 1)
                turn(2)
                turn(3)
                pe.wait_ge(nv_taken, 1)
                for t in range(NT):
                    if t % 4 == 0:
                        pe.wait_ge(taken, t // 4 + 1)
                    if t % 2 == 0 and t >= 8:
                        pe.wait_ge(added, t // 2 - 3)
                    last = nc.tensor.matmul(out[t // 2 % 4][:, t % 2, :], RNT[:, t * P:(t + 1) * P], nv[:],
                                            start=True, stop=True)
                    if t % 2:
                        last.then_inc(made, 1)

            @block.scalar
            def _(act):
                act.wait_ge(zeroed, 3)
                for n in range(NCH):
                    act.wait_ge(turned, n + 1)
                    nc.scalar.activation(RNT[0:HEADS, n * CH:(n + 1) * CH], tps[n % 3][:],
                                         ACT.Copy).then_inc(taken, 1)

            @block.vector
            def _(dve):
                dve.wait_ge(zeroed, 2)
                dve.wait_ge(loaded, 16)
                diagonal = VN[0:DH].rearrange("p a b -> p (a b)")[:, ::HEADS + 1]
                nc.vector.tensor_copy(diagonal, bc(column[:], [DH, HEADS])).then_inc(placed, 1)
                dve.wait_ge(nv_made, 1)
                nc.vector.tensor_copy(nv[0:HEADS, :], nvps[:]).then_inc(nv_taken, 1)
                for t in range(0, NT, 2):
                    dve.wait_ge(made, t // 2 + 1)
                    nc.vector.tensor_tensor(acc[:, t:t + 2, :], acc[:, t:t + 2, :], out[t // 2 % 4][:],
                                            ALU.add).then_inc(added, 1)


def keys_and_values(k, name, xT, wq_dram, wkv_dram, cond_dram, nb_dram, mask_dram, wo_dram, ident,
                    kA, kB, V, SNG, WO, rq, table, l2):
    nc = k.nc
    scale = 8.0 if l2 else DH ** -0.5
    NB = B * TB
    loaded, dve_done, act_done, mm, pool_done = (k.sem(f"{name}_{s}") for s in
                                                 ("loaded", "dve", "act", "mm", "pool"))
    with ExitStack() as ctx:
        cond = k.sb(name + "_cond", [P, 2, DH], ctx=ctx)
        nb = k.sb(name + "_nb", [P, HEADS], ctx=ctx)
        SN = k.sb(name + "_SN", [P, NT, HEADS], ctx=ctx)
        wq = k.sb(name + "_wq", [P, KD, HEADS * DH], ctx=ctx)
        wkv = k.sb(name + "_wkv", [P, KD, 2 * DH], ctx=ctx)
        prod = k.sb(name + "_prod", [P, KD, HEADS * DH], ctx=ctx)
        U = k.sb(name + "_U", [P, KD * HEADS], ctx=ctx)
        kn = k.sb(name + "_kn", [P, DH], ctx=ctx)
        qk = k.sb(name + "_qk", [P, 2, DH], ctx=ctx)
        sq = k.sb(name + "_sq", [P, NB, DH], ctx=ctx)
        n1 = k.sb(name + "_n1", [P, NB], ctx=ctx)
        n2 = k.sb(name + "_n2", [P, NB], ctx=ctx)
        kf = k.sb(name + "_kf", [P, NB, DH], ctx=ctx)
        sA = k.sb(name + "_sA", [P, NB, 2 * DH], F32R, ctx=ctx)
        sB = k.sb(name + "_sB", [P, NB, 2 * DH], F32R, ctx=ctx)
        mrow = k.sb(name + "_mrow", [P, B, S], mask_dram.dtype, ctx=ctx)
        kvps = [k.ps(f"{name}_kvps{i}", [P, 4, 2 * DH], ctx) for i in range(4)]
        snps = k.ps(name + "_snps", [P, NT, HEADS], ctx)
        tps = [k.ps(f"{name}_tps{i}", [P, 4, P], ctx) for i in range(2)]
        n_loads = 5 + 2 * bool(l2)

        xk = k.sb(name + "_xk", [P, KD, TOK], ctx=ctx) if table else xT
        turned_round, wo_loaded = k.sem(name + "_turned_round"), k.sem(name + "_wo_loaded")

        with nc.Block() as block:
            @block.sync
            def _(sp):
                sp.dma_start(cond[:], cond_dram.partition_broadcast(P)).then_inc(loaded, 16)
                sp.dma_start(nb[:], nb_dram.partition_broadcast(P)).then_inc(loaded, 16)
                sp.dma_start(wkv[:], wkv_dram).then_inc(loaded, 16)
                sp.dma_start(wq[:], wq_dram).then_inc(loaded, 16)
                sp.dma_start(mrow[DH:DH + 1, :, :], mask_dram[None, :, :]).then_inc(loaded, 16)
                sp.dma_start(WO[:], wo_dram).then_inc(wo_loaded, 16)
                if l2:
                    for n in range(2):
                        sp.dma_start(qk[:, n, :], l2[n].partition_broadcast(P)).then_inc(loaded, 16)
                sp.wait_ge(wo_loaded, 16)

            @block.gpsimd
            def _(pool):
                nc.gpsimd.memset(sB[:].bitcast(F32), 0.0).then_inc(pool_done, 1)

            @block.tensor
            def _(pe):
                pe.wait_ge(loaded, 16 * n_loads)
                if table:
                    pe.wait_ge(turned_round, KD * B)
                for n in range(NB):
                    for c in range(KD):
                        last = nc.tensor.matmul(kvps[n // 4][:, n % 4, :], xk[:, c, n * P:(n + 1) * P],
                                                wkv[:, c, :], start=(c == 0), stop=(c == KD - 1))
                last.then_inc(mm, 1)
                pe.wait_ge(pool_done, 2)
                for t in range(NT):
                    for c in range(KD):
                        last = nc.tensor.matmul(snps[:, t, :], xT[:, c, t * P:(t + 1) * P],
                                                U[:, c * HEADS:(c + 1) * HEADS],
                                                start=(c == 0), stop=(c == KD - 1))
                last.then_inc(mm, 1)
                pe.wait_ge(pool_done, 3)
                for g in range(2 * NB // 4):
                    src = (sA if g < NB // 4 else sB)[:].bitcast(F32)
                    if g >= 2:
                        pe.wait_ge(act_done, g - 1)
                    for j in range(4):
                        last = nc.tensor.transpose(tps[g % 2][:, j, :], src[:, (g % (NB // 4)) * 4 + j, :],
                                                   ident[:])
                    last.then_inc(mm, 1)

            squares, roots = k.sem(name + "_squares"), k.sem(name + "_roots")

            @block.scalar
            def _(act):
                if table:
                    for c in range(KD):
                        for b in range(B):
                            row = xT[:, c, :].rearrange("p (b s) -> p b s", b=B)[:, b, ::-1]
                            nc.scalar.activation(xk[:, c, b * S:(b + 1) * S], row,
                                                 ACT.Copy).then_inc(turned_round, 1)
                if l2:
                    act.wait_ge(mm, 1)
                    for i in range(4):
                        nc.scalar.activation(sq[:, 4 * i:4 * i + 4, :], kvps[i][:, :, 0:DH],
                                             ACT.Square).then_inc(squares, 1)
                    act.wait_ge(roots, 1)
                    nc.scalar.activation(n2[:, 0:1], n1[:, 0:1], ACT.Sqrt).then_inc(roots, 1)
                    act.wait_ge(roots, 3)
                    nc.scalar.activation(n2[:], n1[:], ACT.Sqrt).then_inc(roots, 1)
                for g in range(2 * NB // 4):
                    act.wait_ge(mm, g + 3)
                    dst = (kA if g < NB // 4 else kB)[:].rearrange("p b s -> p (b s)")
                    at = (g % (NB // 4)) * 4 * P
                    nc.scalar.activation(dst[:, at:at + 4 * P].rearrange("p (j n) -> p j n", j=4),
                                         tps[g % 2][:], ACT.Copy).then_inc(act_done, 1)

            @block.vector
            def _(dve):
                s = Steps(dve, dve_done)
                dve.wait_ge(loaded, 16 * n_loads)
                if l2:
                    s.then(nc.vector.tensor_tensor(kn[:], cond[:, 0, :], cond[:, 0, :], ALU.mult))
                    nc.vector.reduce_sum(n1[:, 0:1], kn[:], AX.X).then_inc(roots, 1)
                    dve.wait_ge(roots, 2)
                    s.then(nc.vector.tensor_scalar(n1[:, 0:1], n2[:, 0:1], 1e-12, None, ALU.max))
                    s.then(nc.vector.reciprocal(n2[:, 0:1], n1[:, 0:1]))
                    s.then(nc.vector.tensor_tensor(qk[:, 0, :], qk[:, 0, :], qk[:, 1, :], ALU.mult))
                    s.then(nc.vector.tensor_scalar(qk[:, 0, :], qk[:, 0, :], scale, None, ALU.mult))
                    s.then(nc.vector.tensor_scalar(kn[:], cond[:, 0, :], n2[:, 0:1], None, ALU.mult))
                    s.then(nc.vector.tensor_tensor(kn[:], kn[:], qk[:, 0, :], ALU.mult))
                else:
                    s.then(nc.vector.tensor_scalar(kn[:], cond[:, 0, :], scale, None, ALU.mult))
                knb = bc(kn[:, None, :], [P, KD * HEADS, DH])
                s.then(nc.vector.tensor_tensor(prod[:].rearrange("p c (h d) -> p (c h) d", d=DH),
                                               wq[:].rearrange("p c (h d) -> p (c h) d", d=DH),
                                               knb, ALU.mult))
                s.then(nc.vector.reduce_sum(U[:], prod[:].rearrange("p c (h d) -> p (c h) d", d=DH), AX.X))
                dve.wait_ge(pool_done, 1)
                dve.sem_inc(pool_done, 1)
                dve.wait_ge(mm, 1)
                if l2:
                    dve.wait_ge(squares, 4)
                    nc.vector.reduce_sum(n1[:], sq[:], AX.X).then_inc(roots, 1)
                    dve.wait_ge(roots, 4)
                    s.then(nc.vector.tensor_scalar(n1[:], n2[:], 1e-12, None, ALU.max))
                    s.then(nc.vector.reciprocal(n2[:], n1[:]))
                for i in range(4):
                    if l2:
                        s.did(nc.vector.tensor_tensor(kf[:, 4 * i:4 * i + 4, :], kvps[i][:, :, 0:DH],
                                                      bc(n2[:, 4 * i:4 * i + 4, None], [P, 4, DH]), ALU.mult))
                    else:
                        s.did(nc.vector.tensor_scalar(kf[:, 4 * i:4 * i + 4, :], kvps[i][:, :, 0:DH],
                                                      scale, None, ALU.mult))
                    s.did(nc.vector.tensor_copy(V[:, i // 2, 4 * (i % 2):4 * (i % 2) + 4, 0:DH],
                                                kvps[i][:, :, DH:2 * DH]))
                s.settle()
                if l2:
                    s.then(nc.vector.tensor_tensor(kf[:], kf[:], bc(qk[:, 0:1, :], [P, NB, DH]), ALU.mult))
                s.did(nc.vector.tensor_copy(sA[:, :, 0:DH], kf[:]))
                s.did(nc.vector.tensor_copy(sA[:, :, DH:2 * DH], kf[:]))
                for i in range(4):
                    v = V[:, i // 2, 4 * (i % 2):4 * (i % 2) + 4, :]
                    s.did(nc.vector.tensor_tensor(v[:, :, DH:2 * DH], kvps[i][:, :, DH:2 * DH],
                                                  v[:, :, 0:DH].bitcast(F32), ALU.subtract))
                s.settle()
                nc.vector.tensor_tensor(sB[:, :, 0:DH], kf[:], sA[:, :, 0:DH].bitcast(F32),
                                        ALU.subtract).then_inc(pool_done, 1)
                dve.wait_ge(mm, 2)
                nulls = snps[:]
                if l2:
                    s.then(nc.vector.tensor_tensor(SN[:], snps[:], rq[:], ALU.mult))
                    nulls = SN[:]
                nc.vector.scalar_tensor_tensor(out=SNG[:], in0=nulls, scalar=-1.0,
                                               in1=bc(nb[:, None, :], [P, NT, HEADS]),
                                               op0=ALU.mult, op1=ALU.subtract)
                dve.wait_ge(act_done, 2 * NB // 4)
                for b in range(B):
                    row = mrow[DH:DH + 1, b, ::-1] if table else mrow[DH:DH + 1, b, :]
                    nc.vector.tensor_scalar(kB[DH:DH + 1, b, :], row, 1.0, -FAR, ALU.subtract, ALU.mult)


class Turn:

    def __init__(self, g, ahead=0):
        self.g, self.ahead = g, ahead

    def count(self, per_turn, c):
        return per_turn * self.g + (per_turn * self.ahead + c)

    def part(self, width, offset=0, size=None):
        at = self.count(width, offset)
        size = size or width
        return slice(at, at + size) if isinstance(at, int) else bass.ds(at, size)

    def later(self, n=1):
        return Turn(self.g, self.ahead + n)


def in_turns(eng, early, late):
    early(Turn(0))
    with eng.Fori(0, NG - 1) as g:
        late(Turn(g), True)
        early(Turn(g, 1))
    late(Turn(NG - 1), False)


def heads_loop(k, name, xT, wq_dram, acc, ident, bias_dram, table, rq_dram, kA, kB, V, SNG, WO, RN):
    nc = k.nc
    norm_q = rq_dram is not None
    DUOS, UNITS = TB * B, TB * B * HG
    pairs = [(d // B + 2) // 2 for d in range(DUOS)]
    first = [sum(pairs[:d]) for d in range(DUOS)]
    BANKS = sum(pairs)
    QUERY_STEPS = {1: (0, 1), 3: (0, 3), 9: (1, 0), 11: (1, 2)}
    nth_of_chunk = {0: 0, 2: 1, 1: 2, 3: 3}

    def score_banks(d):
        return [(d, h, j) for h in range(HG) for j in range(1 if d // B + 1 <= CH // P else 2)]

    order = []
    for step in range(-2, DUOS - 2):
        order += score_banks(step + 2)
        if step in QUERY_STEPS:
            order.append(("queries",) + QUERY_STEPS[step])
    SLOTS = len(order)
    place = {what: 3 + n for n, what in enumerate(order)}
    LEAD = 2

    def rotation(count):
        which = [n % 3 for n in range(count)]
        if count % 3 == 1:
            which[-1] = 1
        ago = [next(m for m in range(1, 6) if which[n - m] == which[n]) for n in range(count)]
        return which, ago

    score_bank, score_ago = rotation(SLOTS)
    turn_bank, turn_ago = rotation(BANKS)

    def emptied_by(d, n):
        before = sum(len(score_banks(e % DUOS)) for e in range(d + 2)) + sum(e < d for e in QUERY_STEPS)
        if n < 0:
            return before
        done = len(score_banks((d + 2) % DUOS)) * (n + 1) // pairs[d]
        return before + done + (d in QUERY_STEPS and n == pairs[d] - 1)

    def turned_by(d, n):
        if n < 0 and d == 0:
            return 1
        if n < 0:
            return turned_by(d - 1, pairs[d - 1] - 1)
        return min(first[d] + n + 2, first[d] + pairs[d] + pairs[(d + 1) % DUOS] - 1) + 1

    def share(items, n, parts):
        return items[len(items) * n // parts:len(items) * (n + 1) // parts]

    names = ("filled", "emptied", "exp", "t", "hi", "lo", "pv", "o", "proj", "added", "head0", "dn",
             "pn", "tot", "rec", "rn", "sng", "q_lo", "q_hi", "q_b", "hidden", "wq", "acc0", "ones",
             "dve_mark", "pool_mark", "rq0", "rq1", "bias0", "bias1")
    (filled, emptied, exp_done, t_done, hi_done, lo_done, pv_done, o_taken, proj_done, added, head0_added,
     dn_done, pn_done, tot_done, rec_done, rn_done, sng_done, q_lo, q_hi, q_b, hidden, wq_loaded, acc_zero,
     ones_set, dve_mark, pool_mark, rq0, rq1, bias0, bias1) = (k.sem(f"{name}_{n}") for n in names)
    rq_loaded, bias_loaded = [rq0, rq1], [bias0, bias1]

    with ExitStack() as ctx:
        wq = k.sb(name + "_wqg", [P, KD, HG * DH], ctx=ctx)
        A = [k.sb(f"{name}_A{i}", [P, TOK], F32R, ctx=ctx) for i in range(HG)]
        Bq = [k.sb(f"{name}_B{i}", [P, TOK], F32R, ctx=ctx) for i in range(HG)]
        bt = [k.sb(f"{name}_bt{i}", [P, HG, S], ctx=ctx) for i in range(2)]
        pr = [k.sb(f"{name}_p{i}", [P, HG, S], ctx=ctx) for i in range(4)]
        ph = [k.sb(f"{name}_ph{i}", [P, 2, HG * P], F32R, ctx=ctx) for i in range(3)]
        pl = [k.sb(f"{name}_pl{i}", [P, 2, HG * P], F32R, ctx=ctx) for i in range(3)]
        sng = k.sb(name + "_sng", [P, NT, HG], ctx=ctx)
        NM = k.sb(name + "_NM", [P, UNITS], ctx=ctx)
        NMH = k.sb(name + "_NMH", [P, UNITS], ctx=ctx)
        RS = k.sb(name + "_RS", [P, UNITS], ctx=ctx)
        DN = k.sb(name + "_DN", [P, UNITS], ctx=ctx)
        PN = k.sb(name + "_PN", [P, UNITS], ctx=ctx)
        TT = k.sb(name + "_TT", [P, UNITS], ctx=ctx)
        RI = k.sb(name + "_RI", [P, UNITS], ctx=ctx)
        os_ = k.sb(name + "_os", [P, 2, HG * P], ctx=ctx)
        if norm_q:
            qn = k.sb(name + "_qn", [P, CH], ctx=ctx)
            rqb = [k.sb(f"{name}_rqb{i}", [P, CH], ctx=ctx) for i in range(2)]
        Sps = [k.ps(f"{name}_S{i}", [P, CH], ctx) for i in range(3)]
        Tps = [k.ps(f"{name}_T{i}", [P, 2, HG * P], ctx) for i in range(3)]
        Ops = k.ps(name + "_O", [P, HG * P], ctx)
        Mps = k.ps(name + "_M", [P, HG, D], ctx)

        def widths(i):
            W = (i + 1) * P
            return W, (1 if W <= CH else 2), max(2 * P, W) if W <= CH else W // 2

        def score_cols(i, j):
            W, chunks, n = widths(i)
            lo = S - max(W, 2 * P) if table else 0
            return slice(lo + j * n, lo + (j + 1) * n)

        def wait(eng, sem, value):
            if not isinstance(value, int) or value > 0:
                eng.wait_ge(sem, value)

        def neighbour(T, d, by, more=True):
            if d + by < 0:
                return None if isinstance(T.g, int) and T.g + T.ahead == 0 else (T.later(-1), d + by + DUOS)
            if d + by < DUOS:
                return T, d + by
            return (T.later(), d + by - DUOS) if more else None

        def query_place(T, ahead, chunk):
            return T.count(SLOTS, place[("queries", ahead, chunk)])

        def query_bank(T, ahead, chunk):
            at = place[("queries", ahead, chunk)]
            return score_bank[at - 3], T.count(SLOTS, at)

        def unit(d, h):
            return 4 * (d // B) + HG * (d % B) + h

        with nc.Block() as block:
            @block.sync
            def _(sp):
                def load_bias(T, i):
                    before = neighbour(T, B * i + 1, -2 * B)
                    if before:
                        sp.wait_ge(emptied, before[0].count(SLOTS, place[score_banks(before[1])[-1]]))
                    W = (i + 1) * P
                    src = (bias_dram[T.part(1), :, :, 0:W].rearrange("o p h s -> (o p) h s") if table
                           else bias_dram[T.part(HG), i * P:(i + 1) * P, 0:W].rearrange("h p s -> p h s"))
                    sp.dma_start(bt[i % 2][:, :, 0:W], src).then_inc(bias_loaded[i % 2], 16)

                def load_norms(T, chunk, buf, freed):
                    if norm_q:
                        if freed is not None:
                            sp.wait_ge(emptied, freed)
                        for h in range(HG):
                            sp.dma_start(rqb[buf][h * DH:(h + 1) * DH, :],
                                         rq_dram[T.part(HG, h, 1), chunk * CH:(chunk + 1) * CH]
                                         .broadcast_to([DH, CH])).then_inc(rq_loaded[buf], 16)

                def early(T):
                    first_turn = isinstance(T.g, int)
                    load_norms(T, 1, 0, 1 if first_turn else query_place(T.later(-1), 1, 0))
                    load_norms(T, 3, 1, 2 if first_turn else query_place(T.later(-1), 1, 2))
                    for i in range(2, 6):
                        load_bias(T, i)

                def load_queries_weights(T):
                    sp.dma_start(wq[:], wq_dram[:, :, T.part(HG * DH)]).then_inc(wq_loaded, 16)

                def late(T, more):
                    if more:
                        sp.wait_ge(filled, query_place(T, 0, 3))
                        load_queries_weights(T.later())
                        load_norms(T.later(), 0, 0, query_place(T, 0, 1))
                        load_norms(T.later(), 2, 1, query_place(T, 0, 3))
                    load_bias(T, 6)
                    load_bias(T, 7)
                    if more:
                        load_bias(T.later(), 0)
                        load_bias(T.later(), 1)

                load_queries_weights(Turn(0))
                load_norms(Turn(0), 0, 0, None)
                load_norms(Turn(0), 2, 1, None)
                load_bias(Turn(0), 0)
                load_bias(Turn(0), 1)
                in_turns(sp, early, late)

            @block.gpsimd
            def _(pool):
                for h in range(HG):
                    nc.gpsimd.memset(Bq[h][DH:P, :].bitcast(F32), 0.0).then_inc(ones_set, 1)
                pool.wait_ge(ones_set, 2)
                for h in range(HG):
                    nc.gpsimd.memset(Bq[h][DH:DH + 1, :].bitcast(F32), 1.0).then_inc(ones_set, 1)
                pool.wait_ge(ones_set, 4)
                far = pool.to_reg(FAR)

                def hide_later_keys(T, i):
                    if not table:
                        wait_apart(pool, bias_loaded[i % 2], T.count(16 * (TB // 2), 16 * (i // 2 + 1)),
                                   pool_mark)
                        d = bt[i % 2][:, :, i * P:(i + 1) * P]
                        nc.gpsimd.affine_select(out=d, in_=d, compare_op=ALU.is_ge, fill=far, base=0,
                                                pattern=[[0, HG], [-1, P]],
                                                channel_multiplier=1).then_inc(hidden, 1)

                def second_operand(T, chunk, nth):
                    for h in range(HG):
                        cols = slice(chunk * CH, (chunk + 1) * CH)
                        wait_apart(pool, q_hi, T.count(4 * HG, HG * nth + h + 1), pool_mark)
                        nc.gpsimd.tensor_copy(Bq[h][0:DH, cols],
                                              A[h][0:DH, cols].bitcast(F32)).then_inc(q_b, 1)

                def early(T):
                    second_operand(T, 1, 2)
                    hide_later_keys(T, 2)
                    hide_later_keys(T, 3)
                    second_operand(T, 3, 3)
                    hide_later_keys(T, 4)
                    hide_later_keys(T, 5)

                def late(T, more):
                    hide_later_keys(T, 6)
                    if more:
                        second_operand(T.later(), 0, 0)
                    hide_later_keys(T, 7)
                    if more:
                        second_operand(T.later(), 2, 1)
                        hide_later_keys(T.later(), 0)
                        hide_later_keys(T.later(), 1)

                second_operand(Turn(0), 0, 0)
                second_operand(Turn(0), 2, 1)
                hide_later_keys(Turn(0), 0)
                hide_later_keys(Turn(0), 1)
                in_turns(pool, early, late)

            @block.tensor
            def _(pe):
                def queries(T, chunk, bank, freed):
                    if chunk == 0:
                        pe.wait_ge(wq_loaded, T.count(16, 16))
                    wait(pe, emptied, freed)
                    for c in range(KD):
                        last = nc.tensor.matmul(Sps[bank][:], wq[:, c, :],
                                                xT[:, c, chunk * CH:(chunk + 1) * CH],
                                                start=(c == 0), stop=(c == KD - 1))
                    last.then_inc(filled, 1)

                def scores(T, x):
                    d, h, j = order[x]
                    i, b = d // B, d % B
                    W, chunks, n = widths(i)
                    t = b * TB + i
                    if d in (0, TB) and h == 0 and j == 0:
                        nth = 1 if d == 0 else 3
                        pe.wait_ge(q_b, T.count(4 * HG, HG * (nth + 1)))
                        if norm_q:
                            pe.wait_ge(q_lo, T.count(4 * HG, HG * (nth + 1)))
                    wait(pe, emptied, T.count(SLOTS, 3 + x - score_ago[x]))
                    out = Sps[score_bank[x]][:, 0:n]
                    nc.tensor.matmul(out, A[h][:, t * P:(t + 1) * P], kA[:, b, score_cols(i, j)],
                                     start=True, stop=False)
                    last = nc.tensor.matmul(out, Bq[h][:, t * P:(t + 1) * P], kB[:, b, score_cols(i, j)],
                                            start=False, stop=True)
                    last.then_inc(filled, 1)

                def fill(T, x, more=True):
                    if x >= SLOTS:
                        if more:
                            fill(T.later(), x - SLOTS)
                    elif order[x][0] != "queries":
                        scores(T, x)
                    elif order[x][1] == 0 or more:
                        queries(T.later(order[x][1]), order[x][2], score_bank[x],
                                T.count(SLOTS, 3 + x - score_ago[x]))
                    else:
                        pe.wait_ge(filled, T.count(SLOTS, 2 + x))
                        pe.sem_inc(filled, 1)

                def turn(T, at, more=True):
                    if at >= BANKS:
                        if more:
                            turn(T.later(), at - BANKS)
                        return
                    d = max(e for e in range(DUOS) if first[e] <= at)
                    i, n = d // B, at - first[d]
                    if n == 0:
                        pe.wait_ge(exp_done, T.count(UNITS, HG * (d + 1)))
                    wait(pe, lo_done, T.count(BANKS, at + 1 - turn_ago[at]))
                    for jj in range(2):
                        j = 2 * n + jj
                        if j > i:
                            break
                        for h in range(HG):
                            last = nc.tensor.transpose(Tps[turn_bank[at]][:, jj, h * P:(h + 1) * P],
                                                       pr[d % 4][:, h, j * P:(j + 1) * P], ident[:])
                    last.then_inc(t_done, 1)

                def values(T, d, n):
                    i, b = d // B, d % B
                    at = first[d] + n
                    buf = turn_bank[at]
                    if n == 0:
                        wait(pe, o_taken, T.count(DUOS, d))
                    pe.wait_ge(lo_done, T.count(BANKS, at + 1))
                    for jj in range(2):
                        j = 2 * n + jj
                        if j > i:
                            break
                        vj = V[:, b, (TB - 1 - i + j) if table else j, :]
                        nc.tensor.matmul(Ops[:], vj, ph[buf][:, jj, :], start=(j == 0), stop=False)
                        last = nc.tensor.matmul(Ops[:], vj, pl[buf][:, jj, :], start=False, stop=(j == i))
                    last.then_inc(pv_done, 1)

                def project(T, d):
                    pe.wait_ge(o_taken, T.count(DUOS, d + 1))
                    wait(pe, added, T.count(DUOS, d))
                    for h in range(HG):
                        last = nc.tensor.matmul(Mps[:, h, :], os_[:, d % 2, h * P:(h + 1) * P],
                                                WO[:, T.part(HG * D, h * D, D)], start=True, stop=True)
                    last.then_inc(proj_done, 1)

                def step(T, d, more=True):
                    before = neighbour(T, d, -1)
                    for n in range(pairs[d]):
                        for x in range(emptied_by(d, n - 1) + LEAD, emptied_by(d, n) + LEAD):
                            fill(T, x, more)
                        for at in range(turned_by(d, n - 1), turned_by(d, n)):
                            turn(T, at, more)
                        values(T, d, n)
                        if n == 0 and before:
                            project(*before)

                def early(T):
                    for d in range(DUOS // 2):
                        step(T, d)

                def late(T, more):
                    for d in range(DUOS // 2, DUOS):
                        step(T, d, more)

                queries(Turn(0), 0, 2, 0)
                queries(Turn(0), 2, 1, 0)
                pe.wait_ge(ones_set, 4)
                pe.wait_ge(emptied, 2)
                for x in range(emptied_by(0, -1) + LEAD):
                    fill(Turn(0), x)
                turn(Turn(0), 0)
                in_turns(pe, early, late)
                project(Turn(NG - 1), DUOS - 1)

            @block.scalar
            def _(act):
                def high_queries(T, chunk, bank, at):
                    cols = slice(chunk * CH, (chunk + 1) * CH)
                    if norm_q:
                        act.wait_ge(emptied, at)
                    else:
                        act.wait_ge(filled, at)
                    src = qn if norm_q else Sps[bank]
                    for h in range(HG):
                        nc.scalar.activation(A[h][0:DH, cols], src[h * DH:(h + 1) * DH, :],
                                             ACT.Copy).then_inc(q_hi, 1)

                def exponentials(T, d, h):
                    act.wait_ge(emptied, T.count(SLOTS, place[[x for x in score_banks(d) if x[1] == h][-1]]))
                    u = unit(d, h)
                    p = pr[d % 4][:, h, 0:(d // B + 1) * P]
                    nc.scalar.activation(p, p, ACT.Exp, bias=NM[:, u:u + 1], scale=-1.0,
                                         accum_out=RS[:, u:u + 1]).then_inc(exp_done, 1)

                def high_part(T, d, n):
                    at = first[d] + n
                    js = min(2, d // B + 1 - 2 * n)
                    wait(act, pv_done, T.count(BANKS, at + 1 - turn_ago[at]))
                    act.wait_ge(t_done, T.count(BANKS, at + 1))
                    buf = turn_bank[at]
                    nc.scalar.activation(ph[buf][:, 0:js, :], Tps[buf][:, 0:js, :],
                                         ACT.Copy).then_inc(hi_done, 1)

                def null_exponential(T, i):
                    act.wait_ge(dn_done, T.count(TB, i + 1))
                    nc.scalar.activation(PN[:, 4 * i:4 * i + 4], DN[:, 4 * i:4 * i + 4],
                                         ACT.Exp).then_inc(pn_done, 1)

                def take_outputs(T, d):
                    wait(act, proj_done, T.count(DUOS, d - 1))
                    act.wait_ge(pv_done, T.count(BANKS, first[d] + pairs[d]))
                    nc.scalar.activation(os_[:, d % 2, :], Ops[:], ACT.Copy).then_inc(o_taken, 1)

                def step(T, d, more=True):
                    ahead, before = neighbour(T, d, 2, more), neighbour(T, d, -1)
                    for n in range(pairs[d]):
                        high_part(T, d, n)
                        if n == 0 and before:
                            take_outputs(*before)
                        if n == 0 and d % B == 0:
                            null_exponential(T, d // B)
                        if ahead:
                            for h in share(range(HG), n, pairs[d]):
                                exponentials(*ahead, h)
                    if d in QUERY_STEPS:
                        turns, chunk = QUERY_STEPS[d]
                        if turns == 0 or more:
                            high_queries(T.later(turns), chunk, *query_bank(T, turns, chunk))

                def early(T):
                    for d in range(DUOS // 2):
                        step(T, d)

                def late(T, more):
                    for d in range(DUOS // 2, DUOS):
                        step(T, d, more)

                high_queries(Turn(0), 0, 2, 1)
                high_queries(Turn(0), 2, 1, 2)
                for d in range(2):
                    for h in range(HG):
                        exponentials(Turn(0), d, h)
                in_turns(act, early, late)
                take_outputs(Turn(NG - 1), DUOS - 1)

            @block.vector
            def _(dve):
                def queries_of(T, chunk, bank, at):
                    slot, nth = Sps[bank], nth_of_chunk[chunk]
                    cols = slice(chunk * CH, (chunk + 1) * CH)
                    if norm_q:
                        wait(dve, q_lo, T.count(4 * HG, HG * nth))
                        dve.wait_ge(rq_loaded[nth % 2], T.count(4 * 16, 2 * 16 * (nth // 2 + 1)))
                        dve.wait_ge(filled, at)
                        nc.vector.tensor_tensor(qn[:], slot[:], rqb[nth % 2][:], ALU.mult).then_inc(emptied, 1)
                    else:
                        for h in range(HG):
                            dve.wait_ge(q_hi, T.count(4 * HG, HG * nth + h + 1))
                            last = nc.vector.tensor_tensor(A[h][DH:P, cols], slot[h * DH:(h + 1) * DH, :],
                                                           A[h][0:DH, cols].bitcast(F32), ALU.subtract)
                            last.then_inc(emptied if h == HG - 1 else q_lo, 1)

                def low_queries(T, chunk):
                    cols = slice(chunk * CH, (chunk + 1) * CH)
                    for h in range(HG):
                        dve.wait_ge(q_hi, T.count(4 * HG, HG * nth_of_chunk[chunk] + h + 1))
                        nc.vector.tensor_tensor(A[h][DH:P, cols], qn[h * DH:(h + 1) * DH, :],
                                                A[h][0:DH, cols].bitcast(F32), ALU.subtract).then_inc(q_lo, 1)

                def null_scores(T):
                    nc.vector.tensor_copy(sng[:], SNG[:, :, T.part(HG)]).then_inc(sng_done, 1)

                def add_bias_and_max(T, d, h, j):
                    i, b = d // B, d % B
                    W, chunks, n = widths(i)
                    at = place[(d, h, j)]
                    if d == 0 and h == 0:
                        dve.wait_ge(sng_done, T.count(1, 1))
                    if h == 0 and j == 0:
                        before = neighbour(T, d, -4)
                        if before:
                            dve.wait_ge(t_done, before[0].count(BANKS, first[before[1]] + pairs[before[1]]))
                    if h == 0 and b == 0 and j == 0:
                        if table:
                            dve.wait_ge(bias_loaded[i % 2], T.count(16 * (TB // 2), 16 * (i // 2 + 1)))
                        else:
                            dve.wait_ge(hidden, T.count(TB, i + 1))
                    if j:
                        dve.wait_ge(emptied, T.count(SLOTS, at - 1))
                    wait_apart(dve, filled, T.count(SLOTS, at), dve_mark)
                    off = P if (table and i == 0) else 0
                    nn = min(n, W)
                    u = unit(d, h)
                    cols = slice(j * nn, (j + 1) * nn)
                    nc.vector.tensor_tensor_reduce(
                        out=pr[d % 4][:, h, cols], in0=Sps[score_bank[at - 3]][:, off:off + nn],
                        in1=bt[i % 2][:, h, cols], scale=-1.0,
                        scalar=NMH[:, u:u + 1] if j else sng[:, b * TB + i, h:h + 1],
                        op0=ALU.add, op1=ALU.min,
                        accum_out=(NM if j == chunks - 1 else NMH)[:, u:u + 1]).then_inc(emptied, 1)

                def low_part(T, d, n):
                    at = first[d] + n
                    js = min(2, d // B + 1 - 2 * n)
                    dve.wait_ge(hi_done, T.count(BANKS, at + 1))
                    buf = turn_bank[at]
                    nc.vector.tensor_tensor(pl[buf][:, 0:js, :], Tps[buf][:, 0:js, :],
                                            ph[buf][:, 0:js, :].bitcast(F32),
                                            ALU.subtract).then_inc(lo_done, 1)

                def null_difference(T, i):
                    dve.wait_ge(emptied, T.count(SLOTS, place[score_banks(B * i + 1)[-1]]))
                    nc.vector.tensor_tensor(
                        DN[:, 4 * i:4 * i + 4].rearrange("p (b h) -> p b h", b=B),
                        NM[:, 4 * i:4 * i + 4].rearrange("p (b h) -> p b h", b=B),
                        sng[:].rearrange("p (b t) h -> p b t h", b=B)[:, :, i, :],
                        ALU.subtract).then_inc(dn_done, 1)

                def totals(T, i):
                    c = slice(4 * i, 4 * i + 4)
                    dve.wait_ge(exp_done, T.count(UNITS, 4 * (i + 1)))
                    dve.wait_ge(pn_done, T.count(TB, i + 1))
                    nc.vector.tensor_tensor(TT[:, c], RS[:, c], PN[:, c], ALU.add).then_inc(tot_done, 1)

                def reciprocals(T, i):
                    c = slice(4 * i, 4 * i + 4)
                    dve.wait_ge(tot_done, T.count(TB, i + 1))
                    nc.vector.reciprocal(RI[:, c], TT[:, c]).then_inc(rec_done, 1)

                def null_weights(T):
                    dve.wait_ge(rec_done, T.count(TB, TB))
                    nc.vector.tensor_tensor(
                        RN[:, :, T.part(HG)].rearrange("p (b t) h -> p t b h", b=B),
                        PN[:].rearrange("p (t b h) -> p t b h", b=B, h=HG),
                        RI[:].rearrange("p (t b h) -> p t b h", b=B, h=HG), ALU.mult).then_inc(rn_done, 1)

                def accumulate(T, d):
                    i, b = d // B, d % B
                    dve.wait_ge(rec_done, T.count(TB, i + 1))
                    dve.wait_ge(proj_done, T.count(DUOS, d + 1))
                    rows = acc[:, b * TB + i, :]
                    for h in range(HG):
                        if h:
                            dve.wait_ge(head0_added, T.count(DUOS, d + 1))
                        u = unit(d, h)
                        nc.vector.scalar_tensor_tensor(out=rows, in0=Mps[:, h, :], scalar=RI[:, u:u + 1],
                                                       in1=rows, op0=ALU.mult,
                                                       op1=ALU.add).then_inc(added if h else head0_added, 1)

                def step(T, d, more=True):
                    ahead, before = neighbour(T, d, 2, more), neighbour(T, d, -1)
                    if d == DUOS - 2 and ahead:
                        null_scores(ahead[0])
                    if norm_q and d - 1 in QUERY_STEPS:
                        turns, chunk = QUERY_STEPS[d - 1]
                        if turns == 0 or more:
                            low_queries(T.later(turns), chunk)
                    for n in range(pairs[d]):
                        if ahead:
                            for bank in share(score_banks(ahead[1]), n, pairs[d]):
                                add_bias_and_max(ahead[0], *bank)
                        low_part(T, d, n)
                        if n == 0 and d % B == 0:
                            totals(T, d // B)
                    if d in QUERY_STEPS:
                        turns, chunk = QUERY_STEPS[d]
                        if turns == 0 or more:
                            queries_of(T.later(turns), chunk, *query_bank(T, turns, chunk))
                        else:
                            dve.wait_ge(emptied, query_place(T, turns, chunk) - 1)
                            dve.sem_inc(emptied, 1)
                    if d % B == 0:
                        reciprocals(T, d // B)
                    if d == DUOS - 1:
                        null_weights(T)
                    if d % B and ahead:
                        null_difference(ahead[0], ahead[1] // B)
                    if before:
                        accumulate(*before)

                def early(T):
                    for d in range(DUOS // 2):
                        step(T, d)

                def late(T, more):
                    for d in range(DUOS // 2, DUOS):
                        step(T, d, more)

                nc.vector.memset(acc[:], 0.0).then_inc(acc_zero, 1)
                dve.wait_ge(acc_zero, 1)
                for chunk, bank, at in ((0, 2, 1), (2, 1, 2)):
                    queries_of(Turn(0), chunk, bank, at)
                    if norm_q:
                        low_queries(Turn(0), chunk)
                null_scores(Turn(0))
                for d in range(2):
                    for bank in score_banks(d):
                        add_bias_and_max(Turn(0), *bank)
                null_difference(Turn(0), 0)
                in_turns(dve, early, late)
                accumulate(Turn(NG - 1), DUOS - 1)


def load_constants(k, ident, X, x_dram, upper):
    nc = k.nc
    made, loaded = k.sem("const_made"), k.sem("const_loaded")
    with nc.Block() as block:
        @block.sync
        def _(sp):
            sp.dma_start(X[:], x_dram.rearrange("b (i p) d -> p (b i) d", p=P)).then_inc(loaded, 16)
            sp.wait_ge(loaded, 16)

        @block.gpsimd
        def _(pool):
            nc.gpsimd.memset(ident[:], 0.0).then_inc(made, 1)
            nc.gpsimd.memset(upper[:], 1.0).then_inc(made, 1)
            pool.wait_ge(made, 2)
            nc.gpsimd.affine_select(out=ident[:], in_=ident[:], compare_op=ALU.not_equal, fill=1.0,
                                    base=0, pattern=[[-1, P]], channel_multiplier=1)
            nc.gpsimd.affine_select(out=upper[:], in_=upper[:], compare_op=ALU.is_ge, fill=0.0,
                                    base=0, pattern=[[1, P]], channel_multiplier=-1)


def load_vector(k, name, ctx, dram, block_sems):
    t = k.sb(name, [P, dram.shape[0]], ctx=ctx)
    return t


def load_broadcast(k, name, pairs):
    nc = k.nc
    loaded = k.sem(name + "_loaded")
    with nc.Block() as block:
        @block.sync
        def _(sp):
            for tile, dram in pairs:
                sp.dma_start(tile[:], dram.partition_broadcast(P)).then_inc(loaded, 16)
            sp.wait_ge(loaded, 16 * len(pairs))


def fill(k, name, tile, value):
    nc = k.nc
    with nc.Block() as block:
        @block.gpsimd
        def _(pool):
            nc.gpsimd.memset(tile, value)


def store_rows(k, name, src, out_dram):
    nc = k.nc
    stored = k.sem(name)
    with nc.Block() as block:
        @block.sync
        def _(sp):
            sp.dma_start(out_dram.rearrange("b (i p) d -> p (b i) d", p=P), src[:]).then_inc(stored, 16)
            sp.wait_ge(stored, 16)


def layer0(k, a, X, Y, XT, ident):
    with ExitStack() as ctx:
        shares = k.sb("l0_shares", [P, NT, 10], ctx=ctx)
        fill(k, "l0_ones", shares[:, :, 8:10], 1.0)
        to_feature_major(k, "l0_t", X, XT, ident)
        route(k, "l0_r", XT, a["l0_router"], 8, 2, shares, extra=(a["condT"], a["l0_router_cond"]),
              scale=0.5, soft="all")
        gated_experts(k, "l0_e", XT, a["l0_experts"], 10, P, Y, shares, "leaky")
    with ExitStack() as ctx:
        picked = k.sb("l0_picked", [P, NT, 8], ctx=ctx)
        Z = k.sb("l0_z", [P, NT, D], ctx=ctx)
        gamma, beta = k.sb("l0_gamma", [P, D], ctx=ctx), k.sb("l0_beta", [P, D], ctx=ctx)
        load_broadcast(k, "l0_v", [(gamma, a["l0_ln_gamma"]), (beta, a["l0_ln_beta"])])
        to_feature_major(k, "l0_t2", Y, XT, ident)
        route(k, "l0_r2", XT, a["l0_ffn_router"], 4, 1, picked)
        with ExitStack() as inner:
            picked_ffn(k, "l0_f", Y, picked, a["l0_w1"], a["l0_b1"], a["l0_wo"], a["l0_bo"], Z, ident, 4)
        normalise(k, "l0_ln", Z, X, gamma, 1e-12, beta=beta, add_to=X)


def window_views(table_dram):
    return bass.AP(tensor=table_dram.tensor, offset=0,
                   ap=[[HG * TABLE, NG], [1, P], [TABLE, HG], [1, S]])


def layer1_attention(k, a, X, Y, XT, ident, table_dram, rq_dram):
    position_table(k, a, table_dram, ident)
    with ExitStack() as ctx:
        g_in = k.sb("l1_gin", [P, D], ctx=ctx)
        load_broadcast(k, "l1_v", [(g_in, a["l1_g_norm"])])
        normalise(k, "l1_n", X, Y, g_in, 1e-5)
        to_feature_major(k, "l1_t", Y, XT, ident)
    attention(k, "l1_a", XT, (a["l1_wq"], a["l1_wkv"], a["l1_wout"], a["l1_null_attn_bias"]), a["cond"],
              a["condT"], a["mask1"], Y, ident, window_views(table_dram), table=True,
              l2=(a["l1_q_scale"], a["l1_k_scale"]), rq_dram=rq_dram)
    with ExitStack() as ctx:
        g_out = k.sb("l1_gout", [P, D], ctx=ctx)
        load_broadcast(k, "l1_v2", [(g_out, a["l1_g_out"])])
        normalise(k, "l1_no", Y, Y, g_out, 1e-5)


def biased_attention(k, a, layer, X, Y, XT, ident):
    n = f"l{layer}"
    with ExitStack() as ctx:
        g_in = k.sb(n + "_gin", [P, D], ctx=ctx)
        load_broadcast(k, n + "_v", [(g_in, a[n + "_g_in"])])
        normalise(k, n + "_n", X, Y, g_in, 1e-5)
        to_feature_major(k, n + "_t", Y, XT, ident)
    attention(k, n + "_a", XT, (a[n + "_wq"], a[n + "_wkv"], a[n + "_wout"], a[n + "_null_attn_bias"]),
              a["cond"], a["condT"], a["mask0"], Y, ident, a["bias"])
    with ExitStack() as ctx:
        g_out = k.sb(n + "_gout", [P, D], ctx=ctx)
        load_broadcast(k, n + "_v2", [(g_out, a[n + "_g_out"])])
        normalise(k, n + "_no", Y, Y, g_out, 1e-5)


def layer1_ffn(k, a, X, Y, XT, ident):
    with ExitStack() as ctx:
        picked = k.sb("l1_picked", [P, NT, 8], ctx=ctx)
        to_feature_major(k, "l1_t2", Y, XT, ident)
        route(k, "l1_r", XT, a["l1_router"], 8, 1, picked, bias=a["l1_router_b"])
        lora_ffn(k, "l1_f", XT, picked, (a["l1_wi"], a["l1_wi_b"], a["l1_wo"], a["l1_wo_b"],
                                         a["l1_lora_a"], a["l1_lora_b"]), X, ident)


def layer2_ffn(k, a, X, Y, XT, ident):
    with ExitStack() as ctx:
        scale = k.sb("l2_scale", [P, 1], ctx=ctx)
        round_to_e4m3(k, "l2_q", Y, Y, a["l2_input_scale"], scale)
        to_feature_major(k, "l2_t2", Y, XT, ident)
        linear(k, "l2_f", XT, a["l2_w"], a["l2_weight_scale"], a["l2_bias"], X)


def layer3_ffn(k, a, X, Y, XT, ident, upper, rows_dram, out_dram):
    with ExitStack() as ctx:
        shares = k.sb("l3_shares", [P, NT, 8], ctx=ctx)
        chosen = k.sb("l3_chosen", [P, NT, 8], ctx=ctx)
        rank = k.sb("l3_rank", [P, NT, 8], ctx=ctx)
        to_feature_major(k, "l3_t2", Y, XT, ident)
        route(k, "l3_r", XT, a["l3_router"], 8, 2, shares, bias=a["l3_router_b"], soft="chosen",
              ones=chosen)
        places(k, "l3_p", chosen, rank, upper)
        drop_over_capacity(k, "l3_d", shares, rank)
        sent_experts(k, "l3_e", Y, shares, chosen, rank, a["l3_experts"], 4 * P, 8, X, rows_dram, out_dram,
                     ident)


def four_layers(nc, a, out):
    with ExitStack() as ctx:
        k = Kit(nc, ctx)
        X = k.sb("X", [P, NT, D])
        Y = k.sb("Y", [P, NT, D])
        XT = k.sb("XT", [P, KD, TOK])
        ident, upper = k.sb("ident", [P, P]), k.sb("upper", [P, P])
        table_dram = nc.dram_tensor("position_table", [HEADS, TABLE], F32, kind="Internal").ap()
        rq_dram = nc.dram_tensor("query_norms", [HEADS, TOK], F32, kind="Internal").ap()
        rows_dram, out_dram = (nc.dram_tensor(n, [8 * CAPACITY, D], F32, kind="Internal").ap()
                               for n in ("sent_rows", "expert_rows"))
        load_constants(k, ident, X, a["x"], upper)
        with k.stage():
            layer0(k, a, X, Y, XT, ident)
        with k.stage():
            layer1_attention(k, a, X, Y, XT, ident, table_dram, rq_dram)
        with k.stage():
            layer1_ffn(k, a, X, Y, XT, ident)
        with k.stage():
            biased_attention(k, a, 2, X, Y, XT, ident)
        with k.stage():
            layer2_ffn(k, a, X, Y, XT, ident)
        with k.stage():
            biased_attention(k, a, 3, X, Y, XT, ident)
        with k.stage():
            layer3_ffn(k, a, X, Y, XT, ident, upper, rows_dram, out_dram)
        store_rows(k, "stored", X, out)


def lay_out(inputs):
    import numpy as np

    def rows(w):
        w = np.asarray(w)
        return np.ascontiguousarray(w.reshape(w.shape[0] // 128, 128, -1).transpose(1, 0, 2))

    g = {n: np.asarray(a) for n, a in inputs.items()}

    def experts(gate, up, down):
        out = []
        for a, b, c in zip(gate, up, down):
            out.append(np.concatenate([rows(x).reshape(128, -1) for x in (a, b, c)], axis=1))
        return np.ascontiguousarray(np.stack(out))

    def halves(w):
        return [w[:, :w.shape[1] // 2], w[:, w.shape[1] // 2:]]

    a = {"x": g["x"], "cond": g["cond_64"], "condT": g["cond_64"].T, "bias": g["fside_16xSxS_0"],
         "mask1": g["mask_BxS_bf1"], "mask0": g["mask_BxS_bk0"]}
    down = g["L0_cond_sw_down"]
    a["l0_router"] = rows(g["L0_cond_wt"].T)
    a["l0_router_cond"] = g["L0_cond_wg"].T
    a["l0_experts"] = experts(list(g["L0_cond_w_gate"]) + halves(g["L0_cond_sw_gate"]),
                              list(g["L0_cond_w_up"]) + halves(g["L0_cond_sw_up"]),
                              list(g["L0_cond_w_down"]) + [down[:128], down[128:]])
    a["l0_ffn_router"] = rows(g["L0_ffn_W_router"])
    a["l0_w1"] = g["L0_ffn_W1"].reshape(4, 2, 128, 1024).transpose(2, 0, 1, 3)
    a["l0_b1"] = g["L0_ffn_b1"]
    a["l0_wo"] = rows(g["L0_ffn_Wo"])
    for n in ("bo", "ln_gamma", "ln_beta"):
        a["l0_" + n] = g["L0_ffn_" + n]
    for n in ("g_norm", "q_scale", "k_scale", "null_attn_bias", "b0", "g0", "b1", "g1", "b2", "g_out"):
        a["l1_" + n] = g["L1_cond_" + n]
    a["l1_w0"] = g["L1_cond_w0"][0]
    a["l1_w1"] = rows(g["L1_cond_w1"])
    a["l1_w2"] = rows(g["L1_cond_w2"])
    for layer, wo in ((1, "L1_cond_Wout"), (2, "L2_cond_Wo"), (3, "L3_cond_Wo")):
        a[f"l{layer}_wq"] = rows(g[f"L{layer}_cond_Wq"])
        a[f"l{layer}_wkv"] = rows(g[f"L{layer}_cond_Wkv"])
        heads = g[wo].reshape(16, 64, 256).transpose(1, 0, 2).reshape(64, -1)
        a[f"l{layer}_wout"] = np.concatenate([heads, heads])
    a["l1_router"] = rows(g["L1_ffn_gate_W"].T)
    a["l1_router_b"] = g["L1_ffn_gate_b"]
    a["l1_wi"] = rows(g["L1_ffn_wi_W"].T)
    a["l1_wi_b"] = g["L1_ffn_wi_b"].reshape(8, 128).T
    a["l1_wo"] = rows(g["L1_ffn_wo_W"].T)
    a["l1_wo_b"] = g["L1_ffn_wo_b"]
    a["l1_lora_a"] = rows(g["L1_ffn_lora_A"].reshape(32, 256).T)
    a["l1_lora_b"] = g["L1_ffn_lora_B"].transpose(0, 2, 1).reshape(32, 1024)
    for layer in (2, 3):
        for n in ("g_in", "null_attn_bias", "g_out"):
            a[f"l{layer}_{n}"] = g[f"L{layer}_cond_{n}"]
    a["l2_w"] = rows(g["L2_ffn_weight_fp8"].T)
    for n in ("bias", "input_scale", "weight_scale"):
        a["l2_" + n] = g["L2_ffn_" + n]
    a["l3_router"] = rows(g["L3_ffn_router_w"].T)
    a["l3_router_b"] = g["L3_ffn_router_b"]
    a["l3_experts"] = experts(g["L3_ffn_W"], g["L3_ffn_V"], g["L3_ffn_W_out"])
    return {n: np.ascontiguousarray(v) for n, v in a.items()}


_OUT = ((2, 1024, 256), "float32")


def kernel(**inputs):
    import numpy as _np
    import concourse.bacc as _bacc
    from concourse import mybir as _mybir
    from concourse.bass_utils import run_bass_kernel_spmd as _run

    nc = _bacc.Bacc("TRN2", target_bir_lowering=False, num_devices=1)
    laid = lay_out(inputs)
    arrays = {f"in_{n}": a for n, a in laid.items()}
    dram = {n: nc.dram_tensor(f"in_{n}", a.shape, _mybir.dt.from_np(a.dtype), kind="ExternalInput").ap()
            for n, a in laid.items()}
    out = nc.dram_tensor("out_0", _OUT[0], _mybir.dt.from_np(_np.dtype(_OUT[1])), kind="ExternalOutput").ap()
    four_layers(nc, dram, out)
    return _run(nc, [arrays], core_ids=[0]).results[0]["out_0"]
```

```python
from contextlib import ExitStack, contextmanager

import concourse.bass as bass
from concourse import mybir

P = 128
B, S, D = 2, 1024, 256
TOK = B * S
NT = TOK // P
TB = S // P
KD = D // P
DH = 64
HEADS = 16
HG = 2
NG = HEADS // HG
CH = 512
NCH = TOK // CH
TPC = CH // P

ALU = mybir.AluOpType
ACT = mybir.ActivationFunctionType
AX = mybir.AxisListType
F32 = mybir.dt.float32
F32R = mybir.dt.float32r
U32 = mybir.dt.uint32
I32 = mybir.dt.int32
U8 = mybir.dt.uint8

FAR = -1.0e30


class Kit:

    def __init__(self, nc, ctx):
        self.nc, self.ctx = nc, ctx
        self.sem_ctx, self.sems = ctx, []

    @contextmanager
    def stage(self):
        before = self.sem_ctx, self.sems
        with ExitStack() as own:
            self.sem_ctx, self.sems = own, []
            yield
            with self.nc.Block() as block:
                @block.gpsimd
                def _(pool):
                    for s in self.sems:
                        pool.sem_clear(s)
        self.sem_ctx, self.sems = before

    def sb(self, name, shape, dtype=F32, ctx=None):
        return (ctx or self.ctx).enter_context(self.nc.sbuf_tensor(name, shape, dtype))

    def ps(self, name, shape, ctx):
        return ctx.enter_context(self.nc.psum_tensor(name, shape, F32))

    def sem(self, name):
        self.sems.append(self.sem_ctx.enter_context(self.nc.semaphore(name)))
        return self.sems[-1]


class Steps:

    def __init__(self, eng, sem):
        self.eng, self.sem, self.n = eng, sem, 0

    def did(self, instruction):
        instruction.then_inc(self.sem, 1)
        self.n += 1

    def settle(self):
        self.eng.wait_ge(self.sem, self.n)

    def then(self, instruction):
        self.did(instruction)
        self.settle()


def wait_apart(eng, sem, value, mark):
    eng.wait_ge(sem, value)
    eng.sem_inc(mark, 1)


def bc(ap, shape):
    return ap.broadcast_to(shape)


def to_feature_major(k, name, src, dst, ident):
    nc = k.nc
    NT = src.shape[1]
    turned, out_a, out_v = k.sem(name + "_turned"), k.sem(name + "_outa"), k.sem(name + "_outv")
    with ExitStack() as ctx:
        banks = [k.ps(f"{name}_ps{i}", [P, KD, 2 * P], ctx) for i in range(4)]
        with nc.Block() as block:
            @block.tensor
            def _(pe):
                for g in range(NT // 2):
                    if g >= 4:
                        pe.wait_ge(out_a if g % 2 == 0 else out_v, (g - 4) // 2 + 1)
                    for c in range(KD):
                        for t in range(2):
                            last = nc.tensor.transpose(banks[g % 4][:, c, t * P:(t + 1) * P],
                                                       src[:, 2 * g + t, c * P:(c + 1) * P], ident[:])
                    last.then_inc(turned, 1)

            @block.scalar
            def _(act):
                for g in range(0, NT // 2, 2):
                    act.wait_ge(turned, g + 1)
                    nc.scalar.activation(dst[:, :, 2 * g * P:(2 * g + 2) * P], banks[g % 4][:],
                                         ACT.Copy).then_inc(out_a, 1)

            @block.vector
            def _(dve):
                for g in range(1, NT // 2, 2):
                    dve.wait_ge(turned, g + 1)
                    nc.vector.tensor_copy(dst[:, :, 2 * g * P:(2 * g + 2) * P],
                                          banks[g % 4][:]).then_inc(out_v, 1)


def normalise(k, name, src, dst, gamma, eps, beta=None, add_to=None, loads=()):
    nc = k.nc
    NT = src.shape[1]
    done, sd_ready, var_ready, loaded, centred, scaled = (
        k.sem(f"{name}_{s}") for s in ("dve", "sd", "var", "loaded", "centred", "scaled"))
    more = beta is not None or add_to is not None
    with ExitStack() as ctx:
        st = k.sb(name + "_st", [P, NT, 6], ctx=ctx)
        mv = k.sb(name + "_mv", [P, NT, 2], ctx=ctx)
        ve = k.sb(name + "_ve", [P, NT], ctx=ctx)
        sd = k.sb(name + "_sd_t", [P, NT], ctx=ctx)
        rs = k.sb(name + "_rs", [P, NT], ctx=ctx)
        tmp = k.sb(name + "_tmp", [P, NT, D], ctx=ctx)
        with nc.Block() as block:
            @block.sync
            def _(sp):
                for tile, dram in loads:
                    sp.dma_start(tile[:], dram.partition_broadcast(P)).then_inc(loaded, 16)

            @block.vector
            def _(dve):
                s = Steps(dve, done)
                for t in range(NT):
                    s.did(nc.vector.bn_stats(st[:, t, :], src[:, t, :]))
                s.settle()
                for t in range(NT):
                    s.did(nc.vector.bn_aggr(mv[:, t, :], st[:, t, :]))
                s.settle()
                nc.vector.tensor_scalar(ve[:], mv[:, :, 1], eps, None, ALU.add).then_inc(var_ready, 1)
                if loads:
                    dve.wait_ge(loaded, 16 * len(loads))
                for t in range(NT):
                    nc.vector.scalar_tensor_tensor(out=tmp[:, t, :], in0=src[:, t, :], scalar=mv[:, t, 0:1],
                                                   in1=gamma[:], op0=ALU.subtract,
                                                   op1=ALU.mult).then_inc(centred, 1)
                    if t == 1:
                        dve.wait_ge(sd_ready, 1)
                        nc.vector.reciprocal(rs[:], sd[:]).then_inc(sd_ready, 1)
                if more:
                    for t in range(0, NT, 4):
                        rows = slice(t, t + 4)
                        dve.wait_ge(scaled, t + 4)
                        if beta is not None:
                            s.then(nc.vector.tensor_tensor(tmp[:, rows, :], tmp[:, rows, :],
                                                           bc(beta[:, None, :], [P, 4, D]), ALU.add))
                        nc.vector.tensor_tensor(dst[:, rows, :], tmp[:, rows, :], add_to[:, rows, :], ALU.add)

            @block.scalar
            def _(act):
                act.wait_ge(var_ready, 1)
                nc.scalar.activation(sd[:], ve[:], ACT.Sqrt).then_inc(sd_ready, 1)
                act.wait_ge(sd_ready, 2)
                for t in range(NT):
                    act.wait_ge(centred, t + 1)
                    nc.scalar.activation((tmp if more else dst)[:, t, :], tmp[:, t, :], ACT.Copy,
                                         scale=rs[:, t:t + 1]).then_inc(scaled, 1)


def route(k, name, xT, w_dram, E, top, shares, ident, bias=None, extra=None, scale=1.0, soft=None,
          ones=None):
    nc = k.nc
    EP = 8
    loaded, logit, dve_done, exped, iot = (k.sem(f"{name}_{s}") for s in
                                           ("loaded", "logit", "dve", "exp", "iota"))
    with ExitStack() as ctx:
        w = k.sb(name + "_w", [P, KD, E], ctx=ctx)
        bt = k.sb(name + "_b", [P, E], ctx=ctx)
        io = k.sb(name + "_io", [P, EP], ctx=ctx)
        L = k.sb(name + "_L", [P, NT, EP], ctx=ctx)
        M8 = k.sb(name + "_M8", [P, NT, 8], ctx=ctx)
        I8 = k.sb(name + "_I8", [P, NT, 8], U32, ctx=ctx)
        If = k.sb(name + "_If", [P, NT, 2], ctx=ctx)
        Ex = k.sb(name + "_E", [P, NT, EP], ctx=ctx)
        oh = k.sb(name + "_oh", [P, NT, EP], ctx=ctx)
        r1 = k.sb(name + "_r1", [P, NT], ctx=ctx)
        r2 = k.sb(name + "_r2", [P, NT], ctx=ctx)
        if extra is not None:
            condT_dram, wg_dram = extra
            cT = k.sb(name + "_cT", [DH, B], ctx=ctx)
            wg = k.sb(name + "_wg", [DH, E], ctx=ctx)
            cb = k.sb(name + "_cb", [DH, B, CH], ctx=ctx)
        LT = k.sb(name + "_LT", [E, TOK], ctx=ctx)
        lps = [k.ps(f"{name}_lps{i}", [E, CH], ctx) for i in range(NCH)]
        ps = k.ps(name + "_ps", [P, NT, E], ctx)
        columns, taken = k.sem(name + "_columns"), k.sem(name + "_taken")
        n_loads = 1 + (bias is not None) + 2 * (extra is not None)
        with nc.Block() as block:
            @block.sync
            def _(sp):
                sp.dma_start(w[:], w_dram).then_inc(loaded, 16)
                if bias is not None:
                    sp.dma_start(bt[:], bias.partition_broadcast(P)).then_inc(loaded, 16)
                if extra is not None:
                    sp.dma_start(cT[:], condT_dram, allow_slow_non_contiguous=True).then_inc(loaded, 16)
                    sp.dma_start(wg[:], wg_dram).then_inc(loaded, 16)

            @block.gpsimd
            def _(pool):
                nc.gpsimd.iota(io[:], [[1, EP]], base=0, channel_multiplier=0,
                               allow_small_or_imprecise_dtypes=True).then_inc(iot, 1)

            @block.tensor
            def _(pe):
                pe.wait_ge(loaded, 16 * n_loads)
                if extra is not None:
                    pe.wait_ge(iot, 2)
                for n in range(NCH):
                    for c in range(KD):
                        last = nc.tensor.matmul(lps[n][:], w[:, c, :], xT[:, c, n * CH:(n + 1) * CH],
                                                start=(c == 0), stop=(c == KD - 1 and extra is None))
                    if extra is not None:
                        last = nc.tensor.matmul(lps[n][:], wg[:], cb[:, n * CH // S, :],
                                                start=False, stop=True)
                    last.then_inc(columns, 1)
                for t in range(NT):
                    if t % TPC == 0:
                        pe.wait_ge(taken, t // TPC + 1)
                    last = nc.tensor.transpose(ps[:, t, :], LT[:, t * P:(t + 1) * P], ident[0:E, 0:E])
                last.then_inc(logit, 1)

            @block.scalar
            def _(act):
                for n in range(NCH):
                    act.wait_ge(columns, n + 1)
                    nc.scalar.activation(LT[:, n * CH:(n + 1) * CH], lps[n][:], ACT.Copy).then_inc(taken, 1)
                if soft:
                    act.wait_ge(exped, 1)
                    nc.scalar.activation(Ex[:], Ex[:], ACT.Exp).then_inc(exped, 1)

            @block.vector
            def _(dve):
                s = Steps(dve, dve_done)
                if extra is not None:
                    dve.wait_ge(loaded, 16 * n_loads)
                    dve.wait_ge(iot, 1)
                    nc.vector.tensor_copy(cb[:], bc(cT[:, :, None], [DH, B, CH])).then_inc(iot, 1)
                if E < EP:
                    s.then(nc.vector.memset(L[:], -3.0e38))
                dve.wait_ge(logit, 1)
                if bias is not None:
                    s.then(nc.vector.tensor_tensor(L[:, :, 0:E], ps[:], bc(bt[:, None, :], [P, NT, E]),
                                                   ALU.add))
                else:
                    s.then(nc.vector.tensor_scalar(L[:, :, 0:E], ps[:], scale, None, ALU.mult))
                for t in range(NT):
                    s.did(nc.vector.max(M8[:, t, :], L[:, t, :]))
                s.settle()
                for t in range(NT):
                    s.did(nc.vector.max_index(I8[:, t, :], M8[:, t, :], L[:, t, :]))
                s.settle()
                s.then(nc.vector.tensor_copy(If[:], I8[:, :, 0:2]))
                dve.wait_ge(iot, 1)
                iob = bc(io[:, None, 0:EP], [P, NT, EP])
                pick = ones if ones is not None else (shares if not soft else oh)
                s.then(nc.vector.tensor_tensor(pick[:], iob, bc(If[:, :, 0:1], [P, NT, EP]), ALU.is_equal))
                if top == 2:
                    s.then(nc.vector.tensor_tensor(Ex[:], iob, bc(If[:, :, 1:2], [P, NT, EP]),
                                                   ALU.is_equal))
                    s.then(nc.vector.tensor_tensor(pick[:], pick[:], Ex[:], ALU.add))
                if soft:
                    nc.vector.tensor_tensor(Ex[:], L[:], bc(M8[:, :, 0:1], [P, NT, EP]),
                                            ALU.subtract).then_inc(exped, 1)
                    dve.wait_ge(exped, 2)
                    if soft == "all":
                        s.then(nc.vector.reduce_sum(r1[:], Ex[:], AX.X))
                        s.then(nc.vector.reciprocal(r2[:], r1[:]))
                        s.then(nc.vector.tensor_tensor(Ex[:], Ex[:], bc(r2[:, :, None], [P, NT, EP]),
                                                       ALU.mult))
                    s.then(nc.vector.tensor_tensor(Ex[:], Ex[:], pick[:], ALU.mult))
                    s.then(nc.vector.reduce_sum(r1[:], Ex[:], AX.X))
                    if soft == "all":
                        s.then(nc.vector.tensor_scalar(r1[:], r1[:], 1e-20, None, ALU.add))
                    s.then(nc.vector.reciprocal(r2[:], r1[:]))
                    s.then(nc.vector.tensor_tensor(shares[:, :, 0:EP], Ex[:],
                                                   bc(r2[:, :, None], [P, NT, EP]), ALU.mult))


def gated_experts(k, name, xT, w_dram, n_experts, y, shares):
    nc = k.nc
    per, turns = 2 * NCH, n_experts // 2
    WF = 2 * KD * P + D
    first_loaded = k.sem(name + "_first_loaded")
    names = ("loaded", "x_hi", "x_lo", "w_hi", "w_lo", "gu", "f", "g", "a", "h_hi", "h_lo", "down", "shared", "added")
    (w_loaded, x_high, x_low, w_high, w_low, gu_done, f_done, g_done, a_done, hid_high, hid_low, down_done, shared,
     added) = (k.sem(f"{name}_{s}") for s in names)
    with ExitStack() as ctx:
        w = k.sb(name + "_w", [P, n_experts, WF], ctx=ctx)
        wh = [k.sb(f"{name}_wh{u}", [P, WF], F32R, ctx=ctx) for u in range(2)]
        wl = [k.sb(f"{name}_wl{u}", [P, WF], F32R, ctx=ctx) for u in range(2)]
        xh, xl = (k.sb(f"{name}_x{n}", [P, KD, TOK], F32R, ctx=ctx) for n in "hl")
        fs, gs, hf = ([k.sb(f"{name}_{n}{i}", [P, CH], ctx=ctx) for i in range(2)] for n in ("f", "g", "hf"))
        hh, hl = ([k.sb(f"{name}_{n}{i}", [P, CH], F32R, ctx=ctx) for i in range(2)] for n in ("hh", "hl"))
        part = [k.sb(f"{name}_part{i}", [P, TPC, D], ctx=ctx) for i in range(2)]
        gps = [k.ps(f"{name}_gps{i}", [P, CH], ctx) for i in range(2)]
        ups = [k.ps(f"{name}_ups{i}", [P, CH], ctx) for i in range(2)]
        dps = [k.ps(f"{name}_dps{i}", [P, 2, D], ctx) for i in range(4)]

        def columns(part, c2):
            return slice((part * KD + c2) * P, (part * KD + c2 + 1) * P)

        def in_turns_of_two(eng, turn):
            with eng.Fori(0, turns - 1) as i:
                turn(Turn(i), True)
            turn(Turn(turns - 1), False)

        def next_expert(T, u, more):
            if u == 0:
                return T.part(2, 1, 1), 1
            return (T.later().part(2, 0, 1), 0) if more else None

        with nc.Block() as block:
            @block.sync
            def _(sp):
                sp.dma_start(w[:, 0, :], w_dram[0]).then_inc(first_loaded, 16)
                for e in range(1, n_experts):
                    sp.dma_start(w[:, e, :], w_dram[e]).then_inc(w_loaded, 16)

            @block.gpsimd
            def _(pool):
                def turn(T, more):
                    for n in range(per):
                        pool.wait_ge(shared, T.count(2 * per, 2 * n + 6))
                        pool.wait_ge(added, T.count(per, n + 2))
                        rows = y[:, (n % NCH) * TPC:(n % NCH + 1) * TPC, :]
                        nc.gpsimd.tensor_tensor(rows, rows, part[n % 2][:], ALU.add).then_inc(added, 1)

                nc.gpsimd.memset(y[:], 0.0).then_inc(added, 1)
                pool.wait_ge(added, 1)
                pool.sem_inc(added, 1)
                in_turns_of_two(pool, turn)

            @block.tensor
            def _(pe):
                def gate_up(T, n):
                    u, c = n // NCH, n % NCH
                    if c == 0:
                        pe.wait_ge(w_low, T.count(2, u + 1))
                    pe.wait_ge(a_done, T.count(per, n + 1))
                    cols = slice(c * CH, (c + 1) * CH)
                    for part, ps in enumerate((gps, ups)):
                        for c2 in range(KD):
                            for m, (a, b) in enumerate(((wh, xh), (wh, xl), (wl, xh))):
                                last = nc.tensor.matmul(ps[n % 2][:], a[u][:, columns(part, c2)], b[:, c2, cols],
                                                        start=(c2 == 0 and m == 0),
                                                        stop=(c2 == KD - 1 and m == 2))
                    last.then_inc(gu_done, 1)

                def down_projection(T, n):
                    u = n // NCH
                    pe.wait_ge(hid_low, T.count(per, n + 1))
                    for t2 in range(2):
                        pe.wait_ge(shared, T.count(2 * per, 2 * n + t2 + 1))
                        for t in range(2):
                            rows = slice((2 * t2 + t) * P, (2 * t2 + t + 1) * P)
                            for m, (a, b) in enumerate(((hh, wh), (hh, wl), (hl, wh))):
                                last = nc.tensor.matmul(dps[(2 * n + t2) % 4][:, t, :], a[n % 2][:, rows],
                                                        b[u][:, 2 * KD * P:WF], start=(m == 0), stop=(m == 2))
                        last.then_inc(down_done, 1)

                def turn(T, more):
                    for n in range(per):
                        if n + 1 < per:
                            gate_up(T, n + 1)
                        elif more:
                            gate_up(T.later(), 0)
                        down_projection(T, n)

                pe.wait_ge(x_low, 1)
                gate_up(Turn(0), 0)
                pe.wait_ge(x_low, NCH)
                in_turns_of_two(pe, turn)

            @block.scalar
            def _(act):
                def split(T, e, u):
                    nc.scalar.activation(wh[u][:], w[:, e, :].rearrange("p o f -> p (o f)"),
                                         ACT.Copy).then_inc(w_high, 1)

                def share_rows(T, n):
                    u, c = n // NCH, n % NCH
                    act.wait_ge(added, T.count(per, n + 1))
                    for t2 in range(2):
                        act.wait_ge(down_done, T.count(2 * per, 2 * n + t2 + 1 + 4))
                        for t in range(2):
                            last = nc.scalar.activation(
                                part[n % 2][:, 2 * t2 + t, :], dps[(2 * n + t2) % 4][:, t, :], ACT.Copy,
                                scale=shares[:, c * TPC + 2 * t2 + t, T.part(2, u, 1)])
                        last.then_inc(shared, 1)

                def turn(T, more):
                    for n in range(per):
                        act.wait_ge(a_done, T.count(per, n + 1))
                        act.wait_ge(gu_done, T.count(per, n + 1))
                        nc.scalar.activation(fs[n % 2][:], gps[n % 2][:], ACT.Copy).then_inc(f_done, 1)
                        act.wait_ge(down_done, T.count(2 * per, 2 * n))
                        act.wait_ge(a_done, T.count(per, n + 3))
                        nc.scalar.activation(hh[n % 2][:], hf[n % 2][:], ACT.Copy).then_inc(hid_high, 1)
                        if n:
                            share_rows(T, n - 1)
                        follows = next_expert(T, n // NCH, more)
                        if n % NCH == 1 and follows:
                            split(T, *follows)
                    share_rows(T, per - 1)

                act.sem_inc(shared, 4)
                for c in range(NCH):
                    cols = slice(c * CH, (c + 1) * CH)
                    nc.scalar.activation(xh[:, :, cols], xT[:, :, cols], ACT.Copy).then_inc(x_high, 1)
                    if c == 0:
                        act.wait_ge(first_loaded, 16)
                        split(Turn(0), slice(0, 1), 0)
                act.wait_ge(w_loaded, 16 * (n_experts - 1))
                in_turns_of_two(act, turn)

            @block.vector
            def _(dve):
                def split(T, e, u, nth):
                    dve.wait_ge(w_high, nth)
                    nc.vector.tensor_tensor(wl[u][:], w[:, e, :].rearrange("p o f -> p (o f)"),
                                            wh[u][:].bitcast(F32), ALU.subtract).then_inc(w_low, 1)

                def activate(T, n):
                    dve.wait_ge(f_done, T.count(per, n + 1))
                    nc.vector.scalar_tensor_tensor(out=gs[n % 2][:], in0=fs[n % 2][:], scalar=0.01,
                                                   in1=gps[n % 2][:], op0=ALU.mult,
                                                   op1=ALU.max).then_inc(g_done, 1)
                    dve.wait_ge(g_done, T.count(per, n + 1))
                    nc.vector.tensor_tensor(hf[n % 2][:], gs[n % 2][:], ups[n % 2][:],
                                            ALU.mult).then_inc(a_done, 1)

                def low_part(T, n):
                    dve.wait_ge(hid_high, T.count(per, n + 1))
                    nc.vector.tensor_tensor(hl[n % 2][:], hf[n % 2][:], hh[n % 2][:].bitcast(F32),
                                            ALU.subtract).then_inc(hid_low, 1)

                def turn(T, more):
                    for n in range(per):
                        activate(T, n)
                        low_part(T, n)
                        follows = next_expert(T, n // NCH, more)
                        if n % NCH == 1 and follows:
                            split(T, *follows, T.count(2, n // NCH + 2))

                dve.sem_inc(a_done, 2)
                dve.sem_inc(down_done, 4)
                for c in range(NCH):
                    cols = slice(c * CH, (c + 1) * CH)
                    dve.wait_ge(x_high, c + 1)
                    nc.vector.tensor_tensor(xl[:, :, cols], xT[:, :, cols], xh[:, :, cols].bitcast(F32),
                                            ALU.subtract).then_inc(x_low, 1)
                    if c == 0:
                        split(Turn(0), slice(0, 1), 0, 1)
                in_turns_of_two(dve, turn)


def picked_ffn(k, name, src, picked, w1_dram, b1_dram, wo_dram, bo_dram, dst, ident, E):
    nc = k.nc
    FC = b1_dram.shape[1] // P
    LOW = 32
    R = LOW + E
    names = ("loaded", "b_loaded", "masked", "turned", "taken", "hps", "gelu", "out", "sum", "dve", "oh", "oh_taken",
             "set_up", "bias")
    (loaded, b_loaded, masked, turned, taken, hps_done, gelu_done, out_done, out_sum, dve_done, oh_turned,
     oh_taken, set_up, bias_split) = (k.sem(f"{name}_{s}") for s in names)
    TG = E * TPC // 2
    with ExitStack() as ctx:
        w1 = k.sb(name + "_w1", [P, E, KD, FC * P], ctx=ctx)
        bf = k.sb(name + "_bf", [P, FC * P], ctx=ctx)
        bh = k.sb(name + "_bh", [P, FC * P], F32R, ctx=ctx)
        b1 = k.sb(name + "_b1", [P, FC * P], F32R, ctx=ctx)
        wo = k.sb(name + "_wo", [P, FC, D], ctx=ctx)
        bo = k.sb(name + "_bo", [P, D], ctx=ctx)
        ym = k.sb(name + "_ym", [P, E, TPC, D], ctx=ctx)
        ymT = [k.sb(f"{name}_ymT{i}", [P, E, KD, CH], ctx=ctx) for i in range(2)]
        pk = k.sb(name + "_pk", [P, TPC, R], ctx=ctx)
        pkT = [k.sb(f"{name}_pkT{i}", [P, CH], F32R, ctx=ctx) for i in range(2)]
        hid = k.sb(name + "_hid", [P, FC, CH], ctx=ctx)
        tmp = k.sb(name + "_tmp", [P, 2, 2, D], ctx=ctx)
        tps = [k.ps(f"{name}_tps{i}", [P, KD, 2 * P], ctx) for i in range(2)]
        hps = [k.ps(f"{name}_hps{i}", [P, CH], ctx) for i in range(2)]
        ops = [k.ps(f"{name}_ops{i}", [P, 2, D], ctx) for i in range(2)]
        kps = k.ps(name + "_kps", [R, CH], ctx)

        def in_chunks(eng, run):
            with eng.Fori(0, NCH // 2 - 1) as i:
                run(2 * i, 0, True)
                run(2 * i + 1, 1, True)
            run(NCH - 2, 0, True)
            run(NCH - 1, 1, False)

        with nc.Block() as block:
            @block.sync
            def _(sp):
                for at in (0, LOW):
                    sp.dma_start(bf[at:at + E, :], b1_dram).then_inc(b_loaded, 16)
                sp.dma_start(w1[:], w1_dram).then_inc(loaded, 16)
                sp.dma_start(wo[:], wo_dram).then_inc(loaded, 16)
                sp.dma_start(bo[:], bo_dram.partition_broadcast(P)).then_inc(loaded, 16)

            @block.gpsimd
            def _(pool):
                nc.gpsimd.memset(pk[:], 0.0).then_inc(set_up, 1)
                nc.gpsimd.memset(b1[:].bitcast(F32), 0.0).then_inc(set_up, 1)
                for i in range(2):
                    nc.gpsimd.memset(pkT[i][:].bitcast(F32), 0.0).then_inc(set_up, 1)

            @block.tensor
            def _(pe):
                def turn_picks(c):
                    pe.wait_ge(masked, (E + 2) * c + 2)
                    for t in range(TPC):
                        last = nc.tensor.transpose(kps[:, t * P:(t + 1) * P], pk[:, t, :], ident[:])
                    last.then_inc(oh_turned, 1)

                def turn(c, g):
                    e, t2 = g // 2, g % 2
                    pe.wait_ge(masked, (E + 2) * c + (2 + e + 1))
                    pe.wait_ge(taken, TG * c + (g + 1))
                    for c2 in range(KD):
                        for t in range(2):
                            last = nc.tensor.transpose(tps[g % 2][:, c2, t * P:(t + 1) * P],
                                                       ym[:, e, 2 * t2 + t, c2 * P:(c2 + 1) * P], ident[:])
                    last.then_inc(turned, 1)

                def chunk(c, u, prepare):
                    pe.wait_ge(taken, TG * c + (TG + 2))
                    pe.wait_ge(oh_taken, c + 1)
                    for f in range(FC):
                        pe.wait_ge(gelu_done, FC * c + (f + 1))
                        for e in range(E):
                            for c2 in range(KD):
                                nc.tensor.matmul(hps[f % 2][:], w1[:, e, c2, f * P:(f + 1) * P],
                                                 ymT[u][:, e, c2, :], start=(e == 0 and c2 == 0), stop=False)
                        nc.tensor.matmul(hps[f % 2][:], b1[:, f * P:(f + 1) * P], pkT[u][:],
                                         start=False, stop=True).then_inc(hps_done, 1)
                        if prepare:
                            if f == 0:
                                turn_picks(c + 1)
                            for g in range(f * TG // FC, (f + 1) * TG // FC):
                                turn(c + 1, g)
                    pe.wait_ge(gelu_done, FC * c + (FC + 2))
                    for t2 in range(2):
                        pe.wait_ge(out_sum, 2 * c + (t2 + 1))
                        for t in range(2):
                            for f in range(FC):
                                last = nc.tensor.matmul(ops[t2][:, t, :],
                                                        hid[:, f, (2 * t2 + t) * P:(2 * t2 + t + 1) * P],
                                                        wo[:, f, :], start=(f == 0), stop=(f == FC - 1))
                        last.then_inc(out_done, 1)

                turn_picks(0)
                for g in range(TG):
                    turn(0, g)
                pe.wait_ge(loaded, 48)
                pe.wait_ge(bias_split, 3)
                in_chunks(pe, chunk)

            @block.scalar
            def _(act):
                def chunk(c, u, prepare):
                    for f in range(FC):
                        if f == 0:
                            act.wait_ge(out_done, 2 * c + 2)
                        act.wait_ge(hps_done, FC * c + (f + 1))
                        nc.scalar.activation(hid[:, f, :], hps[f % 2][:], ACT.Gelu).then_inc(gelu_done, 1)

                act.sem_inc(gelu_done, 2)
                in_chunks(act, chunk)

            @block.vector
            def _(dve):
                def mask(c, e):
                    if e == 0:
                        dve.wait_ge(turned, TG * c + 1)
                    rows = src[:, bass.ds(c * TPC, TPC), :]
                    nc.vector.tensor_tensor(ym[:, e], rows,
                                            bc(picked[:, bass.ds(c * TPC, TPC), e:e + 1], [P, TPC, D]),
                                            ALU.mult).then_inc(masked, 1)

                def picks(c):
                    dve.wait_ge(oh_turned, c + 1)
                    for at in (0, LOW):
                        nc.vector.tensor_copy(pk[:, :, at:at + E],
                                              picked[:, bass.ds(c * TPC, TPC), 0:E]).then_inc(masked, 1)

                def take_picks(c, u):
                    dve.wait_ge(oh_turned, c + 2)
                    nc.vector.tensor_copy(pkT[u][0:R, :], kps[:]).then_inc(oh_taken, 1)

                def take(c, u, g):
                    e, t2 = g // 2, g % 2
                    dve.wait_ge(turned, TG * c + (g + 2))
                    nc.vector.tensor_copy(ymT[u][:, e, :, 2 * t2 * P:(2 * t2 + 2) * P],
                                          tps[g % 2][:]).then_inc(taken, 1)

                def chunk(c, u, prepare):
                    if prepare:
                        dve.wait_ge(hps_done, FC * c + 1)
                        picks(c + 1)
                        for e in range(E):
                            mask(c + 1, e)
                        take_picks(c + 1, 1 - u)
                        for g in range(TG):
                            take(c + 1, 1 - u, g)
                    for t2 in range(2):
                        dve.wait_ge(out_done, 2 * c + (t2 + 3))
                        dve.wait_ge(out_sum, 2 * c + (t2 + 1))
                        nc.vector.tensor_tensor(tmp[:, t2], ops[t2][:], bc(bo[:, None, :], [P, 2, D]),
                                                ALU.add).then_inc(dve_done, 1)
                        dve.wait_ge(dve_done, 2 * c + (t2 + 1))
                        nc.vector.tensor_tensor(dst[:, bass.ds(c * TPC + 2 * t2, 2), :], tmp[:, t2],
                                                src[:, bass.ds(c * TPC + 2 * t2, 2), :],
                                                ALU.add).then_inc(out_sum, 1)

                dve.sem_inc(out_done, 2)
                dve.sem_inc(taken, 2)
                dve.sem_inc(out_sum, 2)
                dve.sem_inc(turned, 1)
                dve.sem_inc(oh_turned, 1)
                dve.wait_ge(set_up, 4)
                picks(0)
                for e in range(E):
                    mask(0, e)
                dve.wait_ge(b_loaded, 32)
                nc.vector.tensor_copy(b1[0:E, :], bf[0:E, :]).then_inc(bias_split, 1)
                nc.vector.tensor_copy(bh[LOW:R, :], bf[LOW:R, :]).then_inc(bias_split, 1)
                dve.wait_ge(bias_split, 2)
                nc.vector.tensor_tensor(b1[LOW:R, :], bf[LOW:R, :], bh[LOW:R, :].bitcast(F32),
                                        ALU.subtract).then_inc(bias_split, 1)
                take_picks(0, 0)
                for g in range(TG):
                    take(0, 0, g)
                dve.wait_ge(loaded, 48)
                in_chunks(dve, chunk)


def lora_ffn(k, name, xT, picked, w, x, ident):
    nc = k.nc
    wi_dram, bi_dram, wo_dram, bo_dram, la_dram, lb_dram = w
    R = la_dram.shape[2]
    E = 8
    FC = wi_dram.shape[2] // P
    names = ("loaded", "lb_loaded", "high", "low", "lb_split", "spread", "turned", "pick", "u", "uf", "uh", "um", "hps",
             "relu", "hid_hi", "hid_lo", "out", "sum", "dve")
    (loaded, lb_loaded, high, low, lb_split, spread, turned, pick_done, u_done, u_full, u_high, u_masked, hps_done,
     relu_done, hid_high, hid_low, out_done, out_sum, dve_done) = (k.sem(f"{name}_{s}") for s in names)
    with ExitStack() as ctx:
        wi = k.sb(name + "_wi", [P, KD, FC * P], ctx=ctx)
        bi = k.sb(name + "_bi", [P, FC], ctx=ctx)
        wo = k.sb(name + "_wo", [P, FC, D], ctx=ctx)
        bo = k.sb(name + "_bo", [P, D], ctx=ctx)
        la = k.sb(name + "_la", [P, KD, R], ctx=ctx)
        lb = k.sb(name + "_lb", [3 * R, FC * P], ctx=ctx)
        xh, xl = (k.sb(f"{name}_x{n}", [P, KD, TOK], F32R, ctx=ctx) for n in "hl")
        wih, wil = (k.sb(f"{name}_wi{n}", [P, KD, FC * P], F32R, ctx=ctx) for n in "hl")
        woh, wol = (k.sb(f"{name}_wo{n}", [P, FC, D], F32R, ctx=ctx) for n in "hl")
        lbh = k.sb(name + "_lbh", [3 * R, FC * P], F32R, ctx=ctx)
        lbt = k.sb(name + "_lbt", [3 * R, FC * P], F32R, ctx=ctx)
        pk = k.sb(name + "_pk", [P, TPC, R], ctx=ctx)
        pkT = k.sb(name + "_pkT", [R, CH], ctx=ctx)
        uf = k.sb(name + "_uf", [R, CH], ctx=ctx)
        um = k.sb(name + "_um", [3 * R, CH], F32R, ctx=ctx)
        hf = [k.sb(f"{name}_hf{i}", [P, CH], ctx=ctx) for i in range(2)]
        hh, hl = (k.sb(f"{name}_h{n}", [P, FC, CH], F32R, ctx=ctx) for n in "hl")
        tmp = k.sb(name + "_tmp", [P, 2, 2, D], ctx=ctx)
        hps = [k.ps(f"{name}_hps{i}", [P, CH], ctx) for i in range(2)]
        ops = [k.ps(f"{name}_ops{i}", [P, 2, D], ctx) for i in range(2)]
        kps = k.ps(name + "_kps", [R, CH], ctx)
        ups = k.ps(name + "_ups", [R, CH], ctx)
        whole = ((wi, wih, wil), (xT, xh, xl), (wo, woh, wol))
        with nc.Block() as block:
            @block.sync
            def _(sp):
                for tile, dram in ((wi, wi_dram), (bi, bi_dram), (wo, wo_dram), (la, la_dram)):
                    sp.dma_start(tile[:], dram).then_inc(loaded, 16)
                sp.dma_start(bo[:], bo_dram.partition_broadcast(P)).then_inc(loaded, 16)
                for n in range(3):
                    sp.dma_start(lb[n * R:(n + 1) * R, :], lb_dram).then_inc(lb_loaded, 16)

            @block.tensor
            def _(pe):
                pe.wait_ge(loaded, 5 * 16)
                pe.wait_ge(low, 3 * KD)
                pe.wait_ge(lb_split, 3)

                def three(out, left, right, start, stop):
                    (ah, al), (bh, bl) = left, right
                    nc.tensor.matmul(out, ah, bh, start=start, stop=False)
                    nc.tensor.matmul(out, ah, bl, start=False, stop=False)
                    return nc.tensor.matmul(out, al, bh, start=False, stop=stop)

                with pe.Fori(0, NCH) as c:
                    cols = bass.ts(c, CH)
                    pe.wait_ge(spread, c + 1)
                    for t in range(TPC):
                        last = nc.tensor.transpose(kps[:, t * P:(t + 1) * P], pk[:, t, :], ident[:])
                    last.then_inc(turned, 1)
                    for c2 in range(KD):
                        last = nc.tensor.matmul(ups[:], la[:, c2, :], xT[:, c2, cols],
                                                start=(c2 == 0), stop=(c2 == KD - 1))
                    last.then_inc(u_done, 1)
                    for f in range(FC):
                        pe.wait_ge(relu_done, FC * c + (f + 1))
                        rows = slice(f * P, (f + 1) * P)
                        for c2 in range(KD):
                            three(hps[f % 2][:], (wih[:, c2, rows], wil[:, c2, rows]),
                                  (xh[:, c2, cols], xl[:, c2, cols]), c2 == 0, False)
                        if f == 0:
                            pe.wait_ge(u_masked, 2 * c + 2)
                        nc.tensor.matmul(hps[f % 2][:], lbh[:, rows], um[:],
                                         start=False, stop=True).then_inc(hps_done, 1)
                    for t2 in range(2):
                        pe.wait_ge(out_sum, 2 * c + (t2 + 1))
                        for t in range(2):
                            for f in range(FC):
                                if t2 == 0 and t == 0:
                                    pe.wait_ge(hid_low, FC * c + (f + 3))
                                rows = slice((2 * t2 + t) * P, (2 * t2 + t + 1) * P)
                                last = three(ops[t2][:, t, :], (hh[:, f, rows], hl[:, f, rows]),
                                             (woh[:, f, :], wol[:, f, :]), f == 0, f == FC - 1)
                        last.then_inc(out_done, 1)

            @block.scalar
            def _(act):
                act.sem_inc(relu_done, 2)
                act.wait_ge(loaded, 5 * 16)
                for full, hi, lo in whole:
                    for c2 in range(KD):
                        half = slice(c2 * full.shape[1] // KD, (c2 + 1) * full.shape[1] // KD)
                        nc.scalar.activation(hi[:, half, :], full[:, half, :], ACT.Copy).then_inc(high, 1)
                with act.Fori(0, NCH) as c:
                    for f in range(FC):
                        if f == 0:
                            act.wait_ge(out_done, 2 * c + 1)
                        act.wait_ge(hid_low, FC * c + (f + 1))
                        act.wait_ge(hps_done, FC * c + (f + 1))
                        nc.scalar.activation(hf[f % 2][:], hps[f % 2][:], ACT.Relu,
                                             bias=bi[:, f:f + 1]).then_inc(relu_done, 1)
                        act.wait_ge(relu_done, FC * c + (f + 3))
                        nc.scalar.activation(hh[:, f, :], hf[f % 2][:], ACT.Copy).then_inc(hid_high, 1)

            @block.vector
            def _(dve):
                dve.sem_inc(out_done, 1)
                dve.sem_inc(out_sum, 2)
                dve.sem_inc(hid_low, 2)
                dve.wait_ge(loaded, 5 * 16)
                for n, (full, hi, lo) in enumerate(whole):
                    for c2 in range(KD):
                        half = slice(c2 * full.shape[1] // KD, (c2 + 1) * full.shape[1] // KD)
                        dve.wait_ge(high, KD * n + c2 + 1)
                        nc.vector.tensor_tensor(lo[:, half, :], full[:, half, :], hi[:, half, :].bitcast(F32),
                                                ALU.subtract).then_inc(low, 1)
                dve.wait_ge(lb_loaded, 3 * 16)
                nc.vector.tensor_copy(lbh[0:2 * R, :], lb[0:2 * R, :]).then_inc(lb_split, 1)
                nc.vector.tensor_copy(lbt[2 * R:3 * R, :], lb[2 * R:3 * R, :]).then_inc(lb_split, 1)
                dve.wait_ge(lb_split, 2)
                nc.vector.tensor_tensor(lbh[2 * R:3 * R, :], lb[2 * R:3 * R, :],
                                        lbt[2 * R:3 * R, :].bitcast(F32), ALU.subtract).then_inc(lb_split, 1)
                with dve.Fori(0, NCH) as c:
                    dve.wait_ge(out_done, 2 * c + 1)
                    nc.vector.tensor_copy(pk[:].rearrange("p t (e r) -> p t e r", e=E),
                                          bc(picked[:, bass.ts(c, TPC), :, None], [P, TPC, E, R // E])
                                          ).then_inc(spread, 1)
                    dve.wait_ge(turned, c + 1)
                    nc.vector.tensor_copy(pkT[:], kps[:]).then_inc(pick_done, 1)
                    dve.wait_ge(u_done, c + 1)
                    dve.wait_ge(pick_done, c + 1)
                    nc.vector.tensor_tensor(uf[:], ups[:], pkT[:], ALU.mult).then_inc(u_full, 1)
                    dve.wait_ge(u_full, c + 1)
                    nc.vector.tensor_copy(um[0:R, :], uf[:]).then_inc(u_high, 1)
                    nc.vector.tensor_copy(um[2 * R:3 * R, :], uf[:]).then_inc(u_masked, 1)
                    dve.wait_ge(u_high, c + 1)
                    nc.vector.tensor_tensor(um[R:2 * R, :], uf[:], um[0:R, :].bitcast(F32),
                                            ALU.subtract).then_inc(u_masked, 1)
                    for f in range(FC):
                        dve.wait_ge(hid_high, FC * c + (f + 1))
                        nc.vector.tensor_tensor(hl[:, f, :], hf[f % 2][:], hh[:, f, :].bitcast(F32),
                                                ALU.subtract).then_inc(hid_low, 1)
                    for t2 in range(2):
                        rows = x[:, bass.ds(c * TPC + 2 * t2, 2), :]
                        dve.wait_ge(out_done, 2 * c + (t2 + 2))
                        dve.wait_ge(out_sum, 2 * c + (t2 + 1))
                        nc.vector.tensor_tensor(tmp[:, t2], ops[t2][:], bc(bo[:, None, :], [P, 2, D]),
                                                ALU.add).then_inc(dve_done, 1)
                        dve.wait_ge(dve_done, 2 * c + (t2 + 1))
                        nc.vector.tensor_tensor(rows, tmp[:, t2], rows, ALU.add).then_inc(out_sum, 1)


def round_to_e4m3(k, name, src, dst, in_scale_dram, scale_out):
    nc = k.nc
    loaded, done = k.sem(name + "_loaded"), k.sem(name + "_done")
    with ExitStack() as ctx:
        v = k.sb(name + "_v", [P, NT, D], ctx=ctx)
        m = k.sb(name + "_m", [P, NT, D], ctx=ctx)
        r = k.sb(name + "_r", [P, 1], ctx=ctx)
        with nc.Block() as block:
            @block.sync
            def _(sp):
                sp.dma_start(scale_out[:], in_scale_dram.partition_broadcast(P)).then_inc(loaded, 16)

            @block.vector
            def _(dve):
                s = Steps(dve, done)
                dve.wait_ge(loaded, 16)
                s.then(nc.vector.reciprocal(r[:], scale_out[:]))
                s.then(nc.vector.tensor_scalar(v[:], src[:], r[:, 0:1], 448.0, ALU.mult, ALU.min))
                s.then(nc.vector.tensor_scalar(v[:], v[:], -448.0, None, ALU.max))
                s.then(nc.vector.tensor_scalar(m[:].bitcast(U32), v[:].bitcast(U32), 0x7F800000, None,
                                               ALU.bitwise_and))
                s.then(nc.vector.tensor_scalar(m[:], m[:], 2.0 ** -6, 1.5 * 2.0 ** 20, ALU.max, ALU.mult))
                s.then(nc.vector.tensor_tensor(v[:], v[:], m[:], ALU.add))
                s.then(nc.vector.tensor_tensor(v[:], v[:], m[:], ALU.subtract))
                nc.vector.tensor_scalar(dst[:], v[:], scale_out[:, 0:1], None, ALU.mult)


def linear(k, name, xT, w_dram, scale_dram, bias_dram, x):
    nc = k.nc
    loaded, scaled, mm, tmp_done, added = (k.sem(f"{name}_{s}") for s in
                                           ("loaded", "scaled", "mm", "tmp", "added"))
    with ExitStack() as ctx:
        w = k.sb(name + "_w", [P, KD, D], ctx=ctx)
        ws = k.sb(name + "_ws", [P, KD, D], ctx=ctx)
        bo = k.sb(name + "_b", [P, D], ctx=ctx)
        sc = k.sb(name + "_sc", [P, 1], ctx=ctx)
        tmp = k.sb(name + "_tmp", [P, 4, 2, D], ctx=ctx)
        ps = [k.ps(f"{name}_ps{i}", [P, 2, D], ctx) for i in range(4)]
        with nc.Block() as block:
            @block.sync
            def _(sp):
                sp.dma_start(w[:], w_dram).then_inc(loaded, 16)
                sp.dma_start(bo[:], bias_dram.partition_broadcast(P)).then_inc(loaded, 16)
                sp.dma_start(sc[:], scale_dram.partition_broadcast(P)).then_inc(loaded, 16)

            @block.tensor
            def _(pe):
                pe.wait_ge(scaled, 1)
                for t2 in range(NT // 2):
                    if t2 >= 4:
                        pe.wait_ge(tmp_done, t2 - 3)
                    for t in range(2):
                        tt = 2 * t2 + t
                        for c in range(KD):
                            last = nc.tensor.matmul(ps[t2 % 4][:, t, :], xT[:, c, tt * P:(tt + 1) * P],
                                                    ws[:, c, :], start=(c == 0), stop=(c == KD - 1))
                    last.then_inc(mm, 1)

            @block.vector
            def _(dve):
                dve.wait_ge(loaded, 48)
                nc.vector.tensor_scalar(ws[:], w[:], sc[:, 0:1], None, ALU.mult).then_inc(scaled, 1)
                for t2 in range(NT // 2):
                    rows = x[:, 2 * t2:2 * t2 + 2, :]
                    dve.wait_ge(mm, t2 + 1)
                    nc.vector.tensor_tensor(tmp[:, t2 % 4], ps[t2 % 4][:], bc(bo[:, None, :], [P, 2, D]),
                                            ALU.add).then_inc(tmp_done, 1)
                    dve.wait_ge(tmp_done, t2 + 1)
                    nc.vector.tensor_tensor(rows, tmp[:, t2 % 4], rows, ALU.add).then_inc(added, 1)


CAPACITY = 2 * (2 * 512) * 2 // 8


def places(k, name, chosen, rank, upper):
    nc = k.nc
    EP = 8
    made, mm, done = k.sem(name + "_made"), k.sem(name + "_mm"), k.sem(name + "_done")
    with ExitStack() as ctx:
        ones = k.sb(name + "_ones", [P, P], ctx=ctx)
        before = k.sb(name + "_before", [P, NT, EP], ctx=ctx)
        cps = k.ps(name + "_cps", [P, NT, EP], ctx)
        tps = k.ps(name + "_tps", [P, NT, EP], ctx)
        with nc.Block() as block:
            @block.gpsimd
            def _(pool):
                nc.gpsimd.memset(ones[:], 1.0).then_inc(made, 1)

            @block.tensor
            def _(pe):
                pe.wait_ge(made, 1)
                nc.tensor.matmul(cps[:], upper[:], chosen[:], start=True, stop=True).then_inc(mm, 1)
                nc.tensor.matmul(tps[:], ones[:], chosen[:], start=True, stop=True).then_inc(mm, 1)

            @block.vector
            def _(dve):
                s = Steps(dve, done)
                s.then(nc.vector.memset(before[:], 0.0))
                dve.wait_ge(mm, 2)
                for t in range(1, NT):
                    s.then(nc.vector.tensor_tensor(before[:, t, :], tps[:, t - 1, :], before[:, t - 1, :],
                                                   ALU.add))
                s.then(nc.vector.tensor_tensor(rank[:], cps[:], before[:], ALU.add))


def drop_over_capacity(k, name, shares, rank):
    nc = k.nc
    done = k.sem(name)
    with nc.Block() as block:
        @block.vector
        def _(dve):
            nc.vector.scalar_tensor_tensor(out=shares[:], in0=rank[:], scalar=float(CAPACITY), in1=shares[:],
                                           op0=ALU.is_le, op1=ALU.mult)


def sent_experts(k, name, src, shares, chosen, rank, w_dram, M, E, x, rows_dram, out_dram, ident):
    nc = k.nc
    MC = M // P
    CT = CAPACITY // P
    SLOTS = E * CAPACITY
    OVER, OTHER = float(2 ** 20), float(2 ** 22)
    WF = 2 * KD * M + MC * D
    per, turns = 2 * MC, E // 2
    PIECES = MC - 1
    HALF = CT // 2
    names = ("zeroed", "blank", "index_ready", "base", "dve", "sent", "x_turned", "x_high", "x_low", "w_high",
             "w_low", "w_last", "gu", "f", "product", "h_high", "h_low", "down", "y_act", "y_dve", "stored", "stored_ahead", "added")
    (zeroed, blank, index_ready, base_made, dve_done, sent, x_turned, x_high, x_low, w_high, w_low, w_last, gu_done, f_done,
     product, h_high, h_low, down_done, y_act, y_dve, stored, stored_ahead, added) = (k.sem(f"{name}_{n}") for n in names)
    w_loaded = [k.sem(f"{name}_w_loaded{u}") for u in range(2)]
    x_loaded = [k.sem(f"{name}_x_loaded{u}") for u in range(2)]
    ZB = 4
    BACK = 4
    fetched = [k.sem(f"{name}_fetched{u}") for u in range(BACK)]
    slots_of = lambda dram: dram.rearrange("(e t p) d -> e p t d", e=E, t=CT)
    with ExitStack() as ctx:
        zero = k.sb(name + "_zero", [P, ZB, D], ctx=ctx)
        base = k.sb(name + "_base", [P, E], ctx=ctx)
        v, pick, other = (k.sb(f"{name}_{n}", [P, NT, E], ctx=ctx) for n in ("v", "pick", "other"))
        slot = [k.sb(f"{name}_slot{n}", [P, NT], ctx=ctx) for n in range(2)]
        total = k.sb(name + "_total", [P, NT], ctx=ctx)
        near = k.sb(name + "_near", [P, 2, NT], ctx=ctx)
        send = k.sb(name + "_send", [P, 2, NT], U32, ctx=ctx)
        fetch = k.sb(name + "_fetch", [P, 2, NT], U32, ctx=ctx)
        share = k.sb(name + "_share", [P, 2, NT], ctx=ctx)
        w = [k.sb(f"{name}_w{u}", [P, WF], ctx=ctx) for u in range(2)]
        wh, wl = ([k.sb(f"{name}_{n}{u}", [P, WF], F32R, ctx=ctx) for u in range(2)] for n in ("wh", "wl"))
        xg = [k.sb(f"{name}_xg{u}", [P, CT, D], ctx=ctx) for u in range(2)]
        xh, xl = ([k.sb(f"{name}_{n}{u}", [P, KD, CAPACITY], F32R, ctx=ctx) for u in range(2)]
                  for n in ("xh", "xl"))
        yg = [k.sb(f"{name}_yg{u}", [P, CT, D], ctx=ctx) for u in range(2)]
        fs = [k.sb(f"{name}_f{i}", [P, CAPACITY], ctx=ctx) for i in range(2)]
        hf = [k.sb(f"{name}_hf{i}", [P, CAPACITY], ctx=ctx) for i in range(2)]
        hh, hl = ([k.sb(f"{name}_{n}{i}", [P, MC, CAPACITY], F32R, ctx=ctx) for i in range(2)]
                  for n in ("hh", "hl"))
        back = [k.sb(f"{name}_back{i}", [P, D], ctx=ctx) for i in range(BACK)]
        tps = [k.ps(f"{name}_tps{i}", [P, KD, 2 * P], ctx) for i in range(2)]
        gps = [k.ps(f"{name}_gps{i}", [P, CAPACITY], ctx) for i in range(2)]
        ups = [k.ps(f"{name}_ups{i}", [P, CAPACITY], ctx) for i in range(2)]
        dps = [k.ps(f"{name}_dps{i}", [P, 2, D], ctx) for i in range(2)]

        def part(which, c, m):
            at = (which * KD + c) * M + m * P
            return slice(at, at + P)

        def piece(n):
            return slice(n * WF // PIECES, (n + 1) * WF // PIECES)

        def down_rows(m):
            return slice(2 * KD * M + m * D, 2 * KD * M + (m + 1) * D)

        def in_experts(eng, expert):
            with eng.Fori(0, turns - 1) as i:
                expert(Turn(i), 0, (Turn(i), 1))
                expert(Turn(i), 1, (Turn(i, 1), 0))
            expert(Turn(turns - 1), 0, (Turn(turns - 1), 1))
            expert(Turn(turns - 1), 1, None)

        with nc.Block() as block:
            @block.sync
            def _(sp):
                for u in range(2):
                    sp.dma_start(w[u][:], w_dram[u]).then_inc(w_loaded[u], 16)
                sp.wait_ge(zeroed, 1)
                for n in range(SLOTS // P // ZB):
                    sp.dma_start(rows_dram[n * ZB * P:(n + 1) * ZB * P, :].rearrange("(p t) d -> p t d", t=ZB),
                                 zero[:]).then_inc(blank, 16)
                sp.wait_ge(blank, 16 * (SLOTS // P // ZB))
                sp.sem_inc(stored_ahead, 2)
                sp.wait_ge(sent, 16 * 2 * NT)
                for u in range(2):
                    sp.dma_start(xg[u][:], slots_of(rows_dram)[u]).then_inc(x_loaded[u], 16)

                def store(i, u):
                    sp.wait_ge(y_act, 2 * i + (u + 2))
                    sp.wait_ge(y_dve, 2 * i + (u + 2))
                    sp.dma_start(slots_of(out_dram)[2 * i + u], yg[u][:]).then_inc(stored, 16)
                    sp.wait_ge(stored, 32 * i + 16 * (u + 1))
                    sp.sem_inc(stored_ahead, 1)

                with sp.Fori(0, turns - 1) as i:
                    for u in range(2):
                        sp.wait_ge(x_turned, 4 * i + 2 * (u + 1))
                        sp.dma_start(xg[u][:], slots_of(rows_dram)[2 * i + (2 + u)]).then_inc(x_loaded[u], 16)
                        sp.wait_ge(w_low, (PIECES - 1) * (2 * i + u + 1))
                        sp.wait_ge(w_last, 2 * i + (u + 1))
                        sp.dma_start(w[u][:], w_dram[2 * i + (2 + u)]).then_inc(w_loaded[u], 16)
                        store(i, u)
                for u in range(2):
                    store(turns - 1, u)
                sp.wait_ge(stored, 16 * E)

            @block.gpsimd
            def _(pool):
                nc.gpsimd.memset(zero[:], 0.0).then_inc(zeroed, 1)
                nc.gpsimd.iota(base[:], [[CAPACITY, E]], base=-1, channel_multiplier=0,
                               allow_small_or_imprecise_dtypes=True).then_inc(base_made, 1)
                def low_weights(T, u):
                    for n in range(PIECES - 1):
                        pool.wait_ge(w_high, T.count(2 * PIECES, PIECES * u + n + 1))
                        nc.gpsimd.tensor_tensor(wl[u][:, piece(n)], w[u][:, piece(n)],
                                                wh[u][:, piece(n)].bitcast(F32), ALU.subtract).then_inc(w_low, 1)

                low_weights(Turn(0), 0)
                pool.wait_ge(index_ready, 2)
                pool.wait_ge(blank, 16 * (SLOTS // P // ZB))
                for n in range(2):
                    for t in range(NT):
                        pool.indirect_dma_start(
                            rows_dram, bass.IndirectOffsetOnAxis(ap=send[:, n, t:t + 1], axis=0),
                            src[:, t, :], None, bounds_check=SLOTS - 1, oob_is_err=False).then_inc(sent, 16)

                in_experts(pool, lambda T, u, following: following and low_weights(*following))
                pool.wait_ge(index_ready, 4)
                pool.wait_ge(stored, 16 * E)
                for n in range(2):
                    for t in range(NT):
                        at = n * NT + t
                        if at >= BACK:
                            pool.wait_ge(added, at - BACK + 1)
                        pool.indirect_dma_start(
                            back[at % BACK][:], None, out_dram,
                            bass.IndirectOffsetOnAxis(ap=fetch[:, n, t:t + 1], axis=0),
                            bounds_check=SLOTS - 1, oob_is_err=False).then_inc(fetched[at % BACK], 16)

            @block.tensor
            def _(pe):
                def turn(T, u):
                    pe.wait_ge(x_loaded[u], T.count(16, 16))
                    for half in range(HALF):
                        for c in range(KD):
                            for t in range(2):
                                last = nc.tensor.transpose(tps[half][:, c, t * P:(t + 1) * P],
                                                           xg[u][:, 2 * half + t, c * P:(c + 1) * P], ident[:])
                        last.then_inc(x_turned, 1)

                def gate_up(T, u, m):
                    n = u * MC + m
                    if m == 0:
                        pe.wait_ge(w_low, T.count(2 * (PIECES - 1), (PIECES - 1) * (u + 1)))
                        pe.wait_ge(w_last, T.count(2, u + 1))
                        pe.wait_ge(x_low, T.count(2 * HALF, HALF * (u + 1)))
                    pe.wait_ge(product, T.count(per, n + 1))
                    for which, ps in enumerate((gps, ups)):
                        for c in range(KD):
                            for q, (a, b) in enumerate(((wh, xh), (wh, xl), (wl, xh))):
                                last = nc.tensor.matmul(ps[n % 2][:], a[u][:, part(which, c, m)], b[u][:, c, :],
                                                        start=(c == 0 and q == 0), stop=(c == KD - 1 and q == 2))
                    last.then_inc(gu_done, 1)

                def down_projection(T, u):
                    pe.wait_ge(h_low, T.count(per, (u + 1) * MC + 2))
                    for half in range(HALF):
                        pe.wait_ge((y_act, y_dve)[half], T.count(2, u + 1))
                        for t in range(2):
                            rows = slice((2 * half + t) * P, (2 * half + t + 1) * P)
                            for m in range(MC):
                                for q, (a, b) in enumerate(((hh, wh), (hh, wl), (hl, wh))):
                                    last = nc.tensor.matmul(dps[half][:, t, :], a[u][:, m, rows],
                                                            b[u][:, down_rows(m)], start=(m == 0 and q == 0),
                                                            stop=(m == MC - 1 and q == 2))
                        last.then_inc(down_done, 1)

                def expert(T, u, following):
                    for m in range(1, MC):
                        gate_up(T, u, m)
                    if following:
                        turn(*following)
                        gate_up(*following, 0)
                    down_projection(T, u)

                turn(Turn(0), 0)
                gate_up(Turn(0), 0, 0)
                in_experts(pe, expert)

            @block.scalar
            def _(act):
                def high_columns(T, u):
                    for half in range(HALF):
                        act.wait_ge(x_turned, T.count(2 * HALF, HALF * u + half + 1))
                        nc.scalar.activation(xh[u][:, :, 2 * half * P:(2 * half + 2) * P], tps[half][:],
                                             ACT.Copy).then_inc(x_high, 1)

                def high_weights(T, u, n):
                    act.wait_ge(w_loaded[u], T.count(16, 16))
                    act.wait_ge(down_done, T.count(2 * HALF, HALF * (u + 1)))
                    nc.scalar.activation(wh[u][:, piece(n)], w[u][:, piece(n)], ACT.Copy).then_inc(w_high, 1)

                def hidden(T, u, m):
                    n = u * MC + m
                    act.wait_ge(product, T.count(per, n + 1))
                    act.wait_ge(gu_done, T.count(per, n + 1))
                    nc.scalar.activation(fs[n % 2][:], ups[n % 2][:], ACT.Silu).then_inc(f_done, 1)
                    act.wait_ge(product, T.count(per, n + 3))
                    nc.scalar.activation(hh[u][:, m, :], hf[n % 2][:], ACT.Copy).then_inc(h_high, 1)

                def take_output(T, u):
                    act.wait_ge(down_done, T.count(2 * HALF, HALF * u + 1 + 2 * HALF))
                    act.wait_ge(stored_ahead, T.count(2, u + 1))
                    nc.scalar.activation(yg[u][:, 0:2, :], dps[0][:], ACT.Copy).then_inc(y_act, 1)

                def expert(T, u, following):
                    if following:
                        for n in range(PIECES):
                            high_weights(*following, n)
                    for m in range(1, MC):
                        hidden(T, u, m)
                    if following:
                        high_columns(*following)
                        hidden(*following, 0)
                    take_output(T, u)

                act.sem_inc(y_act, 1)
                act.sem_inc(down_done, 2 * HALF)
                act.wait_ge(w_loaded[0], 16)
                for n in range(PIECES):
                    nc.scalar.activation(wh[0][:, piece(n)], w[0][:, piece(n)], ACT.Copy).then_inc(w_high, 1)
                high_columns(Turn(0), 0)
                hidden(Turn(0), 0, 0)
                in_experts(act, expert)

            @block.vector
            def _(dve):
                s = Steps(dve, dve_done)
                dve.sem_inc(y_dve, 1)
                dve.sem_inc(product, 2)
                dve.sem_inc(h_low, 2)
                dve.wait_ge(base_made, 1)
                s.then(nc.vector.tensor_scalar(v[:], rank[:], float(CAPACITY), OVER, ALU.is_gt, ALU.mult))
                s.then(nc.vector.tensor_tensor(v[:], v[:], rank[:], ALU.add))
                s.then(nc.vector.tensor_tensor(v[:], v[:], bc(base[:, None, :], [P, NT, E]), ALU.add))
                s.then(nc.vector.tensor_scalar(other[:], chosen[:], 1.0, -OTHER, ALU.subtract, ALU.mult))
                s.then(nc.vector.tensor_tensor(other[:], other[:], v[:], ALU.add))
                s.then(nc.vector.tensor_reduce(slot[0][:], other[:], AX.X, ALU.min))
                s.then(nc.vector.tensor_tensor(pick[:], v[:], chosen[:], ALU.mult))
                s.then(nc.vector.reduce_sum(total[:], pick[:], AX.X))
                s.then(nc.vector.tensor_tensor(slot[1][:], total[:], slot[0][:], ALU.subtract))
                for n in range(2):
                    nc.vector.tensor_copy(send[:, n, :], slot[n][:]).then_inc(index_ready, 1)
                for n in range(2):
                    s.then(nc.vector.tensor_scalar(near[:, n, :], slot[n][:], float(SLOTS - 1), None, ALU.min))
                    nc.vector.tensor_copy(fetch[:, n, :], near[:, n, :]).then_inc(index_ready, 1)
                    s.then(nc.vector.tensor_tensor(pick[:], v[:], bc(slot[n][:, :, None], [P, NT, E]),
                                                   ALU.is_equal))
                    s.then(nc.vector.tensor_tensor(pick[:], pick[:], shares[:], ALU.mult))
                    s.then(nc.vector.reduce_sum(share[:, n, :], pick[:], AX.X))

                def last_weights(T, u):
                    dve.wait_ge(w_high, T.count(2 * PIECES, PIECES * (u + 1)))
                    last = piece(PIECES - 1)
                    nc.vector.tensor_tensor(wl[u][:, last], w[u][:, last], wh[u][:, last].bitcast(F32),
                                            ALU.subtract).then_inc(w_last, 1)

                def low_columns(T, u):
                    for half in range(HALF):
                        cols = slice(2 * half * P, (2 * half + 2) * P)
                        dve.wait_ge(x_high, T.count(2 * HALF, HALF * u + half + 1))
                        nc.vector.tensor_tensor(xl[u][:, :, cols], tps[half][:], xh[u][:, :, cols].bitcast(F32),
                                                ALU.subtract).then_inc(x_low, 1)

                def hidden(T, u, m):
                    n = u * MC + m
                    dve.wait_ge(h_low, T.count(per, n + 1))
                    dve.wait_ge(f_done, T.count(per, n + 1))
                    nc.vector.tensor_tensor(hf[n % 2][:], fs[n % 2][:], gps[n % 2][:],
                                            ALU.mult).then_inc(product, 1)
                    dve.wait_ge(h_high, T.count(per, n + 1))
                    nc.vector.tensor_tensor(hl[u][:, m, :], hf[n % 2][:], hh[u][:, m, :].bitcast(F32),
                                            ALU.subtract).then_inc(h_low, 1)

                def take_output(T, u):
                    dve.wait_ge(down_done, T.count(2 * HALF, HALF * u + 2 + 2 * HALF))
                    dve.wait_ge(stored_ahead, T.count(2, u + 1))
                    nc.vector.tensor_copy(yg[u][:, 2:4, :], dps[1][:]).then_inc(y_dve, 1)

                def expert(T, u, following):
                    if following:
                        last_weights(*following)
                    for m in range(1, MC):
                        hidden(T, u, m)
                    if following:
                        low_columns(*following)
                        hidden(*following, 0)
                    take_output(T, u)

                last_weights(Turn(0), 0)
                low_columns(Turn(0), 0)
                hidden(Turn(0), 0, 0)
                in_experts(dve, expert)
                for n in range(2):
                    for t in range(NT):
                        at = n * NT + t
                        dve.wait_ge(fetched[at % BACK], 16 * (at // BACK + 1))
                        if n:
                            dve.wait_ge(added, at - NT + 1)
                        nc.vector.scalar_tensor_tensor(out=x[:, t, :], in0=back[at % BACK][:],
                                                       scalar=share[:, n, t:t + 1], in1=x[:, t, :],
                                                       op0=ALU.mult, op1=ALU.add).then_inc(added, 1)


TABLE = S + P - 1


def position_table(k, a, table_dram, ident):
    nc = k.nc
    NPT = S // P
    with ExitStack() as ctx:
        w0, b0, g0, b1, g1 = (k.sb("pt_" + n, [P, D], ctx=ctx) for n in ("w0", "b0", "g0", "b1", "g1"))
        w1 = k.sb("pt_w1", [P, KD, D], ctx=ctx)
        w2 = k.sb("pt_w2", [P, KD, HEADS], ctx=ctx)
        b2 = k.sb("pt_b2", [HEADS, 1], ctx=ctx)
        pos = k.sb("pt_pos", [P, NPT], ctx=ctx)
        h = k.sb("pt_h", [P, NPT, D], ctx=ctx)
        hn = k.sb("pt_hn", [P, NPT, D], ctx=ctx)
        hT = k.sb("pt_hT", [P, KD, S], ctx=ctx)
        tab = k.sb("pt_tab", [HEADS, TABLE], ctx=ctx)
        loaded, posd, made = k.sem("pt_loaded"), k.sem("pt_posd"), k.sem("pt_made")
        mm, stored, act_done = k.sem("pt_mm"), k.sem("pt_stored"), k.sem("pt_act")
        with nc.Block() as block:
            @block.sync
            def _(sp):
                for tile, n in ((w0, "w0"), (b0, "b0"), (g0, "g0"), (b1, "b1"), (g1, "g1")):
                    sp.dma_start(tile[:], a["l1_" + n].partition_broadcast(P)).then_inc(loaded, 16)
                sp.dma_start(w1[:], a["l1_w1"]).then_inc(loaded, 16)
                sp.dma_start(w2[:], a["l1_w2"]).then_inc(loaded, 16)
                sp.dma_start(b2[:], a["l1_b2"].rearrange("(h o) -> h o", o=1),
                             allow_slow_non_contiguous=True).then_inc(loaded, 16)
                sp.wait_ge(loaded, 8 * 16)

            @block.gpsimd
            def _(pool):
                nc.gpsimd.iota(pos[:], [[P, NPT]], base=0, channel_multiplier=1,
                               allow_small_or_imprecise_dtypes=True).then_inc(posd, 1)

            @block.vector
            def _(dve):
                dve.wait_ge(loaded, 8 * 16)
                dve.wait_ge(posd, 1)
                for t in range(NPT):
                    nc.vector.scalar_tensor_tensor(out=h[:, t, :], in0=w0[:], scalar=pos[:, t:t + 1],
                                                   in1=b0[:], op0=ALU.mult, op1=ALU.add)
        normalise(k, "pt_n0", h, hn, g0, 1e-5)
        with nc.Block() as block:
            @block.scalar
            def _(act):
                nc.scalar.activation(h[:], hn[:], ACT.Silu)
        to_feature_major(k, "pt_t0", h, hT, ident)
        with ExitStack() as inner:
            ps = [k.ps(f"pt_ps{i}", [P, 2, D], inner) for i in range(4)]
            with nc.Block() as block:
                @block.tensor
                def _(pe):
                    for t in range(NPT):
                        for c in range(KD):
                            last = nc.tensor.matmul(ps[t // 2][:, t % 2, :], hT[:, c, t * P:(t + 1) * P],
                                                    w1[:, c, :], start=(c == 0), stop=(c == KD - 1))
                        last.then_inc(mm, 1)

                @block.vector
                def _(dve):
                    for t2 in range(NPT // 2):
                        dve.wait_ge(mm, 2 * t2 + 2)
                        nc.vector.tensor_tensor(h[:, 2 * t2:2 * t2 + 2, :], ps[t2][:],
                                                bc(b1[:, None, :], [P, 2, D]), ALU.add)
        normalise(k, "pt_n1", h, hn, g1, 1e-5)
        with nc.Block() as block:
            @block.scalar
            def _(act):
                nc.scalar.activation(h[:], hn[:], ACT.Silu)
        to_feature_major(k, "pt_t1", h, hT, ident)
        with ExitStack() as inner:
            ps = [k.ps(f"pt_qs{i}", [HEADS, CH], inner) for i in range(2)]
            with nc.Block() as block:
                @block.tensor
                def _(pe):
                    for i in range(2):
                        for c in range(KD):
                            last = nc.tensor.matmul(ps[i][:], w2[:, c, :], hT[:, c, i * CH:(i + 1) * CH],
                                                    start=(c == 0), stop=(c == KD - 1))
                        last.then_inc(mm, 1)

                @block.vector
                def _(dve):
                    nc.vector.memset(tab[:, 0:P - 1], FAR).then_inc(made, 1)
                    for i in range(2):
                        dve.wait_ge(mm, NPT + i + 1)
                        nc.vector.tensor_scalar(tab[:, P - 1 + i * CH:P - 1 + (i + 1) * CH], ps[i][:],
                                                b2[:, 0:1], None, ALU.add).then_inc(made, 1)

                @block.sync
                def _(sp):
                    sp.wait_ge(made, 3)
                    sp.dma_start(table_dram, tab[:]).then_inc(stored, 16)
                    sp.wait_ge(stored, 16)


def attention(k, name, xT, w, cond_dram, condT_dram, mask_dram, acc, ident, bias_dram, table=False,
              l2=None, rq_dram=None):
    wq_dram, wkv_dram, wo_dram, nb_dram = w
    with ExitStack() as ctx:
        kA = k.sb(name + "_kA", [P, B, S], F32R, ctx=ctx)
        kB = k.sb(name + "_kB", [P, B, S], F32R, ctx=ctx)
        V = k.sb(name + "_V", [P, B, TB, 2 * DH], F32R, ctx=ctx)
        SNG = k.sb(name + "_SNG", [P, NT, HEADS], ctx=ctx)
        RN = k.sb(name + "_RN", [P, NT, HEADS], ctx=ctx)
        WO = k.sb(name + "_WO", [P, HEADS * D], ctx=ctx)
        A = [k.sb(f"{name}_A{i}", [P, TOK], F32R, ctx=ctx) for i in range(HG)]
        Bq = [k.sb(f"{name}_B{i}", [P, TOK], F32R, ctx=ctx) for i in range(HG)]
        nv = k.sb(name + "_nvs", [P, D], ctx=ctx)
        with ExitStack() as inner:
            rq = None
            if l2:
                rq = k.sb(name + "_rq", [P, NT, HEADS], ctx=inner)
                query_norms(k, name + "_qn", xT, wq_dram, rq, rq_dram, ident)
            keys_and_values(k, name + "_kv", xT, wq_dram, wkv_dram, cond_dram, condT_dram, nb_dram, mask_dram,
                            wo_dram, ident, kA, kB, V, SNG, WO, rq, Bq, nv, acc, table, l2)
        heads_loop(k, name, xT, wq_dram, acc, ident, bias_dram, table, rq_dram, kA, kB, V, SNG, WO, RN, A, Bq)
        null_values(k, name + "_nv", acc, RN, nv, ident)


def query_norms(k, name, xT, wq_dram, rq, rq_dram, ident):
    nc = k.nc
    loaded, made, squared, summed, small, turned, taken, stored = (
        k.sem(f"{name}_{n}") for n in ("loaded", "made", "squared", "summed", "small", "turned", "taken",
                                       "stored"))
    HALF = HEADS // 2
    UNITS = 2 * NT
    with ExitStack() as ctx:
        wq = k.sb(name + "_wq", [P, KD, HEADS * DH], ctx=ctx)
        sq = [k.sb(f"{name}_sq{i}", [P, HALF, DH], ctx=ctx) for i in range(2)]
        norm = k.sb(name + "_norm", [P, NT, HEADS], ctx=ctx)
        rqT = k.sb(name + "_rqT", [HEADS, TOK], ctx=ctx)
        qps = [k.ps(f"{name}_q{i}", [P, HALF, DH], ctx) for i in range(4)]
        tps = [k.ps(f"{name}_t{i}", [HEADS, CH], ctx) for i in range(4)]
        with nc.Block() as block:
            @block.sync
            def _(sp):
                sp.dma_start(wq[:], wq_dram).then_inc(loaded, 16)
                for n in range(NCH):
                    sp.wait_ge(taken, n + 1)
                    sp.dma_start(rq_dram[:, n * CH:(n + 1) * CH], rqT[:, n * CH:(n + 1) * CH]).then_inc(stored, 16)
                sp.wait_ge(stored, 16 * NCH)

            @block.tensor
            def _(pe):
                pe.wait_ge(loaded, 16)
                for n in range(UNITS):
                    if n >= 4:
                        pe.wait_ge(squared, n - 3)
                    for c in range(KD):
                        last = nc.tensor.matmul(qps[n % 4][:], xT[:, c, (n // 2) * P:(n // 2 + 1) * P],
                                                wq[:, c, (n % 2) * CH:(n % 2 + 1) * CH],
                                                start=(c == 0), stop=(c == KD - 1))
                    last.then_inc(made, 1)
                pe.wait_ge(small, 3)
                for t in range(NT):
                    last = nc.tensor.transpose(tps[t // 4][:, (t % 4) * P:(t % 4 + 1) * P], rq[:, t, :],
                                               ident[:])
                    if t % 4 == 3:
                        last.then_inc(turned, 1)

            @block.scalar
            def _(act):
                for n in range(UNITS):
                    act.wait_ge(made, n + 1)
                    if n >= 2:
                        act.wait_ge(summed, n - 1)
                    nc.scalar.activation(sq[n % 2][:], qps[n % 4][:], ACT.Square).then_inc(squared, 1)
                act.wait_ge(summed, UNITS)
                nc.scalar.activation(rq[:], norm[:], ACT.Sqrt).then_inc(small, 1)
                for n in range(NCH):
                    act.wait_ge(turned, n + 1)
                    nc.scalar.activation(rqT[:, n * CH:(n + 1) * CH], tps[n][:], ACT.Copy).then_inc(taken, 1)

            @block.vector
            def _(dve):
                for n in range(UNITS):
                    dve.wait_ge(squared, n + 1)
                    nc.vector.reduce_sum(norm[:, n // 2, (n % 2) * HALF:(n % 2 + 1) * HALF], sq[n % 2][:],
                                         AX.X).then_inc(summed, 1)
                dve.wait_ge(small, 1)
                nc.vector.tensor_scalar(norm[:], rq[:], 1e-12, None, ALU.max).then_inc(small, 1)
                dve.wait_ge(small, 2)
                nc.vector.reciprocal(rq[:], norm[:]).then_inc(small, 1)


def null_values(k, name, acc, RN, nv, ident):
    nc = k.nc
    zeroed, turned, taken, made, added = (k.sem(f"{name}_{n}") for n in ("zeroed", "turned", "taken", "made",
                                                                         "added"))
    with ExitStack() as ctx:
        RNT = k.sb(name + "_RNT", [P, TOK], ctx=ctx)
        tps = [k.ps(f"{name}_t{i}", [HEADS, CH], ctx) for i in range(4)]
        out = [k.ps(f"{name}_out{i}", [P, 2, D], ctx) for i in range(4)]
        with nc.Block() as block:
            @block.gpsimd
            def _(pool):
                for n in range(NCH):
                    nc.gpsimd.memset(RNT[:, n * CH:(n + 1) * CH], 0.0).then_inc(zeroed, 1)

            @block.tensor
            def _(pe):
                for n in range(NCH):
                    for t in range(4):
                        last = nc.tensor.transpose(tps[n][:, t * P:(t + 1) * P], RN[:, 4 * n + t, :], ident[:])
                    last.then_inc(turned, 1)
                for t in range(NT):
                    if t % 4 == 0:
                        pe.wait_ge(taken, t // 4 + 1)
                    if t % 2 == 0 and t >= 8:
                        pe.wait_ge(added, t // 2 - 3)
                    last = nc.tensor.matmul(out[t // 2 % 4][:, t % 2, :], RNT[:, t * P:(t + 1) * P], nv[:],
                                            start=True, stop=True)
                    if t % 2:
                        last.then_inc(made, 1)

            @block.scalar
            def _(act):
                for n in range(NCH):
                    act.wait_ge(zeroed, n + 1)
                    act.wait_ge(turned, n + 1)
                    nc.scalar.activation(RNT[0:HEADS, n * CH:(n + 1) * CH], tps[n][:],
                                         ACT.Copy).then_inc(taken, 1)

            @block.vector
            def _(dve):
                for t in range(0, NT, 2):
                    dve.wait_ge(made, t // 2 + 1)
                    nc.vector.tensor_tensor(acc[:, t:t + 2, :], acc[:, t:t + 2, :], out[t // 2 % 4][:],
                                            ALU.add).then_inc(added, 1)


def keys_and_values(k, name, xT, wq_dram, wkv_dram, cond_dram, condT_dram, nb_dram, mask_dram, wo_dram,
                    ident, kA, kB, V, SNG, WO, rq, Bq, nv, acc, table, l2):
    nc = k.nc
    scale = 8.0 if l2 else DH ** -0.5
    NB = B * TB
    loaded, dve_done, act_done, mm, pool_done = (k.sem(f"{name}_{s}") for s in
                                                 ("loaded", "dve", "act", "mm", "pool"))
    with ExitStack() as ctx:
        cond = k.sb(name + "_cond", [P, 2, DH], ctx=ctx)
        nb = k.sb(name + "_nb", [P, HEADS], ctx=ctx)
        SN = k.sb(name + "_SN", [P, NT, HEADS], ctx=ctx)
        wq = k.sb(name + "_wq", [P, KD, HEADS * DH], ctx=ctx)
        wkv = k.sb(name + "_wkv", [P, KD, 2 * DH], ctx=ctx)
        prod = k.sb(name + "_prod", [P, KD, HEADS * DH], ctx=ctx)
        U = k.sb(name + "_U", [P, KD * HEADS], ctx=ctx)
        kn = k.sb(name + "_kn", [P, DH], ctx=ctx)
        qk = k.sb(name + "_qk", [P, 2, DH], ctx=ctx)
        sq = k.sb(name + "_sq", [P, NB, DH], ctx=ctx)
        n1 = k.sb(name + "_n1", [P, NB], ctx=ctx)
        n2 = k.sb(name + "_n2", [P, NB], ctx=ctx)
        kf = k.sb(name + "_kf", [P, NB, DH], ctx=ctx)
        sA = k.sb(name + "_sA", [P, NB, 2 * DH], F32R, ctx=ctx)
        sB = k.sb(name + "_sB", [P, NB, 2 * DH], F32R, ctx=ctx)
        mrow = k.sb(name + "_mrow", [P, B, S], mask_dram.dtype, ctx=ctx)
        kvps = [k.ps(f"{name}_kvps{i}", [P, 4, 2 * DH], ctx) for i in range(4)]
        snps = k.ps(name + "_snps", [P, NT, HEADS], ctx)
        tps = [k.ps(f"{name}_tps{i}", [P, 4, P], ctx) for i in range(2)]
        wkv_loaded = k.sem(name + "_wkv_loaded")
        n_loads = 4 + 2 * bool(l2)

        xk = k.sb(name + "_xk", [P, KD, TOK], ctx=ctx) if table else xT
        column = k.sb(name + "_column", [DH, 1], ctx=ctx)
        VN = k.sb(name + "_VN", [P, HEADS, HEADS], ctx=ctx)
        nvps = k.ps(name + "_nvps", [HEADS, D], ctx)
        column_loaded, vn_zero, vn_placed, nv_made, set_up = (
            k.sem(f"{name}_{n}") for n in ("column_loaded", "vn_zero", "vn_placed", "nv_made", "set_up"))
        turned_round, wo_loaded = k.sem(name + "_turned_round"), k.sem(name + "_wo_loaded")

        with nc.Block() as block:
            @block.sync
            def _(sp):
                sp.dma_start(wkv[:], wkv_dram).then_inc(wkv_loaded, 16)
                sp.dma_start(cond[:], cond_dram.partition_broadcast(P)).then_inc(loaded, 16)
                sp.dma_start(nb[:], nb_dram.partition_broadcast(P)).then_inc(loaded, 16)
                sp.dma_start(wq[:], wq_dram).then_inc(loaded, 16)
                sp.dma_start(mrow[DH:DH + 1, :, :], mask_dram[None, :, :]).then_inc(loaded, 16)
                sp.dma_start(column[:], condT_dram[:, 1:2], allow_slow_non_contiguous=True).then_inc(column_loaded, 16)
                sp.dma_start(WO[:], wo_dram).then_inc(wo_loaded, 16)
                if l2:
                    for n in range(2):
                        sp.dma_start(qk[:, n, :], l2[n].partition_broadcast(P)).then_inc(loaded, 16)
                sp.wait_ge(wo_loaded, 16)

            @block.gpsimd
            def _(pool):
                nc.gpsimd.memset(sB[:].bitcast(F32), 0.0).then_inc(pool_done, 1)
                nc.gpsimd.memset(VN[:], 0.0).then_inc(vn_zero, 1)
                nc.gpsimd.memset(nv[:], 0.0).then_inc(vn_zero, 1)
                pool.wait_ge(vn_zero, 2)
                for h in range(HG):
                    nc.gpsimd.memset(Bq[h][DH:P, :].bitcast(F32), 0.0).then_inc(set_up, 1)
                pool.wait_ge(set_up, 2)
                for h in range(HG):
                    nc.gpsimd.memset(Bq[h][DH:DH + 1, :].bitcast(F32), 1.0).then_inc(set_up, 1)
                pool.wait_ge(set_up, 4)
                nc.gpsimd.memset(acc[:], 0.0)

            @block.tensor
            def _(pe):
                pe.wait_ge(wkv_loaded, 16)
                if table:
                    pe.wait_ge(turned_round, KD * B)
                for n in range(NB):
                    for c in range(KD):
                        last = nc.tensor.matmul(kvps[n // 4][:, n % 4, :], xk[:, c, n * P:(n + 1) * P],
                                                wkv[:, c, :], start=(c == 0), stop=(c == KD - 1))
                last.then_inc(mm, 1)
                pe.wait_ge(pool_done, 2)
                for t in range(NT):
                    for c in range(KD):
                        last = nc.tensor.matmul(snps[:, t, :], xT[:, c, t * P:(t + 1) * P],
                                                U[:, c * HEADS:(c + 1) * HEADS],
                                                start=(c == 0), stop=(c == KD - 1))
                last.then_inc(mm, 1)
                pe.wait_ge(wo_loaded, 16)
                pe.wait_ge(vn_placed, 1)
                for h in range(HEADS):
                    last = nc.tensor.matmul(nvps[:], VN[:, h, :], WO[:, h * D:(h + 1) * D],
                                            start=(h == 0), stop=(h == HEADS - 1))
                last.then_inc(nv_made, 1)
                pe.wait_ge(pool_done, 3)
                for g in range(2 * NB // 4):
                    src = (sA if g < NB // 4 else sB)[:].bitcast(F32)
                    if g >= 2:
                        pe.wait_ge(act_done, g - 1)
                    for j in range(4):
                        last = nc.tensor.transpose(tps[g % 2][:, j, :], src[:, (g % (NB // 4)) * 4 + j, :],
                                                   ident[:])
                    last.then_inc(mm, 1)

            squares, roots = k.sem(name + "_squares"), k.sem(name + "_roots")

            @block.scalar
            def _(act):
                if table:
                    for c in range(KD):
                        for b in range(B):
                            row = xT[:, c, :].rearrange("p (b s) -> p b s", b=B)[:, b, ::-1]
                            nc.scalar.activation(xk[:, c, b * S:(b + 1) * S], row,
                                                 ACT.Copy).then_inc(turned_round, 1)
                if l2:
                    act.wait_ge(mm, 1)
                    for i in range(4):
                        nc.scalar.activation(sq[:, 4 * i:4 * i + 4, :], kvps[i][:, :, 0:DH],
                                             ACT.Square).then_inc(squares, 1)
                    act.wait_ge(roots, 1)
                    nc.scalar.activation(n2[:, 0:1], n1[:, 0:1], ACT.Sqrt).then_inc(roots, 1)
                    act.wait_ge(roots, 3)
                    nc.scalar.activation(n2[:], n1[:], ACT.Sqrt).then_inc(roots, 1)
                for g in range(2 * NB // 4):
                    act.wait_ge(mm, g + 3)
                    dst = (kA if g < NB // 4 else kB)[:].rearrange("p b s -> p (b s)")
                    at = (g % (NB // 4)) * 4 * P
                    nc.scalar.activation(dst[:, at:at + 4 * P].rearrange("p (j n) -> p j n", j=4),
                                         tps[g % 2][:], ACT.Copy).then_inc(act_done, 1)

            @block.vector
            def _(dve):
                s = Steps(dve, dve_done)
                dve.wait_ge(column_loaded, 16)
                dve.wait_ge(vn_zero, 2)
                diagonal = VN[0:DH].rearrange("p a b -> p (a b)")[:, ::HEADS + 1]
                nc.vector.tensor_copy(diagonal, bc(column[:], [DH, HEADS])).then_inc(vn_placed, 1)
                dve.wait_ge(loaded, 16 * n_loads)
                if l2:
                    s.then(nc.vector.tensor_tensor(kn[:], cond[:, 0, :], cond[:, 0, :], ALU.mult))
                    nc.vector.reduce_sum(n1[:, 0:1], kn[:], AX.X).then_inc(roots, 1)
                    dve.wait_ge(roots, 2)
                    s.then(nc.vector.tensor_scalar(n1[:, 0:1], n2[:, 0:1], 1e-12, None, ALU.max))
                    s.then(nc.vector.reciprocal(n2[:, 0:1], n1[:, 0:1]))
                    s.then(nc.vector.tensor_tensor(qk[:, 0, :], qk[:, 0, :], qk[:, 1, :], ALU.mult))
                    s.then(nc.vector.tensor_scalar(qk[:, 0, :], qk[:, 0, :], scale, None, ALU.mult))
                    s.then(nc.vector.tensor_scalar(kn[:], cond[:, 0, :], n2[:, 0:1], None, ALU.mult))
                    s.then(nc.vector.tensor_tensor(kn[:], kn[:], qk[:, 0, :], ALU.mult))
                else:
                    s.then(nc.vector.tensor_scalar(kn[:], cond[:, 0, :], scale, None, ALU.mult))
                knb = bc(kn[:, None, :], [P, KD * HEADS, DH])
                s.then(nc.vector.tensor_tensor(prod[:].rearrange("p c (h d) -> p (c h) d", d=DH),
                                               wq[:].rearrange("p c (h d) -> p (c h) d", d=DH),
                                               knb, ALU.mult))
                s.then(nc.vector.reduce_sum(U[:], prod[:].rearrange("p c (h d) -> p (c h) d", d=DH), AX.X))
                dve.wait_ge(pool_done, 1)
                dve.sem_inc(pool_done, 1)
                dve.wait_ge(mm, 1)
                if l2:
                    dve.wait_ge(squares, 4)
                    nc.vector.reduce_sum(n1[:], sq[:], AX.X).then_inc(roots, 1)
                    dve.wait_ge(roots, 4)
                    s.then(nc.vector.tensor_scalar(n1[:], n2[:], 1e-12, None, ALU.max))
                    s.then(nc.vector.reciprocal(n2[:], n1[:]))
                for i in range(4):
                    if l2:
                        s.did(nc.vector.tensor_tensor(kf[:, 4 * i:4 * i + 4, :], kvps[i][:, :, 0:DH],
                                                      bc(n2[:, 4 * i:4 * i + 4, None], [P, 4, DH]), ALU.mult))
                    else:
                        s.did(nc.vector.tensor_scalar(kf[:, 4 * i:4 * i + 4, :], kvps[i][:, :, 0:DH],
                                                      scale, None, ALU.mult))
                    s.did(nc.vector.tensor_copy(V[:, i // 2, 4 * (i % 2):4 * (i % 2) + 4, 0:DH],
                                                kvps[i][:, :, DH:2 * DH]))
                s.settle()
                if l2:
                    s.then(nc.vector.tensor_tensor(kf[:], kf[:], bc(qk[:, 0:1, :], [P, NB, DH]), ALU.mult))
                s.did(nc.vector.tensor_copy(sA[:, :, 0:DH], kf[:]))
                s.did(nc.vector.tensor_copy(sA[:, :, DH:2 * DH], kf[:]))
                for i in range(4):
                    v = V[:, i // 2, 4 * (i % 2):4 * (i % 2) + 4, :]
                    s.did(nc.vector.tensor_tensor(v[:, :, DH:2 * DH], kvps[i][:, :, DH:2 * DH],
                                                  v[:, :, 0:DH].bitcast(F32), ALU.subtract))
                s.settle()
                nc.vector.tensor_tensor(sB[:, :, 0:DH], kf[:], sA[:, :, 0:DH].bitcast(F32),
                                        ALU.subtract).then_inc(pool_done, 1)
                dve.wait_ge(mm, 2)
                nulls = snps[:]
                if l2:
                    s.then(nc.vector.tensor_tensor(SN[:], snps[:], rq[:], ALU.mult))
                    nulls = SN[:]
                nc.vector.scalar_tensor_tensor(out=SNG[:], in0=nulls, scalar=-1.0,
                                               in1=bc(nb[:, None, :], [P, NT, HEADS]),
                                               op0=ALU.mult, op1=ALU.subtract)
                dve.wait_ge(act_done, 2 * NB // 4)
                for b in range(B):
                    row = mrow[DH:DH + 1, b, ::-1] if table else mrow[DH:DH + 1, b, :]
                    nc.vector.tensor_scalar(kB[DH:DH + 1, b, :], row, 1.0, -FAR, ALU.subtract, ALU.mult)
                dve.wait_ge(nv_made, 1)
                nc.vector.tensor_copy(nv[0:HEADS, :], nvps[:])


class Turn:

    def __init__(self, g, ahead=0):
        self.g, self.ahead = g, ahead

    def count(self, per_turn, c):
        return per_turn * self.g + (per_turn * self.ahead + c)

    def part(self, width, offset=0, size=None):
        at = self.count(width, offset)
        size = size or width
        return slice(at, at + size) if isinstance(at, int) else bass.ds(at, size)

    def later(self, n=1):
        return Turn(self.g, self.ahead + n)


def in_turns(eng, early, late):
    early(Turn(0))
    with eng.Fori(0, NG - 1) as g:
        late(Turn(g), True)
        early(Turn(g, 1))
    late(Turn(NG - 1), False)


def heads_loop(k, name, xT, wq_dram, acc, ident, bias_dram, table, rq_dram, kA, kB, V, SNG, WO, RN, A, Bq):
    nc = k.nc
    norm_q = rq_dram is not None
    DUOS, UNITS = TB * B, TB * B * HG
    pairs = [(d // B + 2) // 2 for d in range(DUOS)]
    first = [sum(pairs[:d]) for d in range(DUOS)]
    BANKS = sum(pairs)
    QUERY_STEPS = {1: (0, 1), 3: (0, 3), 9: (1, 0), 11: (1, 2)}
    nth_of_chunk = {0: 0, 2: 1, 1: 2, 3: 3}

    def score_banks(d):
        return [(d, h, j) for h in range(HG) for j in range(1 if d // B + 1 <= CH // P else 2)]

    order = []
    for step in range(-2, DUOS - 2):
        order += score_banks(step + 2)
        if step in QUERY_STEPS:
            order.append(("queries",) + QUERY_STEPS[step])
    SLOTS = len(order)
    place = {what: 3 + n for n, what in enumerate(order)}
    LEAD = 2

    def rotation(count):
        which = [n % 3 for n in range(count)]
        if count % 3 == 1:
            which[-1] = 1
        ago = [next(m for m in range(1, 6) if which[n - m] == which[n]) for n in range(count)]
        return which, ago

    score_bank, score_ago = rotation(SLOTS)
    turn_bank, turn_ago = rotation(BANKS)

    def emptied_by(d, n):
        before = sum(len(score_banks(e % DUOS)) for e in range(d + 2)) + sum(e < d for e in QUERY_STEPS)
        if n < 0:
            return before
        done = len(score_banks((d + 2) % DUOS)) * (n + 1) // pairs[d]
        return before + done + (d in QUERY_STEPS and n == pairs[d] - 1)

    def turned_by(d, n):
        if n < 0 and d == 0:
            return 1
        if n < 0:
            return turned_by(d - 1, pairs[d - 1] - 1)
        return min(first[d] + n + 2, first[d] + pairs[d] + pairs[(d + 1) % DUOS] - 1) + 1

    def share(items, n, parts):
        return items[len(items) * n // parts:len(items) * (n + 1) // parts]

    names = ("filled", "emptied", "exp", "t", "hi", "lo", "pv", "o", "proj", "scaled", "added", "head0", "dn",
             "pn", "tot", "rec", "rn", "sng", "q_lo", "q_hi", "q_b", "hidden", "wq",
             "dve_mark", "pool_mark", "rq0", "rq1", "bias0", "bias1",
             "bias2", "bias3")
    (filled, emptied, exp_done, t_done, hi_done, lo_done, pv_done, o_taken, proj_done, scaled, added, head0_added,
     dn_done, pn_done, tot_done, rec_done, rn_done, sng_done, q_lo, q_hi, q_b, hidden, wq_loaded, dve_mark, pool_mark, rq0, rq1, bias0, bias1, bias2, bias3) = (k.sem(f"{name}_{n}") for n in names)
    rq_loaded, bias_loaded = [rq0, rq1], [bias0, bias1, bias2, bias3]
    BB = len(bias_loaded)

    with ExitStack() as ctx:
        wq = k.sb(name + "_wqg", [P, KD, HG * DH], ctx=ctx)
        bt = [k.sb(f"{name}_bt{i}", [P, HG, (TB - BB + i + 1) * P], ctx=ctx) for i in range(BB)]
        pr = [k.sb(f"{name}_p{i}", [P, HG, S], ctx=ctx) for i in range(4)]
        ph = [k.sb(f"{name}_ph{i}", [P, 2, HG * P], F32R, ctx=ctx) for i in range(3)]
        pl = [k.sb(f"{name}_pl{i}", [P, 2, HG * P], F32R, ctx=ctx) for i in range(3)]
        sng = k.sb(name + "_sng", [P, NT, HG], ctx=ctx)
        NM = k.sb(name + "_NM", [P, UNITS], ctx=ctx)
        NMH = k.sb(name + "_NMH", [P, UNITS], ctx=ctx)
        RS = k.sb(name + "_RS", [P, UNITS], ctx=ctx)
        DN = k.sb(name + "_DN", [P, UNITS], ctx=ctx)
        PN = k.sb(name + "_PN", [P, UNITS], ctx=ctx)
        TT = k.sb(name + "_TT", [P, UNITS], ctx=ctx)
        RI = k.sb(name + "_RI", [P, UNITS], ctx=ctx)
        os_ = k.sb(name + "_os", [P, 2, HG * P], ctx=ctx)
        rows_out = k.sb(name + "_rows_out", [P, 2, HG, D], ctx=ctx)
        if norm_q:
            qn = k.sb(name + "_qn", [P, CH], ctx=ctx)
            rqb = [k.sb(f"{name}_rqb{i}", [P, CH], ctx=ctx) for i in range(2)]
        Sps = [k.ps(f"{name}_S{i}", [P, CH], ctx) for i in range(3)]
        Tps = [k.ps(f"{name}_T{i}", [P, 2, HG * P], ctx) for i in range(3)]
        Ops = k.ps(name + "_O", [P, HG * P], ctx)
        Mps = k.ps(name + "_M", [P, HG, D], ctx)

        def widths(i):
            W = (i + 1) * P
            return W, (1 if W <= CH else 2), max(2 * P, W) if W <= CH else W // 2

        def score_cols(i, j):
            W, chunks, n = widths(i)
            lo = S - max(W, 2 * P) if table else 0
            return slice(lo + j * n, lo + (j + 1) * n)

        def wait(eng, sem, value):
            if not isinstance(value, int) or value > 0:
                eng.wait_ge(sem, value)

        def neighbour(T, d, by, more=True):
            if d + by < 0:
                return None if isinstance(T.g, int) and T.g + T.ahead == 0 else (T.later(-1), d + by + DUOS)
            if d + by < DUOS:
                return T, d + by
            return (T.later(), d + by - DUOS) if more else None

        def query_place(T, ahead, chunk):
            return T.count(SLOTS, place[("queries", ahead, chunk)])

        def query_bank(T, ahead, chunk):
            at = place[("queries", ahead, chunk)]
            return score_bank[at - 3], T.count(SLOTS, at)

        def unit(d, h):
            return 4 * (d // B) + HG * (d % B) + h

        with nc.Block() as block:
            @block.sync
            def _(sp):
                def load_bias(T, i):
                    before = neighbour(T, B * i + 1, -BB * B)
                    if before:
                        sp.wait_ge(emptied, before[0].count(SLOTS, place[score_banks(before[1])[-1]]))
                    W = (i + 1) * P
                    src = (bias_dram[T.part(1), :, :, 0:W].rearrange("o p h s -> (o p) h s") if table
                           else bias_dram[T.part(HG), i * P:(i + 1) * P, 0:W].rearrange("h p s -> p h s"))
                    sp.dma_start(bt[i % BB][:, :, 0:W], src).then_inc(bias_loaded[i % BB], 16)

                def load_norms(T, chunk, buf, freed):
                    if norm_q:
                        if freed is not None:
                            sp.wait_ge(emptied, freed)
                        for h in range(HG):
                            sp.dma_start(rqb[buf][h * DH:(h + 1) * DH, :],
                                         rq_dram[T.part(HG, h, 1), chunk * CH:(chunk + 1) * CH]
                                         .broadcast_to([DH, CH])).then_inc(rq_loaded[buf], 16)

                def early(T):
                    first_turn = isinstance(T.g, int)
                    load_norms(T, 1, 0, 1 if first_turn else query_place(T.later(-1), 1, 0))
                    load_norms(T, 3, 1, 2 if first_turn else query_place(T.later(-1), 1, 2))
                    for i in range(BB, TB):
                        load_bias(T, i)

                def load_queries_weights(T):
                    sp.dma_start(wq[:], wq_dram[:, :, T.part(HG * DH)]).then_inc(wq_loaded, 16)

                def late(T, more):
                    if more:
                        sp.wait_ge(filled, query_place(T, 0, 3))
                        load_queries_weights(T.later())
                        load_norms(T.later(), 0, 0, query_place(T, 0, 1))
                        load_norms(T.later(), 2, 1, query_place(T, 0, 3))
                        for i in range(BB):
                            load_bias(T.later(), i)

                load_queries_weights(Turn(0))
                load_norms(Turn(0), 0, 0, None)
                load_norms(Turn(0), 2, 1, None)
                for i in range(BB):
                    load_bias(Turn(0), i)
                in_turns(sp, early, late)

            @block.gpsimd
            def _(pool):
                far = pool.to_reg(FAR)

                def hide_later_keys(T, i):
                    if not table:
                        wait_apart(pool, bias_loaded[i % BB], T.count(16 * (TB // BB), 16 * (i // BB + 1)),
                                   pool_mark)
                        d = bt[i % BB][:, :, i * P:(i + 1) * P]
                        nc.gpsimd.affine_select(out=d, in_=d, compare_op=ALU.is_ge, fill=far, base=0,
                                                pattern=[[0, HG], [-1, P]],
                                                channel_multiplier=1).then_inc(hidden, 1)

                def second_operand(T, chunk, nth):
                    for h in range(HG):
                        cols = slice(chunk * CH, (chunk + 1) * CH)
                        wait_apart(pool, q_hi, T.count(4 * HG, HG * nth + h + 1), pool_mark)
                        nc.gpsimd.tensor_copy(Bq[h][0:DH, cols],
                                              A[h][0:DH, cols].bitcast(F32)).then_inc(q_b, 1)

                def add_heads(T, d):
                    pool.wait_ge(scaled, T.count(DUOS, d + 1))
                    rows = acc[:, (d % B) * TB + d // B, :]
                    for h in range(HG):
                        if h:
                            pool.wait_ge(head0_added, T.count(DUOS, d + 1))
                        nc.gpsimd.tensor_tensor(rows, rows, rows_out[:, d % 2, h, :],
                                                ALU.add).then_inc(added if h else head0_added, 1)

                def step(T, d, more=True):
                    before = neighbour(T, d, -1)
                    if d % B:
                        row = neighbour(T, d, 5, more)
                        if row:
                            hide_later_keys(row[0], row[1] // B)
                    if d in QUERY_STEPS:
                        turns, chunk = QUERY_STEPS[d]
                        if turns == 0 or more:
                            second_operand(T.later(turns), chunk, nth_of_chunk[chunk])
                    if before:
                        add_heads(*before)

                def early(T):
                    for d in range(DUOS // 2):
                        step(T, d)

                def late(T, more):
                    for d in range(DUOS // 2, DUOS):
                        step(T, d, more)

                hide_later_keys(Turn(0), 0)
                hide_later_keys(Turn(0), 1)
                hide_later_keys(Turn(0), 2)
                in_turns(pool, early, late)
                add_heads(Turn(NG - 1), DUOS - 1)

            @block.tensor
            def _(pe):
                def queries(T, chunk, bank, freed):
                    if chunk == 0:
                        pe.wait_ge(wq_loaded, T.count(16, 16))
                    wait(pe, emptied, freed)
                    for c in range(KD):
                        last = nc.tensor.matmul(Sps[bank][:], wq[:, c, :],
                                                xT[:, c, chunk * CH:(chunk + 1) * CH],
                                                start=(c == 0), stop=(c == KD - 1))
                    last.then_inc(filled, 1)

                def scores(T, x):
                    d, h, j = order[x]
                    i, b = d // B, d % B
                    W, chunks, n = widths(i)
                    t = b * TB + i
                    if d in (0, TB) and h == 0 and j == 0:
                        nth = 1 if d == 0 else 3
                        pe.wait_ge(q_b, T.count(4 * HG, HG * (nth + 1)))
                        if norm_q:
                            pe.wait_ge(q_lo, T.count(4 * HG, HG * (nth + 1)))
                    wait(pe, emptied, T.count(SLOTS, 3 + x - score_ago[x]))
                    out = Sps[score_bank[x]][:, 0:n]
                    nc.tensor.matmul(out, A[h][:, t * P:(t + 1) * P], kA[:, b, score_cols(i, j)],
                                     start=True, stop=False)
                    last = nc.tensor.matmul(out, Bq[h][:, t * P:(t + 1) * P], kB[:, b, score_cols(i, j)],
                                            start=False, stop=True)
                    last.then_inc(filled, 1)

                def fill(T, x, more=True):
                    if x >= SLOTS:
                        if more:
                            fill(T.later(), x - SLOTS)
                    elif order[x][0] != "queries":
                        scores(T, x)
                    elif order[x][1] == 0 or more:
                        queries(T.later(order[x][1]), order[x][2], score_bank[x],
                                T.count(SLOTS, 3 + x - score_ago[x]))
                    else:
                        pe.wait_ge(filled, T.count(SLOTS, 2 + x))
                        pe.sem_inc(filled, 1)

                def turn(T, at, more=True):
                    if at >= BANKS:
                        if more:
                            turn(T.later(), at - BANKS)
                        return
                    d = max(e for e in range(DUOS) if first[e] <= at)
                    i, n = d // B, at - first[d]
                    if n == 0:
                        pe.wait_ge(exp_done, T.count(UNITS, HG * (d + 1)))
                    wait(pe, lo_done, T.count(BANKS, at + 1 - turn_ago[at]))
                    for jj in range(2):
                        j = 2 * n + jj
                        if j > i:
                            break
                        for h in range(HG):
                            last = nc.tensor.transpose(Tps[turn_bank[at]][:, jj, h * P:(h + 1) * P],
                                                       pr[d % 4][:, h, j * P:(j + 1) * P], ident[:])
                    last.then_inc(t_done, 1)

                def values(T, d, n):
                    i, b = d // B, d % B
                    at = first[d] + n
                    buf = turn_bank[at]
                    if n == 0:
                        wait(pe, o_taken, T.count(DUOS, d))
                    pe.wait_ge(lo_done, T.count(BANKS, at + 1))
                    for jj in range(2):
                        j = 2 * n + jj
                        if j > i:
                            break
                        vj = V[:, b, (TB - 1 - i + j) if table else j, :]
                        nc.tensor.matmul(Ops[:], vj, ph[buf][:, jj, :], start=(j == 0), stop=False)
                        last = nc.tensor.matmul(Ops[:], vj, pl[buf][:, jj, :], start=False, stop=(j == i))
                    last.then_inc(pv_done, 1)

                def project(T, d):
                    pe.wait_ge(o_taken, T.count(DUOS, d + 1))
                    wait(pe, scaled, T.count(DUOS, d))
                    for h in range(HG):
                        last = nc.tensor.matmul(Mps[:, h, :], os_[:, d % 2, h * P:(h + 1) * P],
                                                WO[:, T.part(HG * D, h * D, D)], start=True, stop=True)
                    last.then_inc(proj_done, 1)

                def step(T, d, more=True):
                    before = neighbour(T, d, -1)
                    for n in range(pairs[d]):
                        for x in range(emptied_by(d, n - 1) + LEAD, emptied_by(d, n) + LEAD):
                            fill(T, x, more)
                        for at in range(turned_by(d, n - 1), turned_by(d, n)):
                            turn(T, at, more)
                        values(T, d, n)
                        if n == 0 and before:
                            project(*before)

                def early(T):
                    for d in range(DUOS // 2):
                        step(T, d)

                def late(T, more):
                    for d in range(DUOS // 2, DUOS):
                        step(T, d, more)

                queries(Turn(0), 0, 2, 0)
                queries(Turn(0), 2, 1, 0)
                pe.wait_ge(emptied, 2)
                for x in range(emptied_by(0, -1) + LEAD):
                    fill(Turn(0), x)
                turn(Turn(0), 0)
                in_turns(pe, early, late)
                project(Turn(NG - 1), DUOS - 1)

            @block.scalar
            def _(act):
                def high_queries(T, chunk, bank, at):
                    cols = slice(chunk * CH, (chunk + 1) * CH)
                    if norm_q:
                        act.wait_ge(emptied, at)
                    else:
                        act.wait_ge(filled, at)
                    src = qn if norm_q else Sps[bank]
                    for h in range(HG):
                        nc.scalar.activation(A[h][0:DH, cols], src[h * DH:(h + 1) * DH, :],
                                             ACT.Copy).then_inc(q_hi, 1)

                def exponentials(T, d, h):
                    act.wait_ge(emptied, T.count(SLOTS, place[[x for x in score_banks(d) if x[1] == h][-1]]))
                    u = unit(d, h)
                    p = pr[d % 4][:, h, 0:(d // B + 1) * P]
                    nc.scalar.activation(p, p, ACT.Exp, bias=NM[:, u:u + 1], scale=-1.0,
                                         accum_out=RS[:, u:u + 1]).then_inc(exp_done, 1)

                def high_part(T, d, n):
                    at = first[d] + n
                    js = min(2, d // B + 1 - 2 * n)
                    wait(act, pv_done, T.count(BANKS, at + 1 - turn_ago[at]))
                    act.wait_ge(t_done, T.count(BANKS, at + 1))
                    buf = turn_bank[at]
                    nc.scalar.activation(ph[buf][:, 0:js, :], Tps[buf][:, 0:js, :],
                                         ACT.Copy).then_inc(hi_done, 1)

                def null_exponential(T, i):
                    act.wait_ge(dn_done, T.count(TB, i + 1))
                    nc.scalar.activation(PN[:, 4 * i:4 * i + 4], DN[:, 4 * i:4 * i + 4],
                                         ACT.Exp).then_inc(pn_done, 1)

                def take_outputs(T, d):
                    wait(act, proj_done, T.count(DUOS, d - 1))
                    act.wait_ge(pv_done, T.count(BANKS, first[d] + pairs[d]))
                    nc.scalar.activation(os_[:, d % 2, :], Ops[:], ACT.Copy).then_inc(o_taken, 1)

                def normalise_rows(T, d):
                    act.wait_ge(rec_done, T.count(TB, d // B + 1))
                    wait(act, added, T.count(DUOS, d - 1))
                    act.wait_ge(proj_done, T.count(DUOS, d + 1))
                    for h in range(HG):
                        u = unit(d, h)
                        last = nc.scalar.activation(rows_out[:, d % 2, h, :], Mps[:, h, :], ACT.Copy,
                                                    scale=RI[:, u:u + 1])
                    last.then_inc(scaled, 1)

                def step(T, d, more=True):
                    ahead, before = neighbour(T, d, 2, more), neighbour(T, d, -1)
                    for n in range(pairs[d]):
                        high_part(T, d, n)
                        if n == 0 and before:
                            take_outputs(*before)
                        if n == 0 and d % B == 0:
                            null_exponential(T, d // B)
                        if ahead:
                            for h in share(range(HG), n, pairs[d]):
                                exponentials(*ahead, h)
                    if d in QUERY_STEPS:
                        turns, chunk = QUERY_STEPS[d]
                        if turns == 0 or more:
                            high_queries(T.later(turns), chunk, *query_bank(T, turns, chunk))
                    if before:
                        normalise_rows(*before)

                def early(T):
                    for d in range(DUOS // 2):
                        step(T, d)

                def late(T, more):
                    for d in range(DUOS // 2, DUOS):
                        step(T, d, more)

                for nth, (chunk, bank) in enumerate(((0, 2), (2, 1))):
                    high_queries(Turn(0), chunk, bank, nth + 1)
                    cols = slice(chunk * CH, (chunk + 1) * CH)
                    for h in range(HG):
                        act.wait_ge(q_hi, HG * nth + h + 1)
                        nc.scalar.activation(Bq[h][0:DH, cols], A[h][0:DH, cols].bitcast(F32),
                                             ACT.Copy).then_inc(q_b, 1)
                for d in range(2):
                    for h in range(HG):
                        exponentials(Turn(0), d, h)
                in_turns(act, early, late)
                take_outputs(Turn(NG - 1), DUOS - 1)
                normalise_rows(Turn(NG - 1), DUOS - 1)

            @block.vector
            def _(dve):
                def queries_of(T, chunk, bank, at):
                    slot, nth = Sps[bank], nth_of_chunk[chunk]
                    cols = slice(chunk * CH, (chunk + 1) * CH)
                    if norm_q:
                        wait(dve, q_lo, T.count(4 * HG, HG * nth))
                        dve.wait_ge(rq_loaded[nth % 2], T.count(4 * 16, 2 * 16 * (nth // 2 + 1)))
                        dve.wait_ge(filled, at)
                        nc.vector.tensor_tensor(qn[:], slot[:], rqb[nth % 2][:], ALU.mult).then_inc(emptied, 1)
                    else:
                        for h in range(HG):
                            dve.wait_ge(q_hi, T.count(4 * HG, HG * nth + h + 1))
                            last = nc.vector.tensor_tensor(A[h][DH:P, cols], slot[h * DH:(h + 1) * DH, :],
                                                           A[h][0:DH, cols].bitcast(F32), ALU.subtract)
                            last.then_inc(emptied if h == HG - 1 else q_lo, 1)

                def low_queries(T, chunk):
                    cols = slice(chunk * CH, (chunk + 1) * CH)
                    for h in range(HG):
                        dve.wait_ge(q_hi, T.count(4 * HG, HG * nth_of_chunk[chunk] + h + 1))
                        nc.vector.tensor_tensor(A[h][DH:P, cols], qn[h * DH:(h + 1) * DH, :],
                                                A[h][0:DH, cols].bitcast(F32), ALU.subtract).then_inc(q_lo, 1)

                def null_scores(T):
                    wait(dve, dn_done, T.count(TB, 0))
                    nc.vector.tensor_copy(sng[:], SNG[:, :, T.part(HG)]).then_inc(sng_done, 1)

                def add_bias_and_max(T, d, h, j):
                    i, b = d // B, d % B
                    W, chunks, n = widths(i)
                    at = place[(d, h, j)]
                    if d == 0 and h == 0:
                        dve.wait_ge(sng_done, T.count(1, 1))
                    if h == 0 and j == 0:
                        before = neighbour(T, d, -4)
                        if before:
                            dve.wait_ge(t_done, before[0].count(BANKS, first[before[1]] + pairs[before[1]]))
                    if h == 0 and b == 0 and j == 0:
                        if table:
                            dve.wait_ge(bias_loaded[i % BB], T.count(16 * (TB // BB), 16 * (i // BB + 1)))
                        else:
                            dve.wait_ge(hidden, T.count(TB, i + 1))
                    if j:
                        dve.wait_ge(emptied, T.count(SLOTS, at - 1))
                    wait_apart(dve, filled, T.count(SLOTS, at), dve_mark)
                    off = P if (table and i == 0) else 0
                    nn = min(n, W)
                    u = unit(d, h)
                    cols = slice(j * nn, (j + 1) * nn)
                    nc.vector.tensor_tensor_reduce(
                        out=pr[d % 4][:, h, cols], in0=Sps[score_bank[at - 3]][:, off:off + nn],
                        in1=bt[i % BB][:, h, cols], scale=-1.0,
                        scalar=NMH[:, u:u + 1] if j else sng[:, b * TB + i, h:h + 1],
                        op0=ALU.add, op1=ALU.min,
                        accum_out=(NM if j == chunks - 1 else NMH)[:, u:u + 1]).then_inc(emptied, 1)

                def low_part(T, d, n):
                    at = first[d] + n
                    js = min(2, d // B + 1 - 2 * n)
                    dve.wait_ge(hi_done, T.count(BANKS, at + 1))
                    buf = turn_bank[at]
                    nc.vector.tensor_tensor(pl[buf][:, 0:js, :], Tps[buf][:, 0:js, :],
                                            ph[buf][:, 0:js, :].bitcast(F32),
                                            ALU.subtract).then_inc(lo_done, 1)

                def null_difference(T, i):
                    dve.wait_ge(emptied, T.count(SLOTS, place[score_banks(B * i + 1)[-1]]))
                    nc.vector.tensor_tensor(
                        DN[:, 4 * i:4 * i + 4].rearrange("p (b h) -> p b h", b=B),
                        NM[:, 4 * i:4 * i + 4].rearrange("p (b h) -> p b h", b=B),
                        sng[:].rearrange("p (b t) h -> p b t h", b=B)[:, :, i, :],
                        ALU.subtract).then_inc(dn_done, 1)

                def totals(T, i):
                    c = slice(4 * i, 4 * i + 4)
                    dve.wait_ge(exp_done, T.count(UNITS, 4 * (i + 1)))
                    dve.wait_ge(pn_done, T.count(TB, i + 1))
                    nc.vector.tensor_tensor(TT[:, c], RS[:, c], PN[:, c], ALU.add).then_inc(tot_done, 1)

                def reciprocals(T, i):
                    c = slice(4 * i, 4 * i + 4)
                    dve.wait_ge(tot_done, T.count(TB, i + 1))
                    nc.vector.reciprocal(RI[:, c], TT[:, c]).then_inc(rec_done, 1)

                def null_weights(T):
                    dve.wait_ge(rec_done, T.count(TB, TB))
                    nc.vector.tensor_tensor(
                        RN[:, :, T.part(HG)].rearrange("p (b t) h -> p t b h", b=B),
                        PN[:].rearrange("p (t b h) -> p t b h", b=B, h=HG),
                        RI[:].rearrange("p (t b h) -> p t b h", b=B, h=HG), ALU.mult).then_inc(rn_done, 1)

                def step(T, d, more=True):
                    ahead = neighbour(T, d, 2, more)
                    if d == DUOS - 2 and ahead:
                        null_scores(ahead[0])
                    if norm_q and d - 1 in QUERY_STEPS:
                        turns, chunk = QUERY_STEPS[d - 1]
                        if turns == 0 or more:
                            low_queries(T.later(turns), chunk)
                    for n in range(pairs[d]):
                        if ahead:
                            for bank in share(score_banks(ahead[1]), n, pairs[d]):
                                add_bias_and_max(ahead[0], *bank)
                        low_part(T, d, n)
                        if n == 0 and d % B == 0:
                            totals(T, d // B)
                    if d in QUERY_STEPS:
                        turns, chunk = QUERY_STEPS[d]
                        if turns == 0 or more:
                            queries_of(T.later(turns), chunk, *query_bank(T, turns, chunk))
                        else:
                            dve.wait_ge(emptied, query_place(T, turns, chunk) - 1)
                            dve.sem_inc(emptied, 1)
                    if d % B == 0:
                        reciprocals(T, d // B)
                    if d == DUOS - 1:
                        null_weights(T)
                    if d % B and ahead:
                        null_difference(ahead[0], ahead[1] // B)
                def early(T):
                    for d in range(DUOS // 2):
                        step(T, d)

                def late(T, more):
                    for d in range(DUOS // 2, DUOS):
                        step(T, d, more)

                for chunk, bank, at in ((0, 2, 1), (2, 1, 2)):
                    queries_of(Turn(0), chunk, bank, at)
                    if norm_q:
                        low_queries(Turn(0), chunk)
                null_scores(Turn(0))
                for d in range(2):
                    for bank in score_banks(d):
                        add_bias_and_max(Turn(0), *bank)
                null_difference(Turn(0), 0)
                in_turns(dve, early, late)


def load_constants(k, ident, X, x_dram):
    nc = k.nc
    made, loaded = k.sem("const_made"), k.sem("const_loaded")
    with nc.Block() as block:
        @block.sync
        def _(sp):
            sp.dma_start(X[:], x_dram.rearrange("b (i p) d -> p (b i) d", p=P)).then_inc(loaded, 16)
            sp.wait_ge(loaded, 16)

        @block.gpsimd
        def _(pool):
            nc.gpsimd.memset(ident[:], 0.0).then_inc(made, 1)
            pool.wait_ge(made, 1)
            nc.gpsimd.affine_select(out=ident[:], in_=ident[:], compare_op=ALU.not_equal, fill=1.0,
                                    base=0, pattern=[[-1, P]], channel_multiplier=1)


def make_triangle(k, name, upper):
    nc = k.nc
    made = k.sem(name)
    with nc.Block() as block:
        @block.gpsimd
        def _(pool):
            nc.gpsimd.memset(upper[:], 1.0).then_inc(made, 1)
            pool.wait_ge(made, 1)
            nc.gpsimd.affine_select(out=upper[:], in_=upper[:], compare_op=ALU.is_ge, fill=0.0,
                                    base=0, pattern=[[1, P]], channel_multiplier=-1)


def fill(k, name, tile, value):
    nc = k.nc
    with nc.Block() as block:
        @block.gpsimd
        def _(pool):
            nc.gpsimd.memset(tile, value)


def store_rows(k, name, src, out_dram):
    nc = k.nc
    stored = k.sem(name)
    with nc.Block() as block:
        @block.sync
        def _(sp):
            sp.dma_start(out_dram.rearrange("b (i p) d -> p (b i) d", p=P), src[:]).then_inc(stored, 16)
            sp.wait_ge(stored, 16)


def layer0(k, a, X, Y, XT, ident):
    with ExitStack() as ctx:
        shares = k.sb("l0_shares", [P, NT, 10], ctx=ctx)
        fill(k, "l0_ones", shares[:, :, 8:10], 1.0)
        to_feature_major(k, "l0_t", X, XT, ident)
        route(k, "l0_r", XT, a["l0_router"], 8, 2, shares, ident, extra=(a["condT"], a["l0_router_cond"]),
              scale=0.5, soft="all")
        gated_experts(k, "l0_e", XT, a["l0_experts"], 10, Y, shares)
    with ExitStack() as ctx:
        picked = k.sb("l0_picked", [P, NT, 8], ctx=ctx)
        Z = k.sb("l0_z", [P, NT, D], ctx=ctx)
        gamma, beta = k.sb("l0_gamma", [P, D], ctx=ctx), k.sb("l0_beta", [P, D], ctx=ctx)
        to_feature_major(k, "l0_t2", Y, XT, ident)
        route(k, "l0_r2", XT, a["l0_ffn_router"], 4, 1, picked, ident)
        with ExitStack() as inner:
            picked_ffn(k, "l0_f", Y, picked, a["l0_w1"], a["l0_b1"], a["l0_wo"], a["l0_bo"], Z, ident, 4)
        normalise(k, "l0_ln", Z, X, gamma, 1e-12, beta=beta, add_to=X,
                  loads=((gamma, a["l0_ln_gamma"]), (beta, a["l0_ln_beta"])))


def window_views(table_dram):
    return bass.AP(tensor=table_dram.tensor, offset=0,
                   ap=[[HG * TABLE, NG], [1, P], [TABLE, HG], [1, S]])


def layer1_attention(k, a, X, Y, XT, ident, table_dram, rq_dram):
    position_table(k, a, table_dram, ident)
    with ExitStack() as ctx:
        g_in = k.sb("l1_gin", [P, D], ctx=ctx)
        normalise(k, "l1_n", X, Y, g_in, 1e-5, loads=((g_in, a["l1_g_norm"]),))
        to_feature_major(k, "l1_t", Y, XT, ident)
    attention(k, "l1_a", XT, (a["l1_wq"], a["l1_wkv"], a["l1_wout"], a["l1_null_attn_bias"]), a["cond"],
              a["condT"], a["mask1"], Y, ident, window_views(table_dram), table=True,
              l2=(a["l1_q_scale"], a["l1_k_scale"]), rq_dram=rq_dram)
    with ExitStack() as ctx:
        g_out = k.sb("l1_gout", [P, D], ctx=ctx)
        normalise(k, "l1_no", Y, Y, g_out, 1e-5, loads=((g_out, a["l1_g_out"]),))


def biased_attention(k, a, layer, X, Y, XT, ident):
    n = f"l{layer}"
    with ExitStack() as ctx:
        g_in = k.sb(n + "_gin", [P, D], ctx=ctx)
        normalise(k, n + "_n", X, Y, g_in, 1e-5, loads=((g_in, a[n + "_g_in"]),))
        to_feature_major(k, n + "_t", Y, XT, ident)
    attention(k, n + "_a", XT, (a[n + "_wq"], a[n + "_wkv"], a[n + "_wout"], a[n + "_null_attn_bias"]),
              a["cond"], a["condT"], a["mask0"], Y, ident, a["bias"])
    with ExitStack() as ctx:
        g_out = k.sb(n + "_gout", [P, D], ctx=ctx)
        normalise(k, n + "_no", Y, Y, g_out, 1e-5, loads=((g_out, a[n + "_g_out"]),))


def layer1_ffn(k, a, X, Y, XT, ident):
    with ExitStack() as ctx:
        picked = k.sb("l1_picked", [P, NT, 8], ctx=ctx)
        to_feature_major(k, "l1_t2", Y, XT, ident)
        route(k, "l1_r", XT, a["l1_router"], 8, 1, picked, ident, bias=a["l1_router_b"])
        lora_ffn(k, "l1_f", XT, picked, (a["l1_wi"], a["l1_wi_b"], a["l1_wo"], a["l1_wo_b"],
                                         a["l1_lora_a"], a["l1_lora_b"]), X, ident)


def layer2_ffn(k, a, X, Y, XT, ident):
    with ExitStack() as ctx:
        scale = k.sb("l2_scale", [P, 1], ctx=ctx)
        round_to_e4m3(k, "l2_q", Y, Y, a["l2_input_scale"], scale)
        to_feature_major(k, "l2_t2", Y, XT, ident)
        linear(k, "l2_f", XT, a["l2_w"], a["l2_weight_scale"], a["l2_bias"], X)


def layer3_ffn(k, a, X, Y, XT, ident, rows_dram, out_dram):
    with ExitStack() as ctx:
        upper = k.sb("l3_upper", [P, P], ctx=ctx)
        make_triangle(k, "l3_u", upper)
        shares = k.sb("l3_shares", [P, NT, 8], ctx=ctx)
        chosen = k.sb("l3_chosen", [P, NT, 8], ctx=ctx)
        rank = k.sb("l3_rank", [P, NT, 8], ctx=ctx)
        to_feature_major(k, "l3_t2", Y, XT, ident)
        route(k, "l3_r", XT, a["l3_router"], 8, 2, shares, ident, bias=a["l3_router_b"], soft="chosen",
              ones=chosen)
        places(k, "l3_p", chosen, rank, upper)
        drop_over_capacity(k, "l3_d", shares, rank)
        sent_experts(k, "l3_e", Y, shares, chosen, rank, a["l3_experts"], 4 * P, 8, X, rows_dram, out_dram,
                     ident)


def four_layers(nc, a, out):
    with ExitStack() as ctx:
        k = Kit(nc, ctx)
        X = k.sb("X", [P, NT, D])
        Y = k.sb("Y", [P, NT, D])
        XT = k.sb("XT", [P, KD, TOK])
        ident = k.sb("ident", [P, P])
        table_dram = nc.dram_tensor("position_table", [HEADS, TABLE], F32, kind="Internal").ap()
        rq_dram = nc.dram_tensor("query_norms", [HEADS, TOK], F32, kind="Internal").ap()
        rows_dram, out_dram = (nc.dram_tensor(n, [8 * CAPACITY, D], F32, kind="Internal").ap()
                               for n in ("sent_rows", "expert_rows"))
        load_constants(k, ident, X, a["x"])
        with k.stage():
            layer0(k, a, X, Y, XT, ident)
        with k.stage():
            layer1_attention(k, a, X, Y, XT, ident, table_dram, rq_dram)
        with k.stage():
            layer1_ffn(k, a, X, Y, XT, ident)
        with k.stage():
            biased_attention(k, a, 2, X, Y, XT, ident)
        with k.stage():
            layer2_ffn(k, a, X, Y, XT, ident)
        with k.stage():
            biased_attention(k, a, 3, X, Y, XT, ident)
        with k.stage():
            layer3_ffn(k, a, X, Y, XT, ident, rows_dram, out_dram)
        store_rows(k, "stored", X, out)


def lay_out(inputs):
    import numpy as np

    def rows(w):
        w = np.asarray(w)
        return np.ascontiguousarray(w.reshape(w.shape[0] // 128, 128, -1).transpose(1, 0, 2))

    g = {n: np.asarray(a) for n, a in inputs.items()}

    def experts(gate, up, down):
        out = []
        for a, b, c in zip(gate, up, down):
            out.append(np.concatenate([rows(x).reshape(128, -1) for x in (a, b, c)], axis=1))
        return np.ascontiguousarray(np.stack(out))

    def halves(w):
        return [w[:, :w.shape[1] // 2], w[:, w.shape[1] // 2:]]

    a = {"x": g["x"], "cond": g["cond_64"], "condT": g["cond_64"].T, "bias": g["fside_16xSxS_0"],
         "mask1": g["mask_BxS_bf1"], "mask0": g["mask_BxS_bk0"]}
    down = g["L0_cond_sw_down"]
    a["l0_router"] = rows(g["L0_cond_wt"].T)
    a["l0_router_cond"] = g["L0_cond_wg"].T
    a["l0_experts"] = experts(list(g["L0_cond_w_gate"]) + halves(g["L0_cond_sw_gate"]),
                              list(g["L0_cond_w_up"]) + halves(g["L0_cond_sw_up"]),
                              list(g["L0_cond_w_down"]) + [down[:128], down[128:]])
    a["l0_ffn_router"] = rows(g["L0_ffn_W_router"])
    a["l0_w1"] = g["L0_ffn_W1"].reshape(4, 2, 128, 1024).transpose(2, 0, 1, 3)
    a["l0_b1"] = g["L0_ffn_b1"]
    a["l0_wo"] = rows(g["L0_ffn_Wo"])
    for n in ("bo", "ln_gamma", "ln_beta"):
        a["l0_" + n] = g["L0_ffn_" + n]
    for n in ("g_norm", "q_scale", "k_scale", "null_attn_bias", "b0", "g0", "b1", "g1", "b2", "g_out"):
        a["l1_" + n] = g["L1_cond_" + n]
    a["l1_w0"] = g["L1_cond_w0"][0]
    a["l1_w1"] = rows(g["L1_cond_w1"])
    a["l1_w2"] = rows(g["L1_cond_w2"])
    for layer, wo in ((1, "L1_cond_Wout"), (2, "L2_cond_Wo"), (3, "L3_cond_Wo")):
        a[f"l{layer}_wq"] = rows(g[f"L{layer}_cond_Wq"])
        a[f"l{layer}_wkv"] = rows(g[f"L{layer}_cond_Wkv"])
        heads = g[wo].reshape(16, 64, 256).transpose(1, 0, 2).reshape(64, -1)
        a[f"l{layer}_wout"] = np.concatenate([heads, heads])
    a["l1_router"] = rows(g["L1_ffn_gate_W"].T)
    a["l1_router_b"] = g["L1_ffn_gate_b"]
    a["l1_wi"] = rows(g["L1_ffn_wi_W"].T)
    a["l1_wi_b"] = g["L1_ffn_wi_b"].reshape(8, 128).T
    a["l1_wo"] = rows(g["L1_ffn_wo_W"].T)
    a["l1_wo_b"] = g["L1_ffn_wo_b"]
    a["l1_lora_a"] = rows(g["L1_ffn_lora_A"].reshape(32, 256).T)
    a["l1_lora_b"] = g["L1_ffn_lora_B"].transpose(0, 2, 1).reshape(32, 1024)
    for layer in (2, 3):
        for n in ("g_in", "null_attn_bias", "g_out"):
            a[f"l{layer}_{n}"] = g[f"L{layer}_cond_{n}"]
    a["l2_w"] = rows(g["L2_ffn_weight_fp8"].T)
    for n in ("bias", "input_scale", "weight_scale"):
        a["l2_" + n] = g["L2_ffn_" + n]
    a["l3_router"] = rows(g["L3_ffn_router_w"].T)
    a["l3_router_b"] = g["L3_ffn_router_b"]
    a["l3_experts"] = experts(g["L3_ffn_W"], g["L3_ffn_V"], g["L3_ffn_W_out"])
    return {n: np.ascontiguousarray(v) for n, v in a.items()}


_OUT = ((2, 1024, 256), "float32")


def kernel(**inputs):
    import numpy as _np
    import concourse.bacc as _bacc
    from concourse import mybir as _mybir
    from concourse.bass_utils import run_bass_kernel_spmd as _run

    nc = _bacc.Bacc("TRN2", target_bir_lowering=False, num_devices=1)
    laid = lay_out(inputs)
    arrays = {f"in_{n}": a for n, a in laid.items()}
    dram = {n: nc.dram_tensor(f"in_{n}", a.shape, _mybir.dt.from_np(a.dtype), kind="ExternalInput").ap()
            for n, a in laid.items()}
    out = nc.dram_tensor("out_0", _OUT[0], _mybir.dt.from_np(_np.dtype(_OUT[1])), kind="ExternalOutput").ap()
    four_layers(nc, dram, out)
    return _run(nc, [arrays], core_ids=[0]).results[0]["out_0"]
```
